# Optimizing a Trainium2 kernel written in Bass

```python
import numpy as np
import jax
import jax.numpy as jnp

def _softmax(x, axis=-1):
    return jax.nn.softmax(x, axis=axis)

def _gelu(x):
    return jax.nn.gelu(x, approximate=True)

def _silu(x):
    return jax.nn.silu(x)

def _sigmoid(x):
    return jax.nn.sigmoid(x)

def _layernorm(x, axis=-1, eps=1e-05):
    m = jnp.mean(x, axis=axis, keepdims=True)
    v = jnp.var(x, axis=axis, keepdims=True)
    return (x - m) / jnp.sqrt(v + eps)

def _scatter_add(tgt, idx, src, axis=0):
    return tgt.at[idx].add(src)

def _segment_sum(src, seg, n):
    return jax.ops.segment_sum(src, seg, n)
kernel_name = 'mk_gnn_preln_d4_gnn_r32_447097'

def setup_inputs(seed: int=0):
    np.random.seed(seed)
    _w = jnp.asarray

    def _rec_inputs():
        import jax
        import jax.numpy as jnp
        _gk = jax.random.key(seed)
        x = -0.000202 + 1 * jax.random.normal(jax.random.fold_in(_gk, 1), (3125, 128), jnp.float32)
        src = jax.random.randint(jax.random.fold_in(_gk, 2), (100000,), 0, 3125, jnp.int32)
        dst = jnp.minimum((3125 * jax.random.uniform(jax.random.fold_in(_gk, 3), (100000,)) ** 2.0).astype(jnp.int32), 99999)
        _o = jnp.argsort(dst, stable=True)
        src = src[_o]
        dst = dst[_o]
        edge_attr_32 = 0.000196303 + 1.00016 * jax.random.normal(jax.random.fold_in(_gk, 12), (100000, 32), jnp.float32)
        edge_type_8 = jax.random.randint(jax.random.fold_in(_gk, 14), (100000,), 0, 8, jnp.int32)
        edge_weight = jax.random.uniform(jax.random.fold_in(_gk, 15), (100000,), jnp.float32, 0.0, 0.999999)
        return (x, src, dst, edge_attr_32, edge_type_8, edge_weight)
    x, src, dst, edge_attr_32, edge_type_8, edge_weight = _rec_inputs()

    def _L0_gnn_setup():
        import jax, jax.numpy as jnp
        import numpy as np
        N, F, H, E = (50000, 128, 128, 25000)
        BN_EPS = 1e-05
        key = jax.random.key(seed)
        k1, k2, k3, k4, k5, k6 = jax.random.split(key, 6)
        return {'feature': jax.random.normal(k1, (N, F), dtype=jnp.float32), 'weight': jax.random.normal(k2, (F, H), dtype=jnp.float32) * (1.0 / np.sqrt(H)), 'bias': jax.random.normal(k3, (H,), dtype=jnp.float32) * (1.0 / np.sqrt(H)), 'bn_gamma': jnp.ones((H,), dtype=jnp.float32), 'bn_beta': jnp.zeros((H,), dtype=jnp.float32), 'edge_weight': jax.random.uniform(k4, (E,), dtype=jnp.float32), 'edge_row': jax.random.randint(k5, (E,), 0, N, dtype=jnp.int32), 'edge_col': jax.random.randint(k6, (E,), 0, N, dtype=jnp.int32)}
    _L0_gnn_all = _L0_gnn_setup()
    _L0_gnn_in = {k: v for k, v in _L0_gnn_all.items() if k in ('weight', 'bias', 'bn_gamma', 'bn_beta')}
    del _L0_gnn_all

    def _L1_gnn_setup():
        import jax, jax.numpy as jnp
        import numpy as np
        N_NODES = 50000
        N_EDGES = 25000
        IN_FEAT = 128
        OUT_FEAT = 128
        NUM_REL = 8
        key = jax.random.key(seed)
        k_h, k_w, k_s, k_d, k_r = jax.random.split(key, 5)
        h = jax.random.normal(k_h, (N_NODES, IN_FEAT), dtype=jnp.float32)
        gain = float(np.sqrt(2.0))
        bound = gain * float(np.sqrt(6.0 / (IN_FEAT + OUT_FEAT)))
        weight = jax.random.uniform(k_w, (NUM_REL, IN_FEAT, OUT_FEAT), dtype=jnp.float32, minval=-bound, maxval=bound)
        src = jax.random.randint(k_s, (N_EDGES,), 0, N_NODES, dtype=jnp.int64)
        dst = jax.random.randint(k_d, (N_EDGES,), 0, N_NODES, dtype=jnp.int64)
        rel = jax.random.randint(k_r, (N_EDGES,), 0, NUM_REL, dtype=jnp.int64)
        return {'h': h, 'weight': weight, 'src': src, 'dst': dst, 'rel': rel}
    _L1_gnn_all = _L1_gnn_setup()
    _L1_gnn_in = {k: v for k, v in _L1_gnn_all.items() if k in ('weight',)}
    del _L1_gnn_all

    def _L2_gnn_setup():
        import jax, jax.numpy as jnp
        import numpy as np
        N_NODES = 50000
        N_EDGES = 18750
        CHANNELS = 128
        HEADS = 8
        key = jax.random.key(seed)
        k1, k2, k3 = jax.random.split(key, 3)
        x = jax.random.normal(k1, (N_NODES, CHANNELS), dtype=jnp.float32)
        edge_index = jax.random.randint(k2, (2, N_EDGES), 0, N_NODES, dtype=jnp.int32)
        att = jax.random.normal(k3, (HEADS, 2 * (CHANNELS // HEADS)), dtype=jnp.float32)
        return {'x': x, 'edge_index': edge_index, 'att': att}
    _L2_gnn_all = _L2_gnn_setup()
    _L2_gnn_in = {k: v for k, v in _L2_gnn_all.items() if k in ('att',)}
    del _L2_gnn_all

    def _L3_gnn_setup():
        import jax, jax.numpy as jnp
        import numpy as np
        N_NODES = 50000
        N_EDGES = 25000
        IN_F = 128
        OUT_F = 128
        HEADS = 8
        HEAD_DIM = OUT_F // HEADS
        EDGE_F = 32
        key = jax.random.key(seed)
        ks = jax.random.split(key, 14)
        s = lambda fan_in: 1.0 / np.sqrt(fan_in)
        return {'node_features': jax.random.normal(ks[0], (N_NODES, IN_F), jnp.float32), 'edge_index': jax.random.randint(ks[1], (2, N_EDGES), 0, N_NODES, jnp.int64), 'edge_features': jax.random.normal(ks[2], (N_EDGES, EDGE_F), jnp.float32), 'Wq': jax.random.uniform(ks[3], (IN_F, OUT_F), jnp.float32, -s(IN_F), s(IN_F)), 'bq': jnp.zeros((OUT_F,), jnp.float32), 'Wk': jax.random.uniform(ks[4], (IN_F, OUT_F), jnp.float32, -s(IN_F), s(IN_F)), 'bk': jnp.zeros((OUT_F,), jnp.float32), 'Wv': jax.random.uniform(ks[5], (IN_F, OUT_F), jnp.float32, -s(IN_F), s(IN_F)), 'bv': jnp.zeros((OUT_F,), jnp.float32), 'We': jax.random.uniform(ks[6], (EDGE_F, HEADS), jnp.float32, -s(EDGE_F), s(EDGE_F)), 'be': jnp.zeros((HEADS,), jnp.float32), 'Wo': jax.random.uniform(ks[7], (OUT_F, OUT_F), jnp.float32, -s(OUT_F), s(OUT_F)), 'bo': jnp.zeros((OUT_F,), jnp.float32)}
    _L3_gnn_all = _L3_gnn_setup()
    _L3_gnn_in = {k: v for k, v in _L3_gnn_all.items() if k in ('Wq', 'bq', 'Wk', 'bk', 'Wv', 'bv', 'We', 'be', 'Wo', 'bo')}
    del _L3_gnn_all
    return {'x': x, 'src': src, 'dst': dst, 'edge_attr_32': edge_attr_32, 'edge_type_8': edge_type_8, 'edge_weight': edge_weight, 'L0_gnn_weight': _L0_gnn_in['weight'], 'L0_gnn_bias': _L0_gnn_in['bias'], 'L0_gnn_bn_gamma': _L0_gnn_in['bn_gamma'], 'L0_gnn_bn_beta': _L0_gnn_in['bn_beta'], 'L1_gnn_weight': _L1_gnn_in['weight'], 'L2_gnn_att': _L2_gnn_in['att'], 'L3_gnn_Wq': _L3_gnn_in['Wq'], 'L3_gnn_bq': _L3_gnn_in['bq'], 'L3_gnn_Wk': _L3_gnn_in['Wk'], 'L3_gnn_bk': _L3_gnn_in['bk'], 'L3_gnn_Wv': _L3_gnn_in['Wv'], 'L3_gnn_bv': _L3_gnn_in['bv'], 'L3_gnn_We': _L3_gnn_in['We'], 'L3_gnn_be': _L3_gnn_in['be'], 'L3_gnn_Wo': _L3_gnn_in['Wo'], 'L3_gnn_bo': _L3_gnn_in['bo']}

def reference(x, src, dst, edge_attr_32, edge_type_8, edge_weight, L0_gnn_weight, L0_gnn_bias, L0_gnn_bn_gamma, L0_gnn_bn_beta, L1_gnn_weight, L2_gnn_att, L3_gnn_Wq, L3_gnn_bq, L3_gnn_Wk, L3_gnn_bk, L3_gnn_Wv, L3_gnn_bv, L3_gnn_We, L3_gnn_be, L3_gnn_Wo, L3_gnn_bo):
    import jax
    import jax.numpy as jnp

    def _L0_gnn_ref(feature, weight, bias, bn_gamma, bn_beta, edge_weight, edge_row, edge_col):
        import jax, jax.numpy as jnp
        import numpy as np
        N, F, H, E = (50000, 128, 128, 25000)
        BN_EPS = 1e-05
        xw = feature @ weight
        msgs = edge_weight[:, None] * xw[edge_col]
        agg = jax.ops.segment_sum(msgs, edge_row, num_segments=feature.shape[0])
        new_feature = agg + bias
        mean = jnp.mean(new_feature, axis=0)
        var = jnp.var(new_feature, axis=0)
        new_feature = (new_feature - mean) * jax.lax.rsqrt(var + BN_EPS) * bn_gamma + bn_beta
        new_feature = jax.nn.relu(new_feature)
        return feature + new_feature

    def _L1_gnn_ref(h, weight, src, dst, rel):
        import jax, jax.numpy as jnp
        import numpy as np
        N_NODES = 50000
        N_EDGES = 25000
        IN_FEAT = 128
        OUT_FEAT = 128
        NUM_REL = 8
        n_nodes = h.shape[0]
        hw = jnp.einsum('ni,rio->nro', h, weight)
        msg = hw[src, rel]
        out = jax.ops.segment_sum(msg, dst, num_segments=n_nodes)
        return out

    def _L2_gnn_ref(x, edge_index, att):
        import jax, jax.numpy as jnp
        import numpy as np
        N_NODES = 50000
        N_EDGES = 18750
        CHANNELS = 128
        HEADS = 8
        src, dst = (edge_index[0], edge_index[1])
        n = x.shape[0]
        h = att.shape[0]
        d = att.shape[1] // 2
        x_src = x[src].reshape(-1, h, d)
        x_dst = x[dst].reshape(-1, h, d)
        a_src, a_dst = (att[:, :d], att[:, d:])
        alpha = jnp.einsum('ehd,hd->eh', x_src, a_src) + jnp.einsum('ehd,hd->eh', x_dst, a_dst)
        alpha = jnp.where(alpha >= 0, alpha, 0.2 * alpha)
        seg_max = jax.ops.segment_max(alpha, dst, num_segments=n)
        seg_max = jnp.maximum(seg_max, 0.0)
        alpha = jnp.exp(alpha - seg_max[dst])
        seg_sum = jax.ops.segment_sum(alpha, dst, num_segments=n)
        alpha = alpha / jnp.maximum(seg_sum[dst], 1e-10)
        weighted = x_src * alpha[..., None]
        out = jax.ops.segment_sum(weighted, dst, num_segments=n)
        return out.reshape(n, -1)

    def _L3_gnn_ref(node_features, edge_index, edge_features, Wq, bq, Wk, bk, Wv, bv, We, be, Wo, bo):
        import jax, jax.numpy as jnp
        import numpy as np
        N_NODES = 50000
        N_EDGES = 25000
        IN_F = 128
        OUT_F = 128
        HEADS = 8
        HEAD_DIM = OUT_F // HEADS
        EDGE_F = 32
        n_nodes = node_features.shape[0]
        n_edges = edge_index.shape[1]
        sources, targets = (edge_index[0], edge_index[1])
        scale = HEAD_DIM ** (-0.5)
        Q = (node_features @ Wq + bq).reshape(n_nodes, HEADS, HEAD_DIM)
        K = (node_features @ Wk + bk).reshape(n_nodes, HEADS, HEAD_DIM)
        V = (node_features @ Wv + bv).reshape(n_nodes, HEADS, HEAD_DIM)
        Q_t = Q[targets]
        K_s = K[sources]
        V_s = V[sources]
        scores = jnp.sum(Q_t * K_s, axis=-1) * scale
        scores = scores + (edge_features @ We + be)
        max_s = jax.ops.segment_max(scores, targets, num_segments=n_nodes)
        scores = scores - max_s[targets]
        exp_s = jnp.exp(scores)
        denom = jax.ops.segment_sum(exp_s, targets, num_segments=n_nodes) + 1e-10
        probs = exp_s / denom[targets]
        weighted_V = probs[:, :, None] * V_s
        aggregated = jax.ops.segment_sum(weighted_V.reshape(n_edges, -1), targets, num_segments=n_nodes)
        return aggregated @ Wo + bo
    edge_index = jnp.stack([src, dst])
    h = jnp.maximum(_layernorm(x, axis=-1), 0.0)
    x = x + _L0_gnn_ref(h, L0_gnn_weight, L0_gnn_bias, L0_gnn_bn_gamma, L0_gnn_bn_beta, edge_weight, src, dst)
    h = jnp.maximum(_layernorm(x, axis=-1), 0.0)
    x = x + _L1_gnn_ref(h, L1_gnn_weight, src, dst, edge_type_8)
    h = jnp.maximum(_layernorm(x, axis=-1), 0.0)
    x = x + _L2_gnn_ref(h, edge_index, L2_gnn_att)
    h = jnp.maximum(_layernorm(x, axis=-1), 0.0)
    x = x + _L3_gnn_ref(h, edge_index, edge_attr_32, L3_gnn_Wq, L3_gnn_bq, L3_gnn_Wk, L3_gnn_bk, L3_gnn_Wv, L3_gnn_bv, L3_gnn_We, L3_gnn_be, L3_gnn_Wo, L3_gnn_bo)
    return x

_drawn_inputs = setup_inputs


def setup_inputs(seed=0):
    import zlib

    import numpy as np

    out = dict(_drawn_inputs(seed))
    spreads = {'L0_gnn_bn_gamma': (1.0, 0.2),
     'L0_gnn_bn_beta': (0.0, 0.1),
     'L3_gnn_bq': (0.0, 0.8),
     'L3_gnn_bk': (0.0, 0.8),
     'L3_gnn_bv': (0.0, 0.8),
     'L3_gnn_be': (0.0, 0.8),
     'L3_gnn_bo': (0.0, 0.8)}
    factors = {'edge_attr_32': 8.0,
     'L0_gnn_bias': 8.0,
     'L3_gnn_Wq': 8.0,
     'L3_gnn_Wk': 8.0,
     'L3_gnn_Wv': 3.835,
     'L3_gnn_We': 8.0,
     'L3_gnn_Wo': 3.94}
    for name, (base, spread) in spreads.items():
        noise = np.random.default_rng([zlib.crc32(name.encode()), seed]).standard_normal(out[name].shape)
        drawn = base * np.exp(spread * noise) if base else spread * noise
        out[name] = jnp.asarray(drawn.astype(out[name].dtype))
    for name, factor in factors.items():
        out[name] = (out[name] * factor).astype(out[name].dtype)
    return out
```

```python
import concourse.bass as bass
from concourse import mybir
from contextlib import ExitStack

F32 = mybir.dt.float32
BF16 = mybir.dt.bfloat16
I32 = mybir.dt.int32
ALU = mybir.AluOpType
ACT = mybir.ActivationFunctionType
AXX = mybir.AxisListType.X
ENG = mybir.EngineType

P = 128
N = 3125
F = 128
E = 100000
EF = 32
NREL = 8
HEADS = 8
HD = F // HEADS
NB = -(-N // P)
NBX = NB + 1
NLAST = N - (NB - 1) * P
EP = 125
EC = E // EP
REC = 16
D_, S_, T_, W_, POS_, EE_ = 0, 1, 2, 3, 4, 8
NKEY = 64
PADKEY = NKEY * NKEY - 1
BODY = 16
QUAD = 4
HALF = 8
T = -(-(E // P + 1 + NB) // BODY) * BODY
BODIES = T // BODY
CH = P // HEADS
CT = T // CH
CE = CT * P
BIG = 1e30
LN_EPS = 1e-5
ATT_CHUNK = 16
ROWS_V = E + P
NQ = T // QUAD
NH = T // HALF
MG = -(-CT // QUAD)
N_CONSTS = 6 + 7 + 1 + QUAD + 2 * HEADS
assert EP * EC == E and T % CH == 0 and EC % (2 * ATT_CHUNK) == 0 and T * REC * 4 <= 56 * 1024
assert CE * CH == T * P and 2 * CE <= T * REC


def gnn(nc, a, out):
    ctx = ExitStack()
    with ctx:
        def sb(name, shape, dt=F32):
            return ctx.enter_context(nc.sbuf_tensor(name, shape, dt))

        def sem(name):
            return ctx.enter_context(nc.semaphore(name))

        def dram(name, shape, dt=F32):
            return nc.dram_tensor(name, shape, dt, kind="Internal").ap()

        rec = dram("rec", [P * EC, REC])
        rec2 = dram("rec2", [P * EC, REC])
        msgs = dram("msgs", [ROWS_V, F + 1])
        rel_table = dram("rel_table", [NB * P * NREL, F])
        gat_table = dram("gat_table", [NB * P, F + HEADS])
        kv_table = dram("kv_table", [NB * P, 2 * F])
        rows_seq = dram("rows_seq", [P, T * F])
        bias_seq = dram("bias_seq", [P, T * HEADS])

        work = sb("work", [P, T * REC])
        scores = sb("scores", [P, T * HEADS])
        flags = sb("flags", [P, CE + 2], BF16)
        X = sb("X", [P, NB, F])
        nodes = sb("nodes", [P, NBX, F])
        acc = sb("acc", [P, NBX, F + HEADS])
        onehot = sb("onehot", [P, 2, HALF, P])
        onehot_t = sb("onehot_t", [P, 2, QUAD, P])
        dst_local = sb("dst_local", [P, T + BODY])
        src_f = sb("src_f", [P, T])
        weight = sb("weight", [P, T])
        block_lo = sb("block_lo", [P, T])
        maps = sb("maps", [P, T], I32)
        idx_a = sb("idx_a", [P, T + BODY], I32)
        idx_b = sb("idx_b", [P, T + BODY], I32)
        idx_ring = sb("idx_ring", [P, BODY], I32)
        ident_w = sb("ident_w", [P, P + 2 * HEADS])
        src_lo = sb("src_lo", [P, T])
        node_no_i = sb("node_no_i", [P, 1], I32)
        node_no = sb("node_no", [P, 1])
        ones = sb("ones", [P, P])
        lower = sb("lower", [P, P])
        iota = sb("iota", [P, P])
        iota_i = sb("iota_i", [P, P], I32)
        thr = sb("thr", [P, NKEY])
        head_mask = sb("head_mask", [P, HEADS])
        att_col = sb("att_col", [P, 2])
        att_blk = sb("att_blk", [P, 2 * HEADS])
        s_dst = sb("s_dst", [P, NBX, HEADS])
        we_blk = sb("we_blk", [P, QUAD * HEADS])
        be_b = sb("be_b", [P, HEADS])
        w0 = sb("w0", [P, F])
        w_rel = sb("w_rel", [P, NREL, F])
        wqkv = sb("wqkv", [P, 3, F])
        wo = sb("wo", [P, F])
        vecs = sb("vecs", [P, 7, F])
        hT = sb("hT", [P, 2, F])
        col = sb("col", [P, 8, NB])
        cum = sb("cum", [P, 2, 28])
        tot = sb("tot", [P, NKEY])
        totc = sb("totc", [P, NKEY])
        base = sb("base", [P, NKEY])
        tm = sb("tm", [P, 12])
        tmi = sb("tmi", [P, 1], I32)
        tmi2 = sb("tmi2", [P, 1], I32)
        nxt = sb("nxt", [P, 2], I32)
        flag = sb("flag", [P, 1], I32)
        vio = sb("vio", [P, 4])
        bn = sb("bn", [P, 4, F])
        ends = sb("ends", [P, 4])
        link = sb("link", [1, 2, P])
        tails = sb("tails", [1, P])
        carried = sb("carried", [1, P + 2 * HEADS])
        carry = sb("carry", [P, 1])
        psA = ctx.enter_context(nc.psum_tensor("psA", [P, HALF, 256], F32))
        psT = ctx.enter_context(nc.psum_tensor("psT", [P, 2, QUAD, P], F32))
        psG = ctx.enter_context(nc.psum_tensor("psG", [P, 2, QUAD, P], F32))

        recs = work[:, 0:EC * REC].rearrange("p (c w) -> p c w", w=REC)
        tiles = work[:, :].rearrange("p (t w) -> p t w", w=REC)
        H = work[:, 0:NB * F].rearrange("p (b f) -> p b f", f=F)
        H2 = work[:, NB * F:2 * NB * F].rearrange("p (b f) -> p b f", f=F)
        SCAN = work[:, 0:CE]
        MAXS = work[:, CE:2 * CE]
        sc_t = scores[:, :].rearrange("p (t h) -> p t h", h=HEADS)
        by_chunk = MAXS.rearrange("p (j c h) -> p c j h", c=CH, h=HEADS)
        sc_c = scores[:, :].rearrange("p (c j h) -> p j c h", c=CH, h=HEADS)
        msg_ring = work[:, 0:BODY * (F + 1)].rearrange("p (s w) -> p s w", w=F + 1)
        SRC0 = BODY * (F + 1)
        src_local = work[:, SRC0:SRC0 + 2 * HALF]
        gat_ring = work[:, 0:BODY * (F + HEADS)].rearrange("p (s w) -> p s w", w=F + HEADS)
        kv_ring = work[:, 0:BODY * 2 * F].rearrange("p (s w) -> p s w", w=2 * F)
        row_ring = work[:, 0:BODY * F].rearrange("p (s w) -> p s w", w=F)
        prod = work[:, BODY * 2 * F:BODY * 2 * F + QUAD * F]
        seq_ring = work[:, 0:2 * HALF * F].rearrange("p (r s w) -> p r s w", r=2, w=F)
        wgt0 = 2 * HALF * F
        wgt_ring = work[:, wgt0:wgt0 + 2 * HALF * (F + HEADS)].rearrange(
            "p (r s w) -> p r s w", r=2, w=F + HEADS)
        stage0 = 2 * NB * F
        rel_stage = work[:, stage0:stage0 + 2 * NREL * F].rearrange("p (r w) -> p r w", r=2)
        kv_stage = rel_stage[:, :, 0:2 * F]

        dst_i = scores[:, 0:EC].bitcast(I32)
        src_i = scores[:, EC:2 * EC].bitcast(I32)
        typ_i = scores[:, 2 * EC:3 * EC].bitcast(I32)
        w_in = scores[:, 3 * EC:4 * EC]
        key = scores[:, 4 * EC:5 * EC]
        hit = scores[:, 5 * EC:6 * EC]
        cnt = scores[:, 6 * EC:7 * EC]
        key_i = scores[:, 7 * EC:8 * EC].bitcast(I32)
        zeros = onehot[:, :, :, :].rearrange("p a b c -> p (a b c)")[:, 0:EC]
        place = onehot[:, :, :, :].rearrange("p a b c -> p (a b c)")[:, EC:2 * EC]
        ident = ident_w[:, HEADS:HEADS + P]
        place_i = acc[:, :, :].rearrange("p b f -> p (b f)")[:, 0:EC].bitcast(I32)
        sort_rec = acc[:, :, :].rearrange("p b f -> p (b f)")[:, EC:EC + HALF * REC].rearrange(
            "p (c w) -> p c w", w=REC)
        attr = nodes[:, :, :].rearrange("p b f -> p (b f)")[:, 0:2 * ATT_CHUNK * EF].rearrange(
            "p (r c f) -> p r c f", r=2, f=EF)
        dst_id = acc[:, :, :].rearrange("p b f -> p (b f)")[:, 0:T]
        map_tmp = onehot[:, :, :, :].rearrange("p a b c -> p (a b c)")[:, 0:T]
        map_tmp2 = onehot[:, :, :, :].rearrange("p a b c -> p (a b c)")[:, T:2 * T]
        map_rhs = acc[:, :, :].rearrange("p b f -> p (b f)")[:, T:2 * T]
        tile_no = acc[:, :, :].rearrange("p b f -> p (b f)")[:, 2 * T:3 * T]
        tile_no_i = tile_no.bitcast(I32)
        map_src = map_rhs

        def bc(ap, n):
            return ap.rearrange("p (k o) -> p k o", o=1).to_broadcast([ap.shape[0], ap.shape[1], n])

        def rep(ap, n):
            return ap.rearrange("p (o k) -> p o k", o=1).to_broadcast([ap.shape[0], n, ap.shape[1]])

        def blocks_of(engine, row, first, n):
            _, regs = nc.values_load_multi_w_load_instructions(
                maps[row:row + 1, bass.ds(first, n)], engines=[engine], min_val=0, max_val=NB,
                skip_runtime_bounds_check_because="the tile map points to blocks 0 to NB")
            return regs

        def first_edge(engine, row, tile):
            _, regs = nc.values_load_multi_w_load_instructions(
                maps[row:row + 1, bass.ds(tile, 1)], engines=[engine], min_val=0, max_val=E,
                skip_runtime_bounds_check_because="the tile map clamps first edges to E")
            return regs[0]

        pads_set = sem("pads_set")
        edges_in = sem("edges_in")
        consts_in = sem("consts_in")
        x_in = sem("x_in")
        acc_zero = sem("acc_zero")
        iota_set = sem("iota_set")
        dve_consts = sem("dve_consts")
        attr_in = [sem(f"attr_in{i}") for i in range(2)]
        attr_t = sem("attr_t")
        attr_t_sb = sem("attr_t_sb")
        attr_mm = sem("attr_mm")
        bias_put = sem("bias_put")
        counts_set = sem("counts_set")
        base_mm = sem("base_mm")
        recs_set = sem("recs_set")
        rec_out = sem("rec_out")
        flag_set = sem("flag_set")
        so_tot = sem("so_tot")
        so_base = sem("so_base")
        so_place = sem("so_place")
        so_copy = sem("so_copy")
        so_sent = sem("so_sent")
        so_pass = sem("so_pass")
        so_in = sem("so_in")
        map_col = sem("map_col")
        map_mm = sem("map_mm")
        map_set = sem("map_set")
        win_in = [sem(f"win_in{i}") for i in range(8)]
        tail_out = sem("tail_out")
        bias_out = sem("bias_out")
        bias_in = sem("bias_in")
        tiles_set = sem("tiles_set")
        slot = [sem(f"slot{i}") for i in range(BODY)]
        msg_in = [sem(f"msg_in{i}") for i in range(BODY)]
        wb = [sem(f"wb{i}") for i in range(QUAD)]
        seq_in = [sem(f"seq_in{i}") for i in range(2)]
        idx_rdy = sem("idx_rdy")
        oh_rdy = sem("oh_rdy")
        tr_done = sem("tr_done")
        oht_rdy = sem("oht_rdy")
        got = sem("got")
        pool_turns = sem("pool_turns")
        quad_rdy = sem("quad_rdy")
        prod_rdy = sem("prod_rdy")
        agg = sem("agg")
        added = sem("added")
        wgt_rdy = sem("wgt_rdy")
        src_sub = sem("src_sub")
        ln_var = sem("ln_var")
        ln_sd = sem("ln_sd")
        h_rdy = sem("h_rdy")
        h_t = sem("h_t")
        h_t_sb = sem("h_t_sb")
        h_mm = sem("h_mm")
        h_out = sem("h_out")
        h_out_act = sem("h_out_act")
        tab_out = [sem(f"tab_out{i}") for i in range(2)]
        msgs_done = sem("msgs_done")
        bn_in = sem("bn_in")
        bn_mm = sem("bn_mm")
        bn_var = sem("bn_var")
        bn_sd = sem("bn_sd")
        mv_rdy = sem("mv_rdy")
        mv_t = sem("mv_t")
        mv_copy = sem("mv_copy")
        edge_in = sem("edge_in")
        edge_mm = sem("edge_mm")
        raw_done = sem("raw_done")
        diff_rdy = sem("diff_rdy")
        exp_rdy = sem("exp_rdy")
        ring_free = sem("ring_free")
        out_done = sem("out_done")
        block = ctx.enter_context(nc.Block())

        at_slot = {"0a": 0, "1": 16 * BODIES, "2a": 32 * BODIES, "3a": 48 * BODIES}
        at_agg = {"0b": 0, "1": T, "2b": 2 * T, "3b": 3 * T}
        at_quad = {"0a": 0, "2a": NQ, "3a": 2 * NQ}
        at_half = {"2b": 0, "3b": NH}
        at_idx = {"1": 0, "2a": NQ + 3, "3a": 2 * (NQ + 3)}
        at_oh = {"0a": 0, "0b": NQ + 1, "1": NQ + 1 + NH, "2a": 2 * (NQ + 1) + NH, "2b": 3 * (NQ + 1) + NH,
                 "3a": 3 * (NQ + 1) + 2 * NH, "3b": 4 * (NQ + 1) + 2 * NH}
        tab_at = {0: (0, 0), 1: (13, 12), 2: (14, 13), 3: (27, 25)}

        def bodies(engine, body):
            body(0)
            with engine.Fori(1, BODIES) as g:
                body(g)

        def wait_if(engine, semaphore, value):
            if not (isinstance(value, int) and value == 0):
                engine.wait_ge(semaphore, value)

        def pout(b):
            return psA[:, 4 * (b % 2):4 * (b % 2) + 4, :].rearrange("p a b -> p (a b)")

        def load_msgs(eng, engine, ks):
            def load(tile, s):
                e = first_edge(engine, 64, tile)
                eng.dma_start(msg_ring[:, s, :], msgs[bass.ds(e, P), :]).then_inc(msg_in[s], 16)
            eng.wait_ge(msgs_done, 1)
            for h in range(2):
                for k in ks:
                    load(h * HALF + k, h * HALF + k)
            with eng.Fori(0, BODIES - 1) as g:
                for h in range(2):
                    eng.wait_ge(agg, g * BODY + (at_agg["0b"] + (h + 1) * HALF))
                    for k in ks:
                        load(g * BODY + ((h + 2) * HALF + k), h * HALF + k)

        def load_windows(eng, engine, k0):
            with eng.Fori(0, T // 8) as g:
                for k in range(k0, 8, 2):
                    e = first_edge(engine, 96, g * 8 + k)
                    eng.dma_start(tiles[:, bass.ds(g * 8 + k, 1), :],
                                  rec[bass.ds(e, P), :].rearrange("p (o w) -> p o w", o=1)).then_inc(win_in[k], 16)

        @block.sync
        def _(sp):
            sp.wait_ge(pads_set, 1)
            for dst, name in ((dst_i, "dst"), (src_i, "src"), (typ_i, "edge_type_8")):
                sp.dma_start(dst[0:EP, :], a[name].rearrange("(p c) -> p c", c=EC)).then_inc(edges_in, 16)
            sp.dma_start(w_in[0:EP, :], a["edge_weight"].rearrange("(p c) -> p c", c=EC)).then_inc(edges_in, 16)
            with nc.allow_non_contiguous_dma("one element of each partition's successor"):
                sp.dma_start(nxt[0:EP - 1, 0:1], a["dst"].rearrange("(p c) -> p c", c=EC)[1:EP, 0:1])\
                    .then_inc(edges_in, 16)
            attr_d = a["edge_attr_32"].rearrange("(p c) f -> p c f", c=EC)
            for q in range(2):
                sp.dma_start(attr[0:EP, q, :, :], attr_d[:, q * ATT_CHUNK:(q + 1) * ATT_CHUNK, :])\
                    .then_inc(attr_in[q], 16)
            with sp.Fori(0, EC // ATT_CHUNK // 2 - 1) as g:
                for q in range(2):
                    sp.wait_ge(bias_put, g * 2 + (q + 1))
                    sp.dma_start(attr[0:EP, q, :, :],
                                 attr_d[:, bass.ds(g * (2 * ATT_CHUNK) + (q + 2) * ATT_CHUNK, ATT_CHUNK), :])\
                        .then_inc(attr_in[q], 16)
            sp.wait_ge(acc_zero, 1)
            sp.dma_start(msgs[E:E + P, 0:F], acc[:, 0, 0:F]).then_inc(tail_out, 16)
            with nc.allow_non_contiguous_dma("the tail's src words"):
                sp.dma_start(msgs[E:E + P, F:F + 1], acc[:, 1, 0:1]).then_inc(tail_out, 16)
            sp.wait_ge(recs_set, 1)
            sp.dma_start(rec.rearrange("(p c) w -> p (c w)", c=EC), work[:, 0:EC * REC]).then_inc(rec_out, 16)
            sp.wait_ge(rec_out, 16)
            sp.wait_ge(flag_set, 1)
            unsorted = sp.value_load(flag[0:1, 0:1], min_val=0, max_val=1)
            with sp.If(unsorted):
                sp.wait_ge(so_pass, 1)
                sp.dma_start(work[:, 0:EC * REC], rec2.rearrange("(p c) w -> p (c w)", c=EC)).then_inc(so_in, 16)
                sp.wait_ge(so_pass, 2)
            with sp.Else():
                sp.nop()
            sp.wait_ge(map_set, 1)
            load_windows(sp, ENG.SP, 0)
            sp.wait_ge(tiles_set, 1)
            sp.dma_start(bias_seq, scores[:, :]).then_inc(bias_out, 16)
            load_msgs(sp, ENG.SP, range(0, HALF // 2))

            for b in range(NB):
                sp.wait_ge(h_out, NB + b + 1)
                sp.wait_ge(h_out_act, b + 1)
                sp.dma_start(rel_table.rearrange("(n r) f -> n (r f)", r=NREL)[b * P:(b + 1) * P, :],
                             rel_stage[:, b % 2, :]).then_inc(tab_out[b % 2], 16)

            def write_back(n, rows):
                g0 = at_slot[f"{n}a"]
                with sp.Fori(0, BODIES) as g:
                    for k in range(4):
                        for j in range(QUAD):
                            sp.wait_ge(slot[4 * k + j], g * 16 + (g0 + 16))
                        sp.dma_start(rows_seq[:, bass.ds(g * (BODY * F) + 4 * k * F, QUAD * F)]
                                     .rearrange("p (s w) -> p s w", w=F), rows(k)).then_inc(wb[k], 16)

            def read_rows(n):
                for k in range(4):
                    sp.wait_ge(wb[k], 16 * BODIES * (n - 1))
                sp.wait_ge(ring_free, n - 1)
                for h in range(2):
                    sp.dma_start(seq_ring[:, h, :, :], rows_seq[:, h * HALF * F:(h + 1) * HALF * F]
                                 .rearrange("p (s w) -> p s w", w=F)).then_inc(seq_in[h], 16)
                with sp.Fori(0, BODIES - 1) as g:
                    for h in range(2):
                        sp.wait_ge(wgt_rdy, g * 2 + (at_half[f"{n}b"] + h + 1))
                        sp.dma_start(seq_ring[:, h, :, :],
                                     rows_seq[:, bass.ds(g * (BODY * F) + (h + 2) * HALF * F, HALF * F)]
                                     .rearrange("p (s w) -> p s w", w=F)).then_inc(seq_in[h], 16)

            sp.wait_ge(h_rdy, 3)
            sp.dma_start(gat_table.rearrange("(b p) w -> p b w", p=P)[:, :, 0:F], H).then_inc(tab_out[0], 16)
            sp.wait_ge(h_out, 3 * NB)
            sp.dma_start(gat_table.rearrange("(b p) w -> p b w", p=P)[:, :, F:F + HEADS],
                         H2[:, :, 0:HEADS]).then_inc(tab_out[1], 16)
            write_back(2, lambda k: gat_ring[:, 4 * k:4 * k + 4, 0:F])
            read_rows(2)
            for b in range(NB):
                sp.wait_ge(h_out, 3 * NB + b + 1)
                sp.dma_start(kv_table[b * P:(b + 1) * P, :], kv_stage[:, b % 2, :]).then_inc(tab_out[b % 2], 16)
            write_back(3, lambda k: kv_ring[:, 4 * k:4 * k + 4, F:2 * F])
            for k in range(4):
                sp.wait_ge(wb[k], 16 * BODIES * 2)
            sp.wait_ge(raw_done, 1)
            sp.wait_ge(bias_out, 16)
            sp.dma_start(work[:, 0:T * HEADS], bias_seq).then_inc(bias_in, 16)
            read_rows(3)
            sp.wait_ge(h_out, 5 * NB)
            sp.dma_start(out[0:(NB - 1) * P, :].rearrange("(b p) f -> p b f", p=P), X[:, 0:NB - 1, :])\
                .then_inc(out_done, 16)
            sp.dma_start(out[(NB - 1) * P:N, :], X[0:NLAST, NB - 1, :]).then_inc(out_done, 16)
            sp.wait_ge(out_done, 32)

        @block.gpsimd
        def _(pool):
            nc.gpsimd.memset(ident_w[:], 0.0).then_inc(iota_set, 1)
            nc.gpsimd.memset(lower[:], 1.0).then_inc(iota_set, 1)
            nc.gpsimd.memset(head_mask[:], 1.0).then_inc(iota_set, 1)
            nc.gpsimd.iota(iota_i[:], pattern=[[1, P]], base=0, channel_multiplier=0).then_inc(iota_set, 1)
            nc.gpsimd.iota(node_no_i[:], pattern=[[1, 1]], base=0, channel_multiplier=1).then_inc(iota_set, 1)
            nc.gpsimd.iota(tile_no_i, pattern=[[1, T]], base=0, channel_multiplier=0).then_inc(iota_set, 1)
            pool.wait_ge(iota_set, 6)
            nc.gpsimd.affine_select(out=ident_w[:], in_=ident_w[:], compare_op=ALU.not_equal, fill=1.0,
                                    base=HEADS, pattern=[[-1, P + 2 * HEADS]], channel_multiplier=1)\
                .then_inc(iota_set, 1)
            nc.gpsimd.affine_select(out=lower[:], in_=lower[:], compare_op=ALU.is_gt, fill=0.0, base=0,
                                    pattern=[[1, P]], channel_multiplier=-1).then_inc(iota_set, 1)
            nc.gpsimd.affine_select(out=head_mask[:], in_=head_mask[:], compare_op=ALU.is_ge, fill=0.0, base=0,
                                    pattern=[[-HD, HEADS]], channel_multiplier=1).then_inc(iota_set, 1)
            pool.wait_ge(iota_set, 9)
            nc.gpsimd.affine_select(out=head_mask[:], in_=head_mask[:], compare_op=ALU.is_ge, fill=0.0,
                                    base=HD - 1, pattern=[[HD, HEADS]], channel_multiplier=-1)\
                .then_inc(iota_set, 1)
            pool.wait_ge(flag_set, 1)
            unsorted = pool.value_load(flag[0:1, 0:1], min_val=0, max_val=1)
            with pool.If(unsorted):
                pool.wait_ge(rec_out, 16)
                for n, target in enumerate((rec2, rec)):
                    pool.wait_ge(so_place, n + 1)
                    c0, s0 = n * 2 * (EC // HALF), n * 16 * HALF * (EC // HALF)
                    with pool.Fori(0, EC // HALF) as g:
                        nc.gpsimd.tensor_copy(sort_rec, recs[:, bass.ds(g * HALF, HALF), :]).then_inc(so_copy, 1)
                        nc.gpsimd.tensor_copy(idx_ring[:, 0:HALF], place_i[:, bass.ds(g * HALF, HALF)])\
                            .then_inc(so_copy, 1)
                        pool.wait_ge(so_copy, g * 2 + (c0 + 2))
                        pool.sem_inc(pool_turns, 1)
                        for j in range(HALF):
                            nc.gpsimd.indirect_dma_start(
                                target, bass.IndirectOffsetOnAxis(ap=idx_ring[:, j:j + 1], axis=0),
                                sort_rec[:, j, :], None, bounds_check=P * EC - 1, oob_is_err=False)\
                                .then_inc(so_sent, 16)
                        pool.wait_ge(so_sent, g * (16 * HALF) + (s0 + 16 * HALF))
                    pool.sem_inc(so_pass, 1)
            with pool.Else():
                pool.nop()

            pool.wait_ge(tail_out, 32)
            with pool.Fori(0, BODIES) as g:
                for k in range(4):
                    pool.wait_ge(quad_rdy, g * 4 + (k + 1))
                    pool.sem_inc(pool_turns, 1)
                    for j in range(QUAD):
                        s = 4 * k + j
                        nc.gpsimd.indirect_dma_start(
                            msgs, bass.IndirectOffsetOnAxis(ap=idx_ring[:, s:s + 1], axis=0),
                            msg_ring[:, s, :], None, bounds_check=E - 1, oob_is_err=False).then_inc(slot[s], 16)
            for s in range(BODY):
                pool.wait_ge(slot[s], 16 * BODIES)
            pool.sem_inc(msgs_done, 1)
            for n, ph, table, ring in ((1, "1", rel_table, row_ring), (2, "2a", gat_table, gat_ring),
                                       (3, "3a", kv_table, kv_ring)):
                for i in range(2):
                    pool.wait_ge(tab_out[i], 16 * tab_at[n][i])
                with pool.Fori(0, BODIES) as g:
                    for k in range(4):
                        pool.wait_ge(idx_rdy, g * 4 + (at_idx[ph] + k + 1))
                        pool.sem_inc(pool_turns, 1)
                        for j in range(QUAD):
                            s = 4 * k + j
                            nc.gpsimd.indirect_dma_start(
                                ring[:, s, :], None, table,
                                bass.IndirectOffsetOnAxis(ap=idx_ring[:, s:s + 1], axis=0),
                                bounds_check=table.shape[0] - 1, oob_is_err=False).then_inc(slot[s], 16)

        @block.scalar
        def _(act):
            loads = []

            def load(dst, src):
                act.dma_start(dst, src).then_inc(consts_in, 16)
                loads.append(dst)
            act.dma_start(X[:, 0:NB - 1, :], a["x"][0:(NB - 1) * P, :].rearrange("(b p) f -> p b f", p=P))\
                .then_inc(x_in, 16)
            act.wait_ge(pads_set, 2)
            act.dma_start(X[0:NLAST, NB - 1, :], a["x"][(NB - 1) * P:N, :]).then_inc(x_in, 16)
            load(w0[:], a["L0_gnn_weight"])
            load(w_rel[:], a["L1_gnn_weight"].rearrange("r i o -> i r o"))
            for i, n in enumerate(("Wq", "Wk", "Wv")):
                load(wqkv[:, i, :], a["L3_gnn_" + n])
            load(wo[:], a["L3_gnn_Wo"])
            for i, n in enumerate(("L0_gnn_bias", "L0_gnn_bn_gamma", "L0_gnn_bn_beta",
                                   "L3_gnn_bq", "L3_gnn_bk", "L3_gnn_bv", "L3_gnn_bo")):
                load(vecs[:, i, :], a[n].rearrange("(o n) -> o n", o=1).to_broadcast([P, F]))
            load(be_b[:], a["L3_gnn_be"].rearrange("(o n) -> o n", o=1).to_broadcast([P, HEADS]))
            for i in range(QUAD):
                load(we_blk[EF * i:EF * (i + 1), HEADS * i:HEADS * (i + 1)], a["L3_gnn_We"])
            for h in range(HEADS):
                for i in range(2):
                    load(att_col[HD * h:HD * (h + 1), i:i + 1],
                         a["L2_gnn_att"][h, HD * i:HD * (i + 1)].rearrange("(n o) -> n o", o=1))
            assert len(loads) == N_CONSTS

            with act.Fori(0, EC // ATT_CHUNK // 2) as g:
                for q in range(2):
                    act.wait_ge(attr_t, g * 2 + (q + 1))
                    nc.scalar.activation(onehot_t[:, q, :, 0:EP], psT[:, q, :, 0:EP], ACT.Copy)\
                        .then_inc(attr_t_sb, 1)
            act.wait_ge(rec_out, 16)
            act.wait_ge(flag_set, 1)
            unsorted = act.value_load(flag[0:1, 0:1], min_val=0, max_val=1)
            with act.If(unsorted):
                act.wait_ge(so_pass, 2)
            with act.Else():
                act.nop()
            act.wait_ge(map_set, 1)
            load_windows(act, ENG.Activation, 1)

            def std(n):
                act.wait_ge(ln_var, n)
                nc.scalar.activation(col[:, 4, :], col[:, 3, :], ACT.Sqrt).then_inc(ln_sd, 1)

            def transpose_out(n, b):
                act.wait_ge(h_t, n * NB + b + 1)
                nc.scalar.activation(hT[:, b % 2, :], psT[:, b % 2, 0, :], ACT.Copy).then_inc(h_t_sb, 1)

            def onehots_out(ph, g, k):
                act.wait_ge(tr_done, g * 4 + (at_quad[ph] + k + 1))
                nc.scalar.activation(onehot_t[:, k % 2, :, :], psT[:, k % 2, :, :], ACT.Copy).then_inc(oht_rdy, 1)

            def feed(ph, idx):
                def indices(first, s):
                    nc.scalar.activation(idx_ring[:, s:s + QUAD], idx[:, bass.ds(first, QUAD)], ACT.Copy)\
                        .then_inc(idx_rdy, 1)
                for k in range(3):
                    indices(4 * k, 4 * k)

                def body(g):
                    for k in range(4):
                        if ph == "1":
                            act.wait_ge(agg, g * BODY + (at_agg[ph] + 4 * k))
                        else:
                            onehots_out(ph, g, k)
                            act.wait_ge(quad_rdy, g * 4 + (at_quad[ph] + k))
                            wait_if(act, wb[(k + 3) % 4], g * 16 + (16 * BODIES * (ph == "3a") + 16 * (k > 0)))
                        indices(g * BODY + 4 * (k + 3), 4 * ((k + 3) % 4))
                bodies(act, body)

            def exps(n):
                act.wait_ge(diff_rdy, n)
                nc.scalar.activation(SCAN, MAXS, ACT.Exp).then_inc(exp_rdy, 1)

            std(1)
            for b in range(NB):
                transpose_out(0, b)
            with act.Fori(0, BODIES) as g:
                for k in range(4):
                    onehots_out("0a", g, k)
            load_msgs(act, ENG.Activation, range(HALF // 2, HALF))
            act.wait_ge(bn_var, 1)
            nc.scalar.activation(bn[:, 2, :], bn[:, 1, :], ACT.Sqrt).then_inc(bn_sd, 1)
            std(2)
            for b in range(NB):
                transpose_out(1, b)
                act.wait_ge(h_mm, NB + b + 1)
                if b >= 2:
                    act.wait_ge(tab_out[b % 2], 16 * (b // 2))
                nc.scalar.activation(rel_stage[:, b % 2, 0:512], pout(b)[:, 0:512], ACT.Copy)\
                    .then_inc(h_out_act, 1)
            feed("1", idx_b)
            std(3)
            for b in range(NB):
                transpose_out(2, b)
            feed("2a", idx_a)
            exps(1)
            std(4)
            for b in range(NB):
                transpose_out(3, b)
            feed("3a", idx_a)
            exps(2)
            for b in range(NB):
                transpose_out(4, b)

        @block.tensor
        def _(pe):
            def node_products(n, weights):
                pe.wait_ge(h_rdy, n + 1)
                at = 0
                for b in range(NB):
                    nc.tensor.transpose(psT[:, b % 2, 0, :], H[:, b, :], ident).then_inc(h_t, 1)
                    pe.wait_ge(h_t_sb, n * NB + b + 1)
                    if b >= 2:
                        pe.wait_ge(h_out, n * NB + b - 1)
                        if n == 1:
                            pe.wait_ge(h_out_act, b - 1)
                    at = 0
                    for w in weights:
                        width = w.shape[1] * (w.shape[2] if len(w.shape) > 2 else 1)
                        ins = nc.tensor.matmul(pout(b)[:, at:at + width], hT[:, b % 2, :], w, start=True, stop=True)
                        at += width
                    ins.then_inc(h_mm, 1)

            def fetch(ph, rows, width):
                with pe.Fori(0, BODIES) as g:
                    regs = blocks_of(ENG.PE, 0, g * BODY, BODY)
                    for k in range(4):
                        pe.wait_ge(oh_rdy, g * 4 + (at_oh[ph] + k + 1))
                        for j in range(QUAD):
                            ins = nc.tensor.transpose(psT[:, k % 2, j, :], onehot[:, k % 2, j, :], ident)
                        ins.then_inc(tr_done, 1)
                        pe.wait_ge(oht_rdy, g * 4 + (at_quad[ph] + k + 1))
                        for j in range(QUAD):
                            ins = nc.tensor.matmul(psG[:, k % 2, j, 0:width], onehot_t[:, k % 2, j, :],
                                                   rows(regs[4 * k + j]), start=True, stop=True)
                        ins.then_inc(got, 1)

            def move(m, source):
                pe.wait_ge(mv_rdy, m + 1)
                for q in range(MG):
                    if q >= 2:
                        pe.wait_ge(mv_copy, m * MG + q - 1)
                    for j in range(4 * q, min(4 * q + 4, CT)):
                        ins = nc.tensor.transpose(psT[:, q % 2, j % 4, :], source(j), ident)
                    ins.then_inc(mv_t, 1)

            def to_scan(m):
                move(m, lambda j: MAXS[:, j * P:(j + 1) * P])

            def from_scan(m):
                move(m, lambda j: SCAN[:, j * P:(j + 1) * P])

            def weighted_sums(n):
                with pe.Fori(0, BODIES) as g:
                    for h in range(2):
                        pe.wait_ge(oh_rdy, g * 2 + (at_oh[f"{n}b"] + h + 1))
                        pe.wait_ge(wgt_rdy, g * 2 + (at_half[f"{n}b"] + h + 1))
                        for j in range(HALF):
                            nc.tensor.matmul(psA[:, j, 0:F + HEADS], onehot[:, h, j, :], wgt_ring[:, h, j, :],
                                             start=True, stop=True).then_inc(agg, 1)

            def carries(d):
                pe.wait_ge(edge_in, 2 * d + 3)
                nc.tensor.matmul(psG[0:1, 0, 0, :], MAXS[:, CE - 1:CE] if d % 2 == 0 else MAXS[:, 0:1], ident,
                                 start=True, stop=True).then_inc(edge_mm, 1)
                pe.wait_ge(edge_in, 2 * d + 4)
                sh = 0 if d % 2 == 0 else 2 * HEADS
                nc.tensor.matmul(psG[:, 1, 0, 0:1], carried[0:1, sh:sh + P], ones[0:1, 0:1],
                                 start=True, stop=True).then_inc(edge_mm, 1)

            pe.wait_ge(iota_set, 10)
            pe.wait_ge(dve_consts, 1)
            pe.wait_ge(consts_in, 16 * N_CONSTS)
            with pe.Fori(0, EC // ATT_CHUNK // 2) as g:
                for q in range(2):
                    pe.wait_ge(attr_in[q], g * 16 + 16)
                    for j in range(QUAD):
                        ins = nc.tensor.transpose(
                            psT[:, q, j, 0:EP],
                            attr[0:EP, q, 4 * j:4 * j + 4, :].rearrange("p c f -> p (c f)"), ident[0:EP, 0:EP])
                    ins.then_inc(attr_t, 1)
                    pe.wait_ge(attr_t_sb, g * 2 + (q + 1))
                    for j in range(QUAD):
                        ins = nc.tensor.matmul(psG[0:EP, q, 0, 32 * j:32 * j + 32], onehot_t[:, q, j, 0:EP],
                                               we_blk[:], start=True, stop=True)
                    ins.then_inc(attr_mm, 1)
            pe.wait_ge(counts_set, 1)
            nc.tensor.matmul(psG[:, 0, 0, 0:NB], lower[:], tot[:, 0:NB], start=True, stop=False)
            nc.tensor.matmul(psG[:, 0, 0, 0:NB], ones[:], cum[:, 1, 0:NB], start=False, stop=True)
            nc.tensor.matmul(psG[:, 0, 1, 0:2], ones[:], vio[:, 2:4], start=True, stop=True)
            for m in range(2):
                for i in range(2):
                    ins = nc.tensor.matmul(psG[0:NBX, 0, 2, 2 * m + i:2 * m + i + 1], cum[:, m, i:i + NBX],
                                           ones[:, 0:1], start=True, stop=True)
            ins.then_inc(base_mm, 1)
            pe.wait_ge(flag_set, 1)
            unsorted = pe.value_load(flag[0:1, 0:1], min_val=0, max_val=1)
            with pe.If(unsorted):
                for n in range(2):
                    pe.wait_ge(so_tot, n + 1)
                    nc.tensor.matmul(psG[:, 1, 0, 0:NKEY], lower[:], tot[:], start=True, stop=False)
                    nc.tensor.matmul(psG[:, 1, 0, 0:NKEY], ones[:], totc[:], start=False, stop=True)\
                        .then_inc(so_base, 1)
            with pe.Else():
                pe.nop()
            for m in range(2):
                pe.wait_ge(map_col, 3 * m + 1)
                nc.tensor.matmul(psG[0:NBX, 1, 2, 0:1], lower[0:NBX, 0:NBX], tm[0:NBX, 2:3],
                                 start=True, stop=True).then_inc(map_mm, 1)
                for i in range(2):
                    pe.wait_ge(map_col, 3 * m + 2 + i)
                    for c in range(2):
                        ins = nc.tensor.matmul(psA[:, 2 * c:2 * c + 2, :].rearrange("p a b -> p (a b)")[:, 0:T // 2],
                                               ones[0:NBX, :], map_rhs[0:NBX, c * (T // 2):(c + 1) * (T // 2)],
                                               start=True, stop=True)
                    ins.then_inc(map_mm, 1)
            to_scan(0)
            pe.wait_ge(edge_in, 1)
            nc.tensor.matmul(psG[:, 0, 0, 0:1], ident_w[:, 0:P], ends[:, 1:2], start=True, stop=True)
            nc.tensor.matmul(psG[:, 0, 0, 1:2], ident_w[:, 2 * HEADS:2 * HEADS + P], ends[:, 0:1],
                             start=True, stop=True).then_inc(edge_mm, 1)
            pe.wait_ge(edge_in, 2)
            nc.tensor.matmul(psG[0:1, 0, 0, :], ends[:, 2:3], ident, start=True, stop=True)
            nc.tensor.matmul(psG[0:1, 0, 1, :], ends[:, 3:4], ident, start=True, stop=True).then_inc(edge_mm, 1)

            node_products(0, [w0[:]])
            fetch("0a", lambda r: nodes[:, bass.ds(r, 1), :], F)
            with pe.Fori(0, BODIES) as g:
                for h in range(2):
                    pe.wait_ge(oh_rdy, g * 2 + (at_oh["0b"] + h + 1))
                    for j in range(HALF):
                        nc.tensor.matmul(psA[:, j, 0:F], onehot[:, h, j, :], msg_ring[:, h * HALF + j, 0:F],
                                         start=True, stop=True).then_inc(agg, 1)
            for i, src in enumerate((H, H2)):
                pe.wait_ge(bn_in, i + 1)
                for b in range(NB):
                    k = NLAST if b == NB - 1 else P
                    ins = nc.tensor.matmul(psG[:, 0, 0, :], ones[0:k, :], src[0:k, b, :],
                                           start=(b == 0), stop=(b == NB - 1))
                ins.then_inc(bn_mm, 1)
            node_products(1, [w_rel[:, 0:4, :], w_rel[:, 4:8, :]])
            with pe.Fori(0, BODIES) as g:
                for k in range(4):
                    pe.wait_ge(oh_rdy, g * 4 + (at_oh["1"] + k + 1))
                    for j in range(QUAD):
                        s = 4 * k + j
                        pe.wait_ge(slot[s], g * 16 + (at_slot["1"] + 16))
                        nc.tensor.matmul(psA[:, s % HALF, 0:F], onehot[:, k % 2, j, :], row_ring[:, s, :],
                                         start=True, stop=True).then_inc(agg, 1)
            node_products(2, [att_blk[:]])
            fetch("2a", lambda r: s_dst[:, bass.ds(r, 1), :], HEADS)
            to_scan(1)
            carries(0)
            carries(1)
            from_scan(2)
            weighted_sums(2)
            node_products(3, [wqkv[:, :, :]])
            fetch("3a", lambda r: nodes[:, bass.ds(r, 1), :], F)
            to_scan(3)
            carries(2)
            carries(3)
            from_scan(4)
            weighted_sums(3)
            node_products(4, [wo[:]])

        @block.vector
        def _(dve):
            V = nc.vector
            sc = scores[:, :].rearrange("p (c j h) -> p c j h", c=CH, h=HEADS)

            def drain():
                dve.drain()

            def one_hots(first, k):
                V.tensor_tensor(onehot[:, k % 2, 0:QUAD, :], rep(iota[:, :], QUAD),
                                bc(dst_local[:, bass.ds(first, QUAD)], P), ALU.is_equal).then_inc(oh_rdy, 1)

            def add(ph, reg, g, t, s, width):
                if t % 2 == 0:
                    dve.wait_ge(agg, g * BODY + (at_agg[ph] + t + 2))
                wait_if(dve, added, g * BODY + (at_agg[ph] + t))
                V.tensor_tensor(acc[:, bass.ds(reg, 1), 0:width], acc[:, bass.ds(reg, 1), 0:width],
                                psA[:, s:s + 1, 0:width], ALU.add).then_inc(added, 1)

            def layernorm(n):
                V.tensor_reduce(col[:, 0, :], X[:, :, :], AXX, ALU.add)
                drain()
                V.tensor_scalar(col[:, 1, :], col[:, 0, :], 1.0 / F, None, ALU.mult)
                drain()
                V.tensor_tensor(H, X[:, :, :], bc(col[:, 1, :], F), ALU.subtract)
                drain()
                V.tensor_tensor(H2, H, H, ALU.mult)
                drain()
                V.tensor_reduce(col[:, 2, :], H2, AXX, ALU.add)
                drain()
                V.tensor_scalar(col[:, 3, :], col[:, 2, :], 1.0 / F, LN_EPS, ALU.mult, ALU.add).then_inc(ln_var, 1)
                dve.wait_ge(ln_sd, n)
                V.reciprocal(col[:, 5, :], col[:, 4, :])
                drain()
                V.tensor_tensor(H, H, bc(col[:, 5, :], F), ALU.mult)
                drain()
                V.tensor_scalar(H, H, 0.0, None, ALU.max).then_inc(h_rdy, 1)

            def block_out(n, b, put):
                dve.wait_ge(h_mm, n * NB + b + 1)
                put(b, pout(b)).then_inc(h_out, 1)

            def move_out(m, dest):
                for q in range(MG):
                    k = min(4, CT - 4 * q)
                    dve.wait_ge(mv_t, m * MG + q + 1)
                    d, s = dest(q, k, psT[:, q % 2, 0:k, :])
                    V.tensor_copy(d, s).then_inc(mv_copy, 1)
                drain()

            def to_scan_out(m):
                move_out(m, lambda q, k, ps: (SCAN[:, 4 * q * P:(4 * q + k) * P].rearrange("p (j e) -> p j e", e=P), ps))

            def from_scan_out(m):
                move_out(m, lambda q, k, ps: (sc_c[:, 4 * q:4 * q + k, :, :],
                                              ps.rearrange("p j (c h) -> p j c h", h=HEADS)))

            def segment_max(d0):
                for d in range(2):
                    fwd = d == 0
                    rev = slice(None) if fwd else slice(None, None, -1)
                    fl = flags[:, 0:CE] if fwd else flags[:, 1:CE + 1]
                    start = SCAN if fwd else MAXS
                    V.tensor_tensor_scan(MAXS[:, rev], fl[:, rev], start[:, rev], -BIG, ALU.add, ALU.max)\
                        .then_inc(edge_in, 1)
                    dve.wait_ge(edge_mm, 2 * (d0 + d) + 3)
                    V.tensor_copy(tails[0:1, :], psG[0:1, 0, 0, :])
                    V.memset(carried[0:1, :], -BIG)
                    drain()
                    row = carried[0:1, HEADS:HEADS + P]
                    for h in range(HEADS):
                        V.tensor_tensor_scan(row[:, h::HEADS][:, rev], link[0:1, d, h::HEADS][:, rev],
                                             tails[0:1, h::HEADS][:, rev], -BIG, ALU.add, ALU.max)
                    drain()
                    V.tensor_copy(tails[0:1, 0:1], carried[0:1, 0:1]).then_inc(edge_in, 1)
                    dve.wait_ge(edge_mm, 2 * (d0 + d) + 4)
                    V.tensor_copy(carry[:, 0:1], psG[:, 1, 0, 0:1])
                    drain()
                    V.tensor_tensor_scan(MAXS[:, rev], fl[:, rev], MAXS[:, rev], carry[:, 0:1], ALU.add, ALU.max)
                    drain()

            def weighted(n):
                ph = f"{n}b"
                with dve.Fori(0, BODIES) as g:
                    for h in range(2):
                        regs = blocks_of(ENG.DVE, 0, g * BODY + h * HALF, HALF)
                        dve.wait_ge(seq_in[h], g * 16 + (16 * BODIES * (n - 2) + 16))
                        ex = sc_t[:, bass.ds(g * BODY + h * HALF, HALF), :]
                        V.tensor_tensor(
                            wgt_ring[:, h, :, 0:F].rearrange("p s (h d) -> p s h d", d=HD),
                            seq_ring[:, h, :, :].rearrange("p s (h d) -> p s h d", d=HD),
                            ex.rearrange("p s (h o) -> p s h o", o=1).to_broadcast([P, HALF, HEADS, HD]), ALU.mult)
                        V.tensor_copy(wgt_ring[:, h, :, F:F + HEADS], ex).then_inc(wgt_rdy, 1)
                        V.tensor_tensor(onehot[:, h, :, :], rep(iota[:, :], HALF),
                                        bc(dst_local[:, bass.ds(g * BODY + h * HALF, HALF)], P), ALU.is_equal)\
                            .then_inc(oh_rdy, 1)
                        for j in range(HALF):
                            add(ph, regs[j], g, h * HALF + j, j, F + HEADS)
                dve.wait_ge(added, at_agg[ph] + T)

            def shares(eps_op):
                den = H2[:, :, 0:HEADS]
                V.tensor_scalar(den, acc[:, 0:NB, F:F + HEADS], 1e-10, None, eps_op)
                drain()
                V.reciprocal(den, den)
                drain()
                V.tensor_tensor(H.rearrange("p b (h d) -> p b h d", d=HD),
                                acc[:, 0:NB, 0:F].rearrange("p b (h d) -> p b h d", d=HD),
                                den.rearrange("p b (h o) -> p b h o", o=1).to_broadcast([P, NB, HEADS, HD]), ALU.mult)

            V.memset(dst_i, PADKEY)
            V.memset(src_i, PADKEY)
            V.memset(typ_i, 0)
            V.memset(nxt[:], PADKEY)
            V.memset(w_in, 0.0).then_inc(pads_set, 1)
            V.memset(X[:, NB - 1, :], 0.0)
            V.memset(we_blk[:], 0.0).then_inc(pads_set, 1)
            V.memset(acc[:, 0:2, :], 0.0).then_inc(acc_zero, 1)
            V.memset(work[:, :], 0.0)
            V.memset(ones[:], 1.0)
            V.memset(nodes[:, NB, :], 0.0)
            V.memset(s_dst[:, NB, :], 0.0)
            V.memset(zeros, 0.0)
            V.memset(place, 0.0)
            V.memset(vio[:], 0.0)
            V.memset(dst_local[:, T:T + BODY], -1.0)
            V.memset(idx_a[:, T:T + BODY], 0)
            V.memset(idx_b[:, T:T + BODY], 0)
            dve.wait_ge(iota_set, 10)
            V.tensor_copy(iota[:], iota_i[:])
            V.tensor_copy(node_no[:], node_no_i[:])
            V.tensor_copy(map_src, tile_no_i)
            drain()
            V.tensor_copy(tile_no, map_src)
            V.tensor_scalar(thr[:], iota[:, 0:NKEY], float(P), None, ALU.mult)
            drain()
            V.tensor_copy(node_no[:], node_no_i[:]).then_inc(dve_consts, 1)
            with dve.Fori(0, EC // ATT_CHUNK // 2) as g:
                for q in range(2):
                    dve.wait_ge(attr_mm, g * 2 + (q + 1))
                    V.tensor_tensor(recs[0:EP, bass.ds(g * (2 * ATT_CHUNK) + q * ATT_CHUNK, ATT_CHUNK), EE_:EE_ + HEADS],
                                    psG[0:EP, q, 0, :].rearrange("p (c h) -> p c h", h=HEADS),
                                    rep(be_b[0:EP, :], ATT_CHUNK), ALU.add).then_inc(bias_put, 1)
            dve.wait_ge(consts_in, 16 * N_CONSTS)
            V.tensor_scalar(att_blk[:, 0:HEADS], head_mask[:], att_col[:, 0:1], None, ALU.mult)
            V.tensor_scalar(att_blk[:, HEADS:2 * HEADS], head_mask[:], att_col[:, 1:2], None, ALU.mult)
            dve.wait_ge(edges_in, 5 * 16)
            V.tensor_copy(recs[:, :, D_], dst_i)
            V.tensor_copy(recs[:, :, S_], src_i)
            V.tensor_copy(recs[:, :, T_], typ_i)
            V.tensor_copy(recs[:, :, W_], w_in)
            V.tensor_tensor(hit[:, 0:EC - 1], dst_i[:, 0:EC - 1], dst_i[:, 1:EC], ALU.is_gt)
            V.tensor_tensor(vio[:, 1:2], dst_i[:, EC - 1:EC], nxt[:, 0:1], ALU.is_gt)
            drain()
            V.tensor_reduce(vio[:, 0:1], hit[:, 0:EC - 1], AXX, ALU.add)
            drain()
            V.tensor_tensor(vio[:, 2:3], vio[:, 0:1], vio[:, 1:2], ALU.add)
            V.tensor_copy(key, dst_i)
            V.tensor_copy(cnt, src_i)
            drain()
            with dve.Fori(0, NBX + 1) as b:
                for m, x in enumerate((key, cnt)):
                    V.tensor_scalar(hit, x, thr[:, bass.ds(b, 1)], 0.0, ALU.is_lt, ALU.add,
                                    accum_out=cum[:, m, bass.ds(b, 1)])
                    drain()
            V.tensor_tensor(tot[:, 0:NB], cum[:, 1, 1:NB + 1], cum[:, 1, 0:NB], ALU.subtract)
            V.tensor_scalar(key_i, src_i, 7, None, ALU.arith_shift_right)
            drain()
            V.tensor_copy(key, key_i).then_inc(counts_set, 1)
            dve.wait_ge(base_mm, 1)
            V.tensor_scalar(base[:, 0:NB], psG[:, 0, 0, 0:NB], -1.0, None, ALU.add)
            V.tensor_scalar(flag[:, 0:1], psG[:, 0, 1, 0:1], 0.5, None, ALU.is_gt)
            V.tensor_copy(tm[0:NBX, 8:12], psG[0:NBX, 0, 2, 0:4])
            drain()

            def places(n):
                with dve.Fori(0, n) as b:
                    V.tensor_scalar(hit, key, iota[:, bass.ds(b, 1)], None, ALU.is_equal)
                    drain()
                    V.tensor_tensor_scan(cnt, hit, zeros, base[:, bass.ds(b, 1)], ALU.add, ALU.add)
                    drain()
                    V.tensor_tensor(cnt, cnt, hit, ALU.mult)
                    drain()
                    V.tensor_tensor(place, place, cnt, ALU.add)
                    drain()

            places(NB)
            V.tensor_copy(recs[:, :, POS_], place)
            drain()
            V.tensor_copy(tot[:, 0:1], zeros[:, 0:1]).then_inc(recs_set, 1)
            dve.wait_ge(tail_out, 32)
            drain()
            V.tensor_copy(tm[0:NBX, 7:8], node_no[0:NBX, :]).then_inc(flag_set, 1)
            unsorted = dve.value_load(flag[0:1, 0:1], min_val=0, max_val=1)
            with dve.If(unsorted):
                dve.wait_ge(rec_out, 16)
                for n in range(2):
                    if n:
                        dve.wait_ge(so_in, 16)
                    V.tensor_copy(dst_i, recs[:, :, D_])
                    V.memset(place, 0.0)
                    drain()
                    if n:
                        V.tensor_scalar(key_i, dst_i, 6, None, ALU.arith_shift_right)
                    else:
                        V.tensor_scalar(key_i, dst_i, NKEY - 1, None, ALU.bitwise_and)
                    drain()
                    V.tensor_copy(key, key_i)
                    drain()
                    with dve.Fori(0, NKEY) as b:
                        V.tensor_scalar(hit, key, iota[:, bass.ds(b, 1)], 0.0, ALU.is_equal, ALU.add,
                                        accum_out=tot[:, bass.ds(b, 1)])
                        drain()
                    V.tensor_tensor_scan(totc[:], tot[:], zeros[:, 0:NKEY], 0.0, ALU.add, ALU.add)
                    drain()
                    V.tensor_tensor(totc[:], totc[:], tot[:], ALU.subtract).then_inc(so_tot, 1)
                    dve.wait_ge(so_base, n + 1)
                    V.tensor_scalar(base[:], psG[:, 1, 0, 0:NKEY], -1.0, None, ALU.add)
                    drain()
                    places(NKEY)
                    V.tensor_copy(place_i, place).then_inc(so_place, 1)
                dve.wait_ge(so_pass, 2)
            with dve.Else():
                dve.nop()

            for m in range(2):
                first, below = tm[0:NBX, 8 + 2 * m:9 + 2 * m], tm[0:NBX, 9 + 2 * m:10 + 2 * m]
                V.tensor_tensor(tm[0:NBX, 0:1], below, first, ALU.subtract)
                drain()
                V.tensor_scalar(tmi[0:NBX, :], tm[0:NBX, 0:1], float(P - 1), None, ALU.add)
                drain()
                V.tensor_scalar(tmi2[0:NBX, :], tmi[0:NBX, :], 7, None, ALU.arith_shift_right)
                drain()
                V.tensor_copy(tm[0:NBX, 2:3], tmi2[0:NBX, :]).then_inc(map_col, 1)
                dve.wait_ge(map_mm, 3 * m + 1)
                V.tensor_copy(tm[0:NBX, 3:4], psG[0:NBX, 1, 2, 0:1])
                drain()
                V.tensor_tensor(tm[0:NBX, 4:5], tm[0:NBX, 3:4], tm[0:NBX, 2:3], ALU.add)
                V.tensor_scalar(tm[0:NBX, 5:6], ident[0:NBX, NB:NB + 1], 1e6, None, ALU.mult)
                V.tensor_scalar(tm[0:NBX, 6:7], tm[0:NBX, 3:4], -float(P), None, ALU.mult)
                drain()
                V.tensor_tensor(tm[0:NBX, 4:5], tm[0:NBX, 4:5], tm[0:NBX, 5:6], ALU.add)
                V.tensor_tensor(tm[0:NBX, 6:7], tm[0:NBX, 6:7], first, ALU.add)
                drain()
                V.tensor_scalar(map_tmp[0:NBX, :], tile_no[0:NBX, :], tm[0:NBX, 3:4], None, ALU.is_ge)
                V.tensor_scalar(map_tmp2[0:NBX, :], tile_no[0:NBX, :], tm[0:NBX, 4:5], None, ALU.is_lt)
                drain()
                V.tensor_tensor(map_tmp[0:NBX, :], map_tmp[0:NBX, :], map_tmp2[0:NBX, :], ALU.mult)
                drain()
                for i in range(2):
                    V.tensor_scalar(map_rhs[0:NBX, :], map_tmp[0:NBX, :],
                                    node_no[0:NBX, :] if i == 0 else tm[0:NBX, 6:7], None, ALU.mult)\
                        .then_inc(map_col, 1)
                    dve.wait_ge(map_mm, 3 * m + 2 + i)
                    for c in range(2):
                        ps = psA[:, 2 * c:2 * c + 2, :].rearrange("p a b -> p (a b)")[:, 0:T // 2]
                        cs = slice(c * (T // 2), (c + 1) * (T // 2))
                        if i == 0:
                            row = 0 if m == 0 else 32
                            V.tensor_copy(maps[row:row + 32, cs], ps[row:row + 32, :])
                            V.tensor_scalar((block_lo if m == 0 else src_lo)[:, cs], ps, float(P), None, ALU.mult)
                        else:
                            row = 96 if m == 0 else 64
                            V.scalar_tensor_tensor(map_tmp2[:, cs], tile_no[:, cs], float(P), ps, ALU.mult, ALU.add)
                            drain()
                            V.tensor_scalar(maps[row:row + 32, cs], map_tmp2[row:row + 32, cs], float(E), None, ALU.min)
                    drain()
            V.tensor_copy(tm[:, 0:1], ones[:, 0:1]).then_inc(map_set, 1)

            for k in range(8):
                dve.wait_ge(win_in[k], 16 * (T // 8))
            V.tensor_copy(sc_t, tiles[:, :, EE_:EE_ + HEADS])
            V.tensor_tensor(dst_local[:, 0:T], tiles[:, :, D_], block_lo[:], ALU.subtract)
            V.tensor_copy(weight[:], tiles[:, :, W_])
            V.tensor_copy(src_f[:], tiles[:, :, S_])
            V.tensor_scalar(map_tmp, tiles[:, :, POS_], -float(E), None, ALU.add)
            V.tensor_scalar(dst_id, tiles[:, :, D_], 1.0, None, ALU.add)
            drain()
            V.tensor_scalar(map_tmp2, dst_local[:, 0:T], float(P), None, ALU.is_lt)
            V.tensor_scalar(map_rhs, src_f[:], float(NB * P - 1), None, ALU.min)
            drain()
            V.tensor_tensor(map_tmp, map_tmp, map_tmp2, ALU.mult)
            V.tensor_tensor(dst_id, dst_id, map_tmp2, ALU.mult)
            V.scalar_tensor_tensor(idx_b[:, 0:T], map_rhs, float(NREL), tiles[:, :, T_], ALU.mult, ALU.add)
            drain()
            V.tensor_scalar(idx_a[:, 0:T], map_tmp, float(E), None, ALU.add).then_inc(tiles_set, 1)
            V.tensor_copy(by_chunk, dst_id.rearrange("p (c j o) -> p c j o", c=CH, o=1)
                          .to_broadcast([P, CH, CT, HEADS])).then_inc(mv_rdy, 1)
            to_scan_out(0)
            V.tensor_copy(ends[:, 0:1], SCAN[:, 0:1])
            V.tensor_copy(ends[:, 1:2], SCAN[:, CE - 1:CE]).then_inc(edge_in, 1)
            V.tensor_tensor(flags[:, 1:CE], SCAN[:, 1:CE], SCAN[:, 0:CE - 1], ALU.not_equal)
            dve.wait_ge(edge_mm, 1)
            V.tensor_tensor(flags[:, 0:1], ends[:, 0:1], psG[:, 0, 0, 0:1], ALU.not_equal)
            V.tensor_tensor(flags[:, CE:CE + 1], ends[:, 1:2], psG[:, 0, 0, 1:2], ALU.not_equal)
            drain()
            V.tensor_scalar(flags[:, 0:CE + 1], flags[:, 0:CE + 1], -BIG, None, ALU.mult)
            drain()
            V.tensor_reduce(ends[:, 2:3], flags[:, 0:CE], AXX, ALU.min)
            V.tensor_reduce(ends[:, 3:4], flags[:, 1:CE + 1], AXX, ALU.min).then_inc(edge_in, 1)
            dve.wait_ge(edge_mm, 2)
            V.tensor_copy(link[0:1, :, :], psG[0:1, 0, 0:2, :])
            V.memset(acc[:, :, :], 0.0)

            dve.wait_ge(x_in, 32)
            layernorm(1)
            for b in range(NB):
                block_out(0, b, lambda b, ps: V.tensor_copy(nodes[:, b, :], ps[:, 0:F]))
            V.tensor_tensor(X[:, :, :], X[:, :, :], H, ALU.add)
            drain()
            one_hots(0, 0)

            def messages(g):
                for k in range(4):
                    wait_if(dve, tr_done, g * 4 + (at_quad["0a"] + k))
                    one_hots(g * BODY + 4 * (k + 1), k + 1)
                    dve.wait_ge(got, g * 4 + (at_quad["0a"] + k + 1))
                    for j in range(QUAD):
                        wait_if(dve, slot[4 * k + j], g * 16)
                    V.tensor_tensor(msg_ring[:, 4 * k:4 * k + 4, 0:F], psG[:, k % 2, :, :],
                                    bc(weight[:, bass.ds(g * BODY + 4 * k, QUAD)], F), ALU.mult)
                    V.tensor_copy(msg_ring[:, 4 * k:4 * k + 4, F], src_f[:, bass.ds(g * BODY + 4 * k, QUAD)])
                    V.tensor_copy(idx_ring[:, 4 * k:4 * k + 4], idx_a[:, bass.ds(g * BODY + 4 * k, QUAD)])\
                        .then_inc(quad_rdy, 1)
            bodies(dve, messages)
            dve.wait_ge(msgs_done, 1)
            V.tensor_scalar(idx_a[:, 0:T], src_f[:], float(NB * P - 1), None, ALU.min)

            def message_sums(g):
                for h in range(2):
                    regs = blocks_of(ENG.DVE, 32, g * BODY + h * HALF, HALF)
                    for j in range(HALF):
                        dve.wait_ge(msg_in[h * HALF + j], g * 16 + 16)
                    dve.wait_ge(oh_rdy, g * 2 + (at_oh["0b"] + h))
                    V.tensor_tensor(src_local[:, h * HALF:(h + 1) * HALF], msg_ring[:, h * HALF:(h + 1) * HALF, F],
                                    src_lo[:, bass.ds(g * BODY + h * HALF, HALF)], ALU.subtract).then_inc(src_sub, 1)
                    dve.wait_ge(src_sub, g * 2 + (h + 1))
                    V.tensor_tensor(onehot[:, h, :, :], rep(iota[:, :], HALF),
                                    bc(src_local[:, h * HALF:(h + 1) * HALF], P), ALU.is_equal).then_inc(oh_rdy, 1)
                    for j in range(HALF):
                        add("0b", regs[j], g, h * HALF + j, j, F)
            bodies(dve, message_sums)
            dve.wait_ge(added, at_agg["0b"] + T)
            V.tensor_tensor(H, acc[:, 0:NB, 0:F], rep(vecs[:, 0, :], NB), ALU.add).then_inc(bn_in, 1)
            dve.wait_ge(bn_mm, 1)
            V.tensor_scalar(bn[:, 0, :], psG[:, 0, 0, :], 1.0 / N, None, ALU.mult)
            drain()
            V.tensor_tensor(H, H, rep(bn[:, 0, :], NB), ALU.subtract)
            drain()
            V.tensor_tensor(H2, H, H, ALU.mult).then_inc(bn_in, 1)
            dve.wait_ge(bn_mm, 2)
            V.tensor_scalar(bn[:, 1, :], psG[:, 0, 0, :], 1.0 / N, LN_EPS, ALU.mult, ALU.add).then_inc(bn_var, 1)
            dve.wait_ge(bn_sd, 1)
            V.reciprocal(bn[:, 3, :], bn[:, 2, :])
            drain()
            V.tensor_tensor(bn[:, 3, :], bn[:, 3, :], vecs[:, 1, :], ALU.mult)
            drain()
            V.tensor_tensor(H, H, rep(bn[:, 3, :], NB), ALU.mult)
            drain()
            V.tensor_tensor(H, H, rep(vecs[:, 2, :], NB), ALU.add)
            drain()
            V.scalar_tensor_tensor(X[:, :, :], H, 0.0, X[:, :, :], ALU.max, ALU.add)
            V.memset(acc[:, :, :], 0.0)
            drain()

            layernorm(2)

            def rel_out(b, ps):
                if b >= 2:
                    dve.wait_ge(tab_out[b % 2], 16 * (b // 2))
                return V.tensor_copy(rel_stage[:, b % 2, 512:1024], ps[:, 512:1024])
            for b in range(NB):
                block_out(1, b, rel_out)
            one_hots(0, 0)
            with dve.Fori(0, BODIES) as g:
                for k in range(4):
                    dve.wait_ge(agg, g * BODY + (at_agg["1"] + 4 * k))
                    one_hots(g * BODY + 4 * (k + 1), k + 1)
                    regs = blocks_of(ENG.DVE, 0, g * BODY + 4 * k, QUAD)
                    for j in range(QUAD):
                        add("1", regs[j], g, 4 * k + j, (4 * k + j) % HALF, F)
            dve.wait_ge(added, at_agg["1"] + T)
            V.tensor_tensor(X[:, :, :], X[:, :, :], acc[:, 0:NB, 0:F], ALU.add)
            drain()
            V.memset(acc[:, :, :], 0.0)

            layernorm(3)

            def gat_out(b, ps):
                V.tensor_copy(H2[:, b, 0:HEADS], ps[:, 0:HEADS])
                return V.tensor_copy(s_dst[:, b, :], ps[:, HEADS:2 * HEADS])
            for b in range(NB):
                block_out(2, b, gat_out)
            one_hots(0, 0)
            with dve.Fori(0, BODIES) as g:
                for k in range(4):
                    dve.wait_ge(tr_done, g * 4 + (at_quad["2a"] + k))
                    one_hots(g * BODY + 4 * (k + 1), k + 1)
                    dve.wait_ge(got, g * 4 + (at_quad["2a"] + k + 1))
                    for j in range(QUAD):
                        dve.wait_ge(slot[4 * k + j], g * 16 + (at_slot["2a"] + 16))
                    V.tensor_tensor(sc_t[:, bass.ds(g * BODY + 4 * k, QUAD), :], psG[:, k % 2, :, 0:HEADS],
                                    gat_ring[:, 4 * k:4 * k + 4, F:F + HEADS], ALU.add).then_inc(quad_rdy, 1)
            dve.wait_ge(quad_rdy, at_quad["3a"])
            V.scalar_tensor_tensor(scores[:, :], scores[:, :], 0.2, scores[:, :], ALU.mult, ALU.max)
            drain()
            V.tensor_copy(by_chunk, sc).then_inc(mv_rdy, 1)
            for k in range(4):
                dve.wait_ge(wb[k], 16 * BODIES)
            to_scan_out(1)
            segment_max(0)
            V.tensor_scalar(MAXS, MAXS, 0.0, None, ALU.max)
            drain()
            V.tensor_tensor(MAXS, SCAN, MAXS, ALU.subtract).then_inc(diff_rdy, 1)
            dve.wait_ge(exp_rdy, 1)
            V.tensor_copy(carry[:, 0:1], ones[:, 0:1]).then_inc(mv_rdy, 1)
            from_scan_out(2)
            V.tensor_copy(carry[:, 0:1], ones[:, 0:1]).then_inc(ring_free, 1)
            weighted(2)
            shares(ALU.max)
            drain()
            V.tensor_tensor(X[:, :, :], X[:, :, :], H, ALU.add)
            V.memset(acc[:, :, :], 0.0)
            drain()

            layernorm(4)

            def kv_out(b, ps):
                if b >= 2:
                    dve.wait_ge(tab_out[b % 2], 16 * (b // 2 + tab_at[2][b % 2]))
                V.tensor_tensor(nodes[:, b, :], ps[:, 0:F], vecs[:, 3, :], ALU.add)
                return V.tensor_tensor(kv_stage[:, b % 2, :], ps[:, F:3 * F],
                                       vecs[:, 4:6, :].rearrange("p a f -> p (a f)"), ALU.add)
            for b in range(NB):
                block_out(3, b, kv_out)
            one_hots(0, 0)
            with dve.Fori(0, BODIES) as g:
                for k in range(4):
                    dve.wait_ge(tr_done, g * 4 + (at_quad["3a"] + k))
                    one_hots(g * BODY + 4 * (k + 1), k + 1)
                    dve.wait_ge(got, g * 4 + (at_quad["3a"] + k + 1))
                    for j in range(QUAD):
                        dve.wait_ge(slot[4 * k + j], g * 16 + (at_slot["3a"] + 16))
                    dve.wait_ge(quad_rdy, g * 4 + (at_quad["3a"] + k))
                    V.tensor_tensor(prod.rearrange("p (s w) -> p s w", w=F), psG[:, k % 2, :, :],
                                    kv_ring[:, 4 * k:4 * k + 4, 0:F], ALU.mult).then_inc(prod_rdy, 1)
                    dve.wait_ge(prod_rdy, g * 4 + (k + 1))
                    V.tensor_reduce(scores[:, bass.ds(g * (BODY * HEADS) + 4 * k * HEADS, QUAD * HEADS)],
                                    prod.rearrange("p (s d) -> p s d", d=HD), AXX, ALU.add).then_inc(quad_rdy, 1)
            dve.wait_ge(quad_rdy, at_quad["3a"] + NQ)
            V.tensor_copy(carry[:, 0:1], ones[:, 0:1]).then_inc(raw_done, 1)
            dve.wait_ge(bias_in, 16)
            V.scalar_tensor_tensor(scores[:, :], scores[:, :], float(HD) ** -0.5, work[:, 0:T * HEADS],
                                   ALU.mult, ALU.add)
            drain()
            V.tensor_copy(by_chunk, sc).then_inc(mv_rdy, 1)
            to_scan_out(3)
            segment_max(2)
            V.tensor_tensor(MAXS, SCAN, MAXS, ALU.subtract).then_inc(diff_rdy, 1)
            dve.wait_ge(exp_rdy, 2)
            V.tensor_copy(carry[:, 0:1], ones[:, 0:1]).then_inc(mv_rdy, 1)
            from_scan_out(4)
            V.tensor_copy(carry[:, 0:1], ones[:, 0:1]).then_inc(ring_free, 1)
            weighted(3)
            shares(ALU.add)
            drain()
            V.tensor_tensor(X[:, :, :], X[:, :, :], rep(vecs[:, 6, :], NB), ALU.add).then_inc(h_rdy, 1)
            for b in range(NB):
                block_out(4, b, lambda b, ps: V.tensor_tensor(X[:, b, :], X[:, b, :], ps[:, 0:F], ALU.add))


_INS = ["x", "src", "dst", "edge_attr_32", "edge_type_8", "edge_weight", "L0_gnn_weight", "L0_gnn_bias",
        "L0_gnn_bn_gamma", "L0_gnn_bn_beta", "L1_gnn_weight", "L2_gnn_att", "L3_gnn_Wq", "L3_gnn_bq",
        "L3_gnn_Wk", "L3_gnn_bk", "L3_gnn_Wv", "L3_gnn_bv", "L3_gnn_We", "L3_gnn_be", "L3_gnn_Wo", "L3_gnn_bo"]


def kernel(**inputs):
    import numpy as np
    import concourse.bacc as bacc
    from concourse.bass_utils import run_bass_kernel_spmd

    nc = bacc.Bacc("TRN2", target_bir_lowering=False, num_devices=1)
    arrays, args = {}, {}
    for name in _INS:
        arr = np.ascontiguousarray(inputs[name])
        arrays[f"in_{name}"] = arr
        args[name] = nc.dram_tensor(f"in_{name}", arr.shape, mybir.dt.from_np(arr.dtype), kind="ExternalInput").ap()
    out = nc.dram_tensor("out_x", (N, F), F32, kind="ExternalOutput").ap()
    gnn(nc, args, out)
    r = run_bass_kernel_spmd(nc, [arrays], core_ids=[0])
    return r.results[0]["out_x"]
```

```python
import concourse.bass as bass
from concourse import mybir
from contextlib import ExitStack

F32 = mybir.dt.float32
BF16 = mybir.dt.bfloat16
I32 = mybir.dt.int32
ALU = mybir.AluOpType
ACT = mybir.ActivationFunctionType
AXX = mybir.AxisListType.X
ENG = mybir.EngineType

P = 128
N = 3125
F = 128
E = 100000
EF = 32
NREL = 8
HEADS = 8
HD = F // HEADS
NB = -(-N // P)
NBX = NB + 1
NLAST = N - (NB - 1) * P
EP = 125
EC = E // EP
REC = 16
D_, S_, T_, W_, POS_, EE_ = 0, 1, 2, 3, 4, 8
NKEY = 64
PADKEY = NKEY * NKEY - 1
BODY = 16
QUAD = 4
HALF = 8
T = -(-(E // P + 1 + NB) // BODY) * BODY
BODIES = T // BODY
CH = P // HEADS
CT = T // CH
CE = CT * P
BIG = 1e30
LN_EPS = 1e-5
ATT = 16
ATT_BUFS = 5
GROUPS = P * EC // P
MG_T = E // P
TC = -(-T // P)
MSG = F + 1
PLACES = P * T
NQ = T // QUAD
NH = T // HALF
MG = -(-CT // QUAD)
N_CONSTS = 6 + 7 + 2 * QUAD + 2 * HEADS
assert EP * EC == E and T % CH == 0 and EC % (2 * ATT * ATT_BUFS) == 0 and T * REC * 4 <= 56 * 1024
assert CE * CH == T * P and 2 * CE <= T * REC


def gnn(nc, a, out):
    ctx = ExitStack()
    with ctx:
        def sb(name, shape, dt=F32):
            return ctx.enter_context(nc.sbuf_tensor(name, shape, dt))

        def sem(name):
            return ctx.enter_context(nc.semaphore(name))

        def dram(name, shape, dt=F32):
            return nc.dram_tensor(name, shape, dt, kind="Internal").ap()

        rec = dram("rec", [P * EC, REC])
        rec2 = dram("rec2", [P * EC, REC])
        msgs = dram("msgs", [PLACES, MSG])
        rel_table = dram("rel_table", [NB * P * NREL, F])
        gat_table = dram("gat_table", [NB * P, F + HEADS])
        kv_table = dram("kv_table", [NB * P, 2 * F])
        rows_seq = dram("rows_seq", [P, T * F])
        bias_seq = dram("bias_seq", [P, T * HEADS])

        work = sb("work", [P, T * REC])
        scores = sb("scores", [P, T * HEADS])
        flags = sb("flags", [P, CE + 2], BF16)
        X = sb("X", [P, NB, F])
        nodes = sb("nodes", [P, NBX, F])
        acc = sb("acc", [P, NBX, F + HEADS])
        onehot = sb("onehot", [P, 2, HALF, P])
        onehot_t = sb("onehot_t", [P, 2, QUAD, P])
        dst_local = sb("dst_local", [P, T + BODY])
        fields = sb("fields", [P, 5, T])
        block_lo = sb("block_lo", [P, T])
        maps = sb("maps", [P, T], I32)
        idx_a = sb("idx_a", [P, T + BODY], I32)
        idx_b = sb("idx_b", [P, T + BODY], I32)
        idx_ring = sb("idx_ring", [P, BODY], I32)
        ident_w = sb("ident_w", [P, P + 2 * HEADS])
        node_no_i = sb("node_no_i", [P, 1], I32)
        node_no = sb("node_no", [P, 1])
        ones = sb("ones", [P, P])
        lower = sb("lower", [P, P])
        iota = sb("iota", [P, P])
        iota_i = sb("iota_i", [P, P], I32)
        thr = sb("thr", [P, NKEY])
        head_mask = sb("head_mask", [P, HEADS])
        att_col = sb("att_col", [P, 2])
        att_blk = sb("att_blk", [P, 2 * HEADS])
        s_dst = sb("s_dst", [P, NBX, HEADS])
        we_blk = sb("we_blk", [P, QUAD * HEADS])
        be_row = sb("be_row", [1, QUAD * HEADS])
        attr = sb("attr", [P, ATT_BUFS, ATT, EF])
        w0 = sb("w0", [P, F])
        w_rel = sb("w_rel", [P, NREL, F])
        wqkv = sb("wqkv", [P, 3, F])
        wo = sb("wo", [P, F])
        vecs = sb("vecs", [P, 7, F])
        hT = sb("hT", [P, 2, F])
        col = sb("col", [P, 8, NB])
        cum = sb("cum", [P, 2, 28])
        tot = sb("tot", [P, NKEY])
        totc = sb("totc", [P, NKEY])
        base = sb("base", [P, NKEY])
        below = sb("below", [NBX, 4])
        rounded = sb("rounded", [NBX, 3], I32)
        rounded_f = sb("rounded_f", [NBX, 3])
        n_tiles = sb("n_tiles", [NBX, 2])
        first_tile = sb("first_tile", [NBX, 2])
        end_tile = sb("end_tile", [NBX, 2])
        shift = sb("shift", [NBX, 1])
        bounds = sb("bounds", [NBX, 3])
        diag = sb("diag", [NBX, 3, NBX])
        group_f = sb("group_f", [P, TC])
        group_i = sb("group_i", [P, TC], I32)
        gap = sb("gap", [P, 4, NB])
        gap_i = sb("gap_i", [P, 3, NB], I32)
        nxt = sb("nxt", [P, 2], I32)
        flag = sb("flag", [P, 1], I32)
        vio = sb("vio", [P, 4])
        bn = sb("bn", [P, 4, F])
        ends = sb("ends", [P, 4])
        link = sb("link", [1, 2, P])
        tails = sb("tails", [1, P])
        carried = sb("carried", [1, P + 2 * HEADS])
        carry = sb("carry", [P, 1])
        psA = ctx.enter_context(nc.psum_tensor("psA", [P, HALF, 256], F32))
        psT = ctx.enter_context(nc.psum_tensor("psT", [P, 2, QUAD, P], F32))
        psG = ctx.enter_context(nc.psum_tensor("psG", [P, 2, QUAD, P], F32))

        recs = work[:, 0:EC * REC].rearrange("p (c w) -> p c w", w=REC)
        H = work[:, 0:NB * F].rearrange("p (b f) -> p b f", f=F)
        H2 = work[:, NB * F:2 * NB * F].rearrange("p (b f) -> p b f", f=F)
        SCAN = work[:, 0:CE]
        MAXS = work[:, CE:2 * CE]
        sc_t = scores[:, :].rearrange("p (t h) -> p t h", h=HEADS)
        by_chunk = MAXS.rearrange("p (j c h) -> p c j h", c=CH, h=HEADS)
        sc_c = scores[:, :].rearrange("p (c j h) -> p j c h", c=CH, h=HEADS)
        msg_ring = work[:, 0:BODY * MSG].rearrange("p (s w) -> p s w", w=MSG)
        SRC0 = BODY * MSG
        group_rows = [work[:, c * P * REC:(c + 1) * P * REC] for c in range(TC - 1)] + [
            attr[:, :, :, :].rearrange("p a b c -> p (a b c)")[:, 0:P * REC]]
        src_lo = flags[:, 0:2 * T].bitcast(F32)
        src_f = fields[:, 1, :]
        weight = fields[:, 3, :]
        src_local = work[:, SRC0:SRC0 + 2 * HALF]
        gat_ring = work[:, 0:BODY * (F + HEADS)].rearrange("p (s w) -> p s w", w=F + HEADS)
        kv_ring = work[:, 0:BODY * 2 * F].rearrange("p (s w) -> p s w", w=2 * F)
        row_ring = work[:, 0:BODY * F].rearrange("p (s w) -> p s w", w=F)
        prod = work[:, BODY * 2 * F:BODY * 2 * F + QUAD * F]
        seq_ring = work[:, 0:2 * HALF * F].rearrange("p (r s w) -> p r s w", r=2, w=F)
        wgt0 = 2 * HALF * F
        wgt_ring = work[:, wgt0:wgt0 + 2 * HALF * (F + HEADS)].rearrange(
            "p (r s w) -> p r s w", r=2, w=F + HEADS)
        stage0 = 2 * NB * F
        rel_stage = work[:, stage0:stage0 + 2 * NREL * F].rearrange("p (r w) -> p r w", r=2)
        kv_stage = rel_stage[:, :, 0:2 * F]

        dst_i = scores[:, 0:EC].bitcast(I32)
        src_i = scores[:, EC:2 * EC].bitcast(I32)
        typ_i = scores[:, 2 * EC:3 * EC].bitcast(I32)
        w_in = scores[:, 3 * EC:4 * EC]
        key = scores[:, 4 * EC:5 * EC]
        hit = scores[:, 5 * EC:6 * EC]
        cnt = scores[:, 6 * EC:7 * EC]
        key_i = scores[:, 7 * EC:8 * EC].bitcast(I32)
        zeros = onehot[:, :, :, :].rearrange("p a b c -> p (a b c)")[:, 0:EC]
        place = onehot[:, :, :, :].rearrange("p a b c -> p (a b c)")[:, EC:2 * EC]
        ident = ident_w[:, HEADS:HEADS + P]
        place_i = acc[:, :, :].rearrange("p b f -> p (b f)")[:, 0:EC].bitcast(I32)
        sort_rec = acc[:, :, :].rearrange("p b f -> p (b f)")[:, EC:EC + HALF * REC].rearrange(
            "p (c w) -> p c w", w=REC)
        dst_id = acc[:, :, :].rearrange("p b f -> p (b f)")[:, 0:T]
        map_tmp = onehot[:, :, :, :].rearrange("p a b c -> p (a b c)")[:, 0:T]
        map_tmp2 = onehot[:, :, :, :].rearrange("p a b c -> p (a b c)")[:, T:2 * T]
        map_rhs = acc[:, :, :].rearrange("p b f -> p (b f)")[:, T:2 * T]
        tile_no = acc[:, :, :].rearrange("p b f -> p (b f)")[:, 2 * T:3 * T]
        tile_no_i = tile_no.bitcast(I32)
        place_t = acc[:, :, :].rearrange("p b f -> p (b f)")[:, 3 * T:4 * T].bitcast(I32)
        place_t2 = idx_a[:, 0:T]

        def bc(ap, n):
            return ap.rearrange("p (k o) -> p k o", o=1).to_broadcast([ap.shape[0], ap.shape[1], n])

        def rep(ap, n):
            return ap.rearrange("p (o k) -> p o k", o=1).to_broadcast([ap.shape[0], n, ap.shape[1]])

        def blocks_of(engine, row, first, n):
            _, regs = nc.values_load_multi_w_load_instructions(
                maps[row:row + 1, bass.ds(first, n)], engines=[engine], min_val=0, max_val=NB,
                skip_runtime_bounds_check_because="the tile map points to blocks 0 to NB")
            return regs

        pads_set = sem("pads_set")
        edges_in = sem("edges_in")
        consts_in = sem("consts_in")
        x_in = sem("x_in")
        row_zero = sem("row_zero")
        work_zero = sem("work_zero")
        work_free = sem("work_free")
        iota_set = sem("iota_set")
        dve_consts = sem("dve_consts")
        attr_in = [sem(f"attr_in{i}") for i in range(ATT_BUFS)]
        attr_t = sem("attr_t")
        attr_t_sb = sem("attr_t_sb")
        attr_mm = sem("attr_mm")
        bias_put = sem("bias_put")
        counts_set = sem("counts_set")
        base_mm = sem("base_mm")
        recs_set = sem("recs_set")
        rec_out = sem("rec_out")
        flag_set = sem("flag_set")
        so_tot = sem("so_tot")
        so_base = sem("so_base")
        so_place = sem("so_place")
        so_copy = sem("so_copy")
        so_sent = sem("so_sent")
        so_pass = sem("so_pass")
        so_in = sem("so_in")
        map_col = sem("map_col")
        map_mm = sem("map_mm")
        map_set = sem("map_set")
        gap_set = sem("gap_set")
        gap_out = sem("gap_out")
        tail_out = sem("tail_out")
        group_in = [sem(f"group_in{i}") for i in range(TC)]
        group_t = sem("group_t")
        field_copy = [sem(f"field_copy{i}") for i in range(2)]
        base_set = sem("base_set")
        bias_out = sem("bias_out")
        bias_in = sem("bias_in")
        tiles_set = sem("tiles_set")
        slot = [sem(f"slot{i}") for i in range(BODY)]
        msg_in = [sem(f"msg_in{i}") for i in range(2)]
        wb = [sem(f"wb{i}") for i in range(QUAD)]
        seq_in = [sem(f"seq_in{i}") for i in range(2)]
        idx_rdy = sem("idx_rdy")
        oh_rdy = sem("oh_rdy")
        tr_done = sem("tr_done")
        oht_rdy = sem("oht_rdy")
        got = sem("got")
        pool_turns = sem("pool_turns")
        quad_rdy = sem("quad_rdy")
        prod_rdy = sem("prod_rdy")
        agg = sem("agg")
        added = sem("added")
        wgt_rdy = sem("wgt_rdy")
        src_sub = sem("src_sub")
        ln_var = sem("ln_var")
        ln_sd = sem("ln_sd")
        h_rdy = sem("h_rdy")
        h_t = sem("h_t")
        h_t_sb = sem("h_t_sb")
        h_mm = sem("h_mm")
        h_out = sem("h_out")
        h_out_act = sem("h_out_act")
        tab_out = [sem(f"tab_out{i}") for i in range(2)]
        msgs_done = sem("msgs_done")
        bn_in = sem("bn_in")
        bn_mm = sem("bn_mm")
        bn_var = sem("bn_var")
        bn_sd = sem("bn_sd")
        mv_rdy = sem("mv_rdy")
        mv_t = sem("mv_t")
        mv_copy = sem("mv_copy")
        edge_in = sem("edge_in")
        edge_mm = sem("edge_mm")
        raw_done = sem("raw_done")
        diff_rdy = sem("diff_rdy")
        exp_rdy = sem("exp_rdy")
        ring_free = sem("ring_free")
        out_done = sem("out_done")
        block = ctx.enter_context(nc.Block())

        at_slot = {"0a": 0, "1": 16 * BODIES, "2a": 32 * BODIES, "3a": 48 * BODIES}
        at_agg = {"0b": 0, "1": T, "2b": 2 * T, "3b": 3 * T}
        at_added = {ph: at + HALF * (i + 1) for i, (ph, at) in enumerate(at_agg.items())}
        at_quad = {"0a": 0, "2a": NQ, "3a": 2 * NQ}
        at_half = {"2b": 0, "3b": NH}
        at_idx = {"1": 0, "2a": NQ + 3, "3a": 2 * (NQ + 3)}
        at_oh = {"0a": 0, "0b": NQ + 1, "1": NQ + 1 + NH, "2a": 2 * (NQ + 1) + NH, "2b": 3 * (NQ + 1) + NH,
                 "3a": 3 * (NQ + 1) + 2 * NH, "3b": 4 * (NQ + 1) + 2 * NH}
        tab_at = {0: (0, 0), 1: (13, 12), 2: (14, 13), 3: (27, 25)}

        def bodies(engine, body):
            body(0)
            with engine.Fori(1, BODIES) as g:
                body(g)

        def wait_if(engine, semaphore, value):
            if not (isinstance(value, int) and value == 0):
                engine.wait_ge(semaphore, value)

        def half_blocks(engine, row, first):
            return blocks_of(engine, row, first, 1)[0], blocks_of(engine, row, first + (HALF - 1), 1)[0]

        def field_out(copy, engine, i):
            engine.wait_ge(group_t, i + 1)
            k = min(P, T - (i // 4) * P)
            ts = slice((i // 4) * P, (i // 4) * P + k)
            ps = psT[:, i % 2, :, 0:k]
            if i % 4 == 0:
                ins = copy(fields[:, 0:4, ts], ps)
            elif i % 4 == 1:
                ins = copy(fields[:, 4, ts], ps[:, 0, :])
            else:
                h = 4 * (i % 4 - 2)
                ins = copy(sc_t[:, ts, h:h + 4].rearrange("p t h -> p h t"), ps)
            ins.then_inc(field_copy[i % 2], 1)

        def pout(b):
            return psA[:, 4 * (b % 2):4 * (b % 2) + 4, :].rearrange("p a b -> p (a b)")

        @block.sync
        def _(sp):
            sp.wait_ge(pads_set, 1)
            for dst, name in ((dst_i, "dst"), (src_i, "src"), (typ_i, "edge_type_8")):
                sp.dma_start(dst[0:EP, :], a[name].rearrange("(p c) -> p c", c=EC)).then_inc(edges_in, 16)
            sp.dma_start(w_in[0:EP, :], a["edge_weight"].rearrange("(p c) -> p c", c=EC)).then_inc(edges_in, 16)
            with nc.allow_non_contiguous_dma("one element of each partition's successor"):
                sp.dma_start(nxt[0:EP - 1, 0:1], a["dst"].rearrange("(p c) -> p c", c=EC)[1:EP, 0:1])\
                    .then_inc(edges_in, 16)
            attr_d = a["edge_attr_32"].rearrange("(p c) f -> p c f", c=EC)
            for i in range(ATT_BUFS):
                sp.dma_start(attr[0:EP, i, :, :], attr_d[:, i * ATT:(i + 1) * ATT, :]).then_inc(attr_in[i], 16)
            with sp.Fori(0, EC // ATT // ATT_BUFS - 1) as g:
                for i in range(ATT_BUFS):
                    sp.wait_ge(attr_mm, g * ATT_BUFS + (i + 1))
                    sp.dma_start(attr[0:EP, i, :, :],
                                 attr_d[:, bass.ds(g * (ATT_BUFS * ATT) + (i + ATT_BUFS) * ATT, ATT), :])\
                        .then_inc(attr_in[i], 16)
            sp.wait_ge(recs_set, 1)
            sp.dma_start(rec.rearrange("(p c) w -> p (c w)", c=EC), work[:, 0:EC * REC]).then_inc(rec_out, 16)
            sp.wait_ge(rec_out, 16)
            sp.wait_ge(flag_set, 1)
            unsorted = sp.value_load(flag[0:1, 0:1], min_val=0, max_val=1)
            with sp.If(unsorted):
                sp.wait_ge(so_pass, 1)
                sp.dma_start(work[:, 0:EC * REC], rec2.rearrange("(p c) w -> p (c w)", c=EC)).then_inc(so_in, 16)
                sp.wait_ge(so_pass, 2)
            with sp.Else():
                sp.nop()
            sp.wait_ge(tiles_set, 1)
            sp.dma_start(bias_seq, scores[:, :]).then_inc(bias_out, 16)
            msgs_p = msgs.rearrange("(p t) w -> p (t w)", t=T)

            def load_half(first, h):
                sp.dma_start(work[:, h * HALF * MSG:(h + 1) * HALF * MSG],
                             msgs_p[:, bass.ds(first * MSG, HALF * MSG)]).then_inc(msg_in[h], 16)
            sp.wait_ge(msgs_done, 1)
            load_half(0, 0)
            load_half(HALF, 1)
            with sp.Fori(0, BODIES - 1) as g:
                for h in range(2):
                    sp.wait_ge(agg, g * BODY + (at_agg["0b"] + (h + 1) * HALF))
                    load_half(g * BODY + (h + 2) * HALF, h)

            for b in range(NB):
                sp.wait_ge(h_out, NB + b + 1)
                sp.wait_ge(h_out_act, b + 1)
                sp.dma_start(rel_table.rearrange("(n r) f -> n (r f)", r=NREL)[b * P:(b + 1) * P, :],
                             rel_stage[:, b % 2, :]).then_inc(tab_out[b % 2], 16)

            def write_back(n, rows):
                g0 = at_slot[f"{n}a"]
                with sp.Fori(0, BODIES) as g:
                    for k in range(4):
                        for j in range(QUAD):
                            sp.wait_ge(slot[4 * k + j], g * 16 + (g0 + 16))
                        sp.dma_start(rows_seq[:, bass.ds(g * (BODY * F) + 4 * k * F, QUAD * F)]
                                     .rearrange("p (s w) -> p s w", w=F), rows(k)).then_inc(wb[k], 16)

            def read_rows(n):
                for k in range(4):
                    sp.wait_ge(wb[k], 16 * BODIES * (n - 1))
                sp.wait_ge(ring_free, n - 1)
                for h in range(2):
                    sp.dma_start(seq_ring[:, h, :, :], rows_seq[:, h * HALF * F:(h + 1) * HALF * F]
                                 .rearrange("p (s w) -> p s w", w=F)).then_inc(seq_in[h], 16)
                with sp.Fori(0, BODIES - 1) as g:
                    for h in range(2):
                        sp.wait_ge(wgt_rdy, g * 2 + (at_half[f"{n}b"] + h + 1))
                        sp.dma_start(seq_ring[:, h, :, :],
                                     rows_seq[:, bass.ds(g * (BODY * F) + (h + 2) * HALF * F, HALF * F)]
                                     .rearrange("p (s w) -> p s w", w=F)).then_inc(seq_in[h], 16)

            sp.wait_ge(h_rdy, 3)
            sp.dma_start(gat_table.rearrange("(b p) w -> p b w", p=P)[:, :, 0:F], H).then_inc(tab_out[0], 16)
            sp.wait_ge(h_out, 3 * NB)
            sp.dma_start(gat_table.rearrange("(b p) w -> p b w", p=P)[:, :, F:F + HEADS],
                         H2[:, :, 0:HEADS]).then_inc(tab_out[1], 16)
            write_back(2, lambda k: gat_ring[:, 4 * k:4 * k + 4, 0:F])
            read_rows(2)
            for b in range(NB):
                sp.wait_ge(h_out, 3 * NB + b + 1)
                sp.dma_start(kv_table[b * P:(b + 1) * P, :], kv_stage[:, b % 2, :]).then_inc(tab_out[b % 2], 16)
            write_back(3, lambda k: kv_ring[:, 4 * k:4 * k + 4, F:2 * F])
            for k in range(4):
                sp.wait_ge(wb[k], 16 * BODIES * 2)
            sp.wait_ge(raw_done, 1)
            sp.wait_ge(bias_out, 16)
            sp.dma_start(work[:, 0:T * HEADS], bias_seq).then_inc(bias_in, 16)
            read_rows(3)
            sp.wait_ge(h_out, 5 * NB)
            sp.dma_start(out[0:(NB - 1) * P, :].rearrange("(b p) f -> p b f", p=P), X[:, 0:NB - 1, :])\
                .then_inc(out_done, 16)
            sp.dma_start(out[(NB - 1) * P:N, :], X[0:NLAST, NB - 1, :]).then_inc(out_done, 16)
            sp.wait_ge(out_done, 32)

        @block.gpsimd
        def _(pool):
            nc.gpsimd.memset(ident_w[:], 0.0).then_inc(iota_set, 1)
            nc.gpsimd.memset(lower[:], 1.0).then_inc(iota_set, 1)
            nc.gpsimd.memset(head_mask[:], 1.0).then_inc(iota_set, 1)
            nc.gpsimd.iota(iota_i[:], pattern=[[1, P]], base=0, channel_multiplier=0).then_inc(iota_set, 1)
            nc.gpsimd.iota(node_no_i[:], pattern=[[1, 1]], base=0, channel_multiplier=1).then_inc(iota_set, 1)
            nc.gpsimd.iota(tile_no_i, pattern=[[1, T]], base=0, channel_multiplier=0).then_inc(iota_set, 1)
            pool.wait_ge(iota_set, 6)
            nc.gpsimd.affine_select(out=ident_w[:], in_=ident_w[:], compare_op=ALU.not_equal, fill=1.0,
                                    base=HEADS, pattern=[[-1, P + 2 * HEADS]], channel_multiplier=1)\
                .then_inc(iota_set, 1)
            nc.gpsimd.affine_select(out=lower[:], in_=lower[:], compare_op=ALU.is_gt, fill=0.0, base=0,
                                    pattern=[[1, P]], channel_multiplier=-1).then_inc(iota_set, 1)
            nc.gpsimd.affine_select(out=head_mask[:], in_=head_mask[:], compare_op=ALU.is_ge, fill=0.0, base=0,
                                    pattern=[[-HD, HEADS]], channel_multiplier=1).then_inc(iota_set, 1)
            pool.wait_ge(iota_set, 9)
            nc.gpsimd.affine_select(out=head_mask[:], in_=head_mask[:], compare_op=ALU.is_ge, fill=0.0,
                                    base=HD - 1, pattern=[[HD, HEADS]], channel_multiplier=-1)\
                .then_inc(iota_set, 1)
            nc.gpsimd.memset(bn[:, :, :], 0.0).then_inc(row_zero, 1)
            pool.wait_ge(row_zero, 1)
            pool.dma_start(msgs.rearrange("(p t) w -> p t w", t=T)[:, MG_T:T, :],
                           rep(bn[:, :, :].rearrange("p a f -> p (a f)")[:, 0:MSG], T - MG_T)).then_inc(tail_out, 16)
            pool.wait_ge(work_free, 1)
            pool.wait_ge(h_t, NB)
            nc.gpsimd.memset(work[:, :], 0.0).then_inc(work_zero, 1)
            pool.wait_ge(tail_out, 16)
            pool.wait_ge(gap_set, 1)
            for b in range(NB):
                nc.gpsimd.indirect_dma_start(
                    msgs, bass.IndirectOffsetOnAxis(ap=gap_i[:, 0, b:b + 1], axis=0),
                    bn[:, :, :].rearrange("p a f -> p (a f)")[:, 0:MSG], None,
                    bounds_check=PLACES - 1, oob_is_err=False).then_inc(gap_out, 16)
            pool.wait_ge(flag_set, 1)
            unsorted = pool.value_load(flag[0:1, 0:1], min_val=0, max_val=1)
            with pool.If(unsorted):
                pool.wait_ge(rec_out, 16)
                for n, target in enumerate((rec2, rec)):
                    pool.wait_ge(so_place, n + 1)
                    c0, s0 = n * 2 * (EC // HALF), n * 16 * HALF * (EC // HALF)
                    with pool.Fori(0, EC // HALF) as g:
                        nc.gpsimd.tensor_copy(sort_rec, recs[:, bass.ds(g * HALF, HALF), :]).then_inc(so_copy, 1)
                        nc.gpsimd.tensor_copy(idx_ring[:, 0:HALF], place_i[:, bass.ds(g * HALF, HALF)])\
                            .then_inc(so_copy, 1)
                        pool.wait_ge(so_copy, g * 2 + (c0 + 2))
                        pool.sem_inc(pool_turns, 1)
                        for j in range(HALF):
                            nc.gpsimd.indirect_dma_start(
                                target, bass.IndirectOffsetOnAxis(ap=idx_ring[:, j:j + 1], axis=0),
                                sort_rec[:, j, :], None, bounds_check=P * EC - 1, oob_is_err=False)\
                                .then_inc(so_sent, 16)
                        pool.wait_ge(so_sent, g * (16 * HALF) + (s0 + 16 * HALF))
                    pool.sem_inc(so_pass, 1)
            with pool.Else():
                pool.nop()
            pool.wait_ge(rec_out, 16)
            pool.wait_ge(map_set, 1)
            for c in range(TC):
                k = min(P, T - c * P)
                nc.gpsimd.indirect_dma_start(
                    group_rows[c][0:k, :], None, rec.rearrange("(g e) w -> g (e w)", e=P),
                    bass.IndirectOffsetOnAxis(ap=group_i[0:k, c:c + 1], axis=0),
                    bounds_check=GROUPS - 1, oob_is_err=False).then_inc(group_in[c], 16)
            pool.wait_ge(gap_out, 16 * NB)
            with pool.Fori(0, BODIES) as g:
                for k in range(4):
                    pool.wait_ge(quad_rdy, g * 4 + (k + 1))
                    pool.sem_inc(pool_turns, 1)
                    for j in range(QUAD):
                        s = 4 * k + j
                        nc.gpsimd.indirect_dma_start(
                            msgs, bass.IndirectOffsetOnAxis(ap=idx_ring[:, s:s + 1], axis=0),
                            msg_ring[:, s, :], None, bounds_check=PLACES - 1, oob_is_err=False).then_inc(slot[s], 16)
            for s in range(BODY):
                pool.wait_ge(slot[s], 16 * BODIES)
            pool.sem_inc(msgs_done, 1)
            for n, ph, table, ring in ((1, "1", rel_table, row_ring), (2, "2a", gat_table, gat_ring),
                                       (3, "3a", kv_table, kv_ring)):
                for i in range(2):
                    pool.wait_ge(tab_out[i], 16 * tab_at[n][i])
                with pool.Fori(0, BODIES) as g:
                    for k in range(4):
                        pool.wait_ge(idx_rdy, g * 4 + (at_idx[ph] + k + 1))
                        pool.sem_inc(pool_turns, 1)
                        for j in range(QUAD):
                            s = 4 * k + j
                            nc.gpsimd.indirect_dma_start(
                                ring[:, s, :], None, table,
                                bass.IndirectOffsetOnAxis(ap=idx_ring[:, s:s + 1], axis=0),
                                bounds_check=table.shape[0] - 1, oob_is_err=False).then_inc(slot[s], 16)

        @block.scalar
        def _(act):
            loads = []

            def load(dst, src):
                act.dma_start(dst, src).then_inc(consts_in, 16)
                loads.append(dst)
            act.dma_start(X[:, 0:NB - 1, :], a["x"][0:(NB - 1) * P, :].rearrange("(b p) f -> p b f", p=P))\
                .then_inc(x_in, 16)
            act.wait_ge(pads_set, 2)
            act.dma_start(X[0:NLAST, NB - 1, :], a["x"][(NB - 1) * P:N, :]).then_inc(x_in, 16)
            load(w0[:], a["L0_gnn_weight"])
            load(w_rel[:], a["L1_gnn_weight"].rearrange("r i o -> i r o"))
            for i, n in enumerate(("Wq", "Wk", "Wv")):
                load(wqkv[:, i, :], a["L3_gnn_" + n])
            load(wo[:], a["L3_gnn_Wo"])
            for i, n in enumerate(("L0_gnn_bias", "L0_gnn_bn_gamma", "L0_gnn_bn_beta",
                                   "L3_gnn_bq", "L3_gnn_bk", "L3_gnn_bv", "L3_gnn_bo")):
                load(vecs[:, i, :], a[n].rearrange("(o n) -> o n", o=1).to_broadcast([P, F]))
            for i in range(QUAD):
                load(be_row[0:1, HEADS * i:HEADS * (i + 1)], a["L3_gnn_be"].rearrange("(o n) -> o n", o=1))
                load(we_blk[EF * i:EF * (i + 1), HEADS * i:HEADS * (i + 1)], a["L3_gnn_We"])
            for h in range(HEADS):
                for i in range(2):
                    load(att_col[HD * h:HD * (h + 1), i:i + 1],
                         a["L2_gnn_att"][h, HD * i:HD * (i + 1)].rearrange("(n o) -> n o", o=1))
            assert len(loads) == N_CONSTS

            def std(n):
                act.wait_ge(ln_var, n)
                nc.scalar.activation(col[:, 4, :], col[:, 3, :], ACT.Sqrt).then_inc(ln_sd, 1)

            def transpose_out(n, b):
                act.wait_ge(h_t, n * NB + b + 1)
                nc.scalar.activation(hT[:, b % 2, :], psT[:, b % 2, 0, :], ACT.Copy).then_inc(h_t_sb, 1)

            def onehots_out(ph, g, k):
                act.wait_ge(tr_done, g * 4 + (at_quad[ph] + k + 1))
                nc.scalar.activation(onehot_t[:, k % 2, :, :], psT[:, k % 2, :, :], ACT.Copy).then_inc(oht_rdy, 1)

            def feed(ph, idx):
                def indices(first, s):
                    nc.scalar.activation(idx_ring[:, s:s + QUAD], idx[:, bass.ds(first, QUAD)], ACT.Copy)\
                        .then_inc(idx_rdy, 1)
                for k in range(3):
                    indices(4 * k, 4 * k)

                def body(g):
                    for k in range(4):
                        if ph == "1":
                            act.wait_ge(agg, g * BODY + (at_agg[ph] + 4 * k))
                        else:
                            onehots_out(ph, g, k)
                            act.wait_ge(quad_rdy, g * 4 + (at_quad[ph] + k))
                            wait_if(act, wb[(k + 3) % 4], g * 16 + (16 * BODIES * (ph == "3a") + 16 * (k > 0)))
                        indices(g * BODY + 4 * (k + 3), 4 * ((k + 3) % 4))
                bodies(act, body)

            def exps(n):
                act.wait_ge(diff_rdy, n)
                nc.scalar.activation(SCAN, MAXS, ACT.Exp).then_inc(exp_rdy, 1)

            std(1)
            for b in range(NB):
                transpose_out(0, b)
            act.wait_ge(work_zero, 1)
            with act.Fori(0, EC // ATT // (2 * ATT_BUFS)) as g:
                for i in range(2 * ATT_BUFS):
                    q = i % 2
                    act.wait_ge(attr_t, g * (2 * ATT_BUFS) + (i + 1))
                    nc.scalar.activation(onehot_t[:, q, :, 0:EP], psT[:, q, :, 0:EP], ACT.Copy)\
                        .then_inc(attr_t_sb, 1)
                    act.wait_ge(attr_mm, g * (2 * ATT_BUFS) + (i + 1))
                    nc.scalar.activation(
                        recs[0:EP, bass.ds(g * (2 * ATT_BUFS * ATT) + i * ATT, ATT), EE_:EE_ + HEADS],
                        psG[0:EP, q, 0, :].rearrange("p (c h) -> p c h", h=HEADS), ACT.Copy).then_inc(bias_put, 1)
            for i in range(1, 4 * TC, 2):
                field_out(nc.scalar.copy, act, i)
            with act.Fori(0, BODIES) as g:
                for k in range(4):
                    onehots_out("0a", g, k)
            act.wait_ge(bn_var, 1)
            nc.scalar.activation(bn[:, 2, :], bn[:, 1, :], ACT.Sqrt).then_inc(bn_sd, 1)
            std(2)
            for b in range(NB):
                transpose_out(1, b)
                act.wait_ge(h_mm, NB + b + 1)
                if b >= 2:
                    act.wait_ge(tab_out[b % 2], 16 * (b // 2))
                nc.scalar.activation(rel_stage[:, b % 2, 0:512], pout(b)[:, 0:512], ACT.Copy)\
                    .then_inc(h_out_act, 1)
            feed("1", idx_b)
            std(3)
            for b in range(NB):
                transpose_out(2, b)
            feed("2a", idx_a)
            exps(1)
            std(4)
            for b in range(NB):
                transpose_out(3, b)
            feed("3a", idx_a)
            exps(2)
            for b in range(NB):
                transpose_out(4, b)

        @block.tensor
        def _(pe):
            def node_products(n, weights):
                pe.wait_ge(h_rdy, n + 1)
                at = 0
                for b in range(NB):
                    nc.tensor.transpose(psT[:, b % 2, 0, :], H[:, b, :], ident).then_inc(h_t, 1)
                    pe.wait_ge(h_t_sb, n * NB + b + 1)
                    if b >= 2:
                        pe.wait_ge(h_out, n * NB + b - 1)
                        if n == 1:
                            pe.wait_ge(h_out_act, b - 1)
                    at = 0
                    for w in weights:
                        width = w.shape[1] * (w.shape[2] if len(w.shape) > 2 else 1)
                        ins = nc.tensor.matmul(pout(b)[:, at:at + width], hT[:, b % 2, :], w, start=True, stop=True)
                        at += width
                    ins.then_inc(h_mm, 1)

            def fetch(ph, rows, width):
                with pe.Fori(0, BODIES) as g:
                    regs = blocks_of(ENG.PE, 0, g * BODY, BODY)
                    for k in range(4):
                        pe.wait_ge(oh_rdy, g * 4 + (at_oh[ph] + k + 1))
                        for j in range(QUAD):
                            ins = nc.tensor.transpose(psT[:, k % 2, j, :], onehot[:, k % 2, j, :], ident)
                        ins.then_inc(tr_done, 1)
                        pe.wait_ge(oht_rdy, g * 4 + (at_quad[ph] + k + 1))
                        for j in range(QUAD):
                            ins = nc.tensor.matmul(psG[:, k % 2, j, 0:width], onehot_t[:, k % 2, j, :],
                                                   rows(regs[4 * k + j]), start=True, stop=True)
                        ins.then_inc(got, 1)

            def move(m, source):
                pe.wait_ge(mv_rdy, m + 1)
                for q in range(MG):
                    if q >= 2:
                        pe.wait_ge(mv_copy, m * MG + q - 1)
                    for j in range(4 * q, min(4 * q + 4, CT)):
                        ins = nc.tensor.transpose(psT[:, q % 2, j % 4, :], source(j), ident)
                    ins.then_inc(mv_t, 1)

            def to_scan(m):
                move(m, lambda j: MAXS[:, j * P:(j + 1) * P])

            def from_scan(m):
                move(m, lambda j: SCAN[:, j * P:(j + 1) * P])

            def sum_half(ph, row, g, h, rows, width):
                first = g * BODY + h * HALF
                lo, hi = half_blocks(ENG.PE, row, first)
                with pe.If(hi - lo):
                    for j in range(HALF):
                        if j in (4, 6):
                            pe.wait_ge(added, g * BODY + (at_added[ph] + h * HALF + j - 2))
                        nc.tensor.matmul(psA[:, 4 * h + j % 4, 0:width], onehot[:, h, j, :], rows(j),
                                         start=True, stop=True).then_inc(agg, 1)
                with pe.Else():
                    for j in range(HALF):
                        ins = nc.tensor.matmul(psA[:, 4 * h, 0:width], onehot[:, h, j, :], rows(j),
                                               start=(j == 0), stop=(j == HALF - 1))
                    ins.then_inc(agg, HALF)

            def weighted_sums(n):
                with pe.Fori(0, BODIES) as g:
                    for h in range(2):
                        pe.wait_ge(wgt_rdy, g * 2 + (at_half[f"{n}b"] + h + 1))
                        pe.wait_ge(oh_rdy, g * 2 + (at_oh[f"{n}b"] + h + 1))
                        sum_half(f"{n}b", 0, g, h, lambda j: wgt_ring[:, h, j, :], F + HEADS)

            def carries(d):
                pe.wait_ge(edge_in, 2 * d + 3)
                nc.tensor.matmul(psG[0:1, 0, 0, :], MAXS[:, CE - 1:CE] if d % 2 == 0 else MAXS[:, 0:1], ident,
                                 start=True, stop=True).then_inc(edge_mm, 1)
                pe.wait_ge(edge_in, 2 * d + 4)
                sh = 0 if d % 2 == 0 else 2 * HEADS
                nc.tensor.matmul(psG[:, 1, 0, 0:1], carried[0:1, sh:sh + P], ones[0:1, 0:1],
                                 start=True, stop=True).then_inc(edge_mm, 1)

            pe.wait_ge(iota_set, 10)
            pe.wait_ge(dve_consts, 1)
            pe.wait_ge(consts_in, 16 * N_CONSTS)
            node_products(0, [w0[:]])
            pe.wait_ge(counts_set, 1)
            for m in range(2):
                for i in range(2):
                    nc.tensor.matmul(psG[0:NBX, 0, 2, 2 * m + i:2 * m + i + 1], cum[:, m, i:i + NBX],
                                     ones[:, 0:1], start=True, stop=True)
            nc.tensor.matmul(psG[:, 0, 1, 0:2], ones[:], vio[:, 2:4], start=True, stop=True).then_inc(base_mm, 1)
            pe.wait_ge(map_col, 1)
            nc.tensor.matmul(psG[0:NBX, 0, 2, 0:2], lower[0:NBX, 0:NBX], n_tiles[:], start=True, stop=True)\
                .then_inc(map_mm, 1)
            pe.wait_ge(map_col, 2)
            nc.tensor.matmul(psG[:, 0, 0, 0:NB], lower[:], tot[:, 0:NB], start=True, stop=False)
            nc.tensor.matmul(psG[:, 0, 0, 0:NB], ones[0:NBX, :], diag[:, 0, 0:NB], start=False, stop=True)
            nc.tensor.matmul(psG[:, 0, 1, 0:2 * NBX], ones[0:NBX, :],
                             diag[:, 1:3, :].rearrange("p a b -> p (a b)"), start=True, stop=True).then_inc(base_mm, 1)
            pe.wait_ge(base_set, 1)
            with pe.Fori(0, EC // ATT // (2 * ATT_BUFS)) as g:
                for i in range(2 * ATT_BUFS):
                    q, r = i % 2, i % ATT_BUFS
                    pe.wait_ge(attr_in[r], g * 32 + 16 * (1 + i // ATT_BUFS))
                    for j in range(QUAD):
                        ins = nc.tensor.transpose(
                            psT[:, q, j, 0:EP],
                            attr[0:EP, r, 4 * j:4 * j + 4, :].rearrange("p c f -> p (c f)"), ident[0:EP, 0:EP])
                    ins.then_inc(attr_t, 1)
                    pe.wait_ge(attr_t_sb, g * (2 * ATT_BUFS) + (i + 1))
                    for j in range(QUAD):
                        dest = psG[0:EP, q, 0, 32 * j:32 * j + 32]
                        nc.tensor.matmul(dest, onehot_t[:, q, j, 0:EP], we_blk[:], start=True, stop=False)
                        ins = nc.tensor.matmul(dest, ones[0:1, 0:EP], be_row[0:1, :], start=False, stop=True)
                    ins.then_inc(attr_mm, 1)
            pe.wait_ge(flag_set, 1)
            unsorted = pe.value_load(flag[0:1, 0:1], min_val=0, max_val=1)
            with pe.If(unsorted):
                for n in range(2):
                    pe.wait_ge(so_tot, n + 1)
                    nc.tensor.matmul(psG[:, 1, 0, 0:NKEY], lower[:], tot[:], start=True, stop=False)
                    nc.tensor.matmul(psG[:, 1, 0, 0:NKEY], ones[:], totc[:], start=False, stop=True)\
                        .then_inc(so_base, 1)
            with pe.Else():
                pe.nop()
            for m in range(2):
                pe.wait_ge(map_col, 3 + m)
                if m == 0:
                    for c in range(TC):
                        k = min(P, T - c * P)
                        nc.tensor.matmul(psG[0:k, 1, 3, c:c + 1], map_tmp[0:NBX, c * P:c * P + k], shift[:],
                                         start=True, stop=True)
                for c in range(2):
                    ins = nc.tensor.matmul(psA[:, 4 * m + 2 * c:4 * m + 2 * c + 2, :]
                                           .rearrange("p a b -> p (a b)")[:, 0:T // 2],
                                           ones[0:NBX, :], map_rhs[0:NBX, c * (T // 2):(c + 1) * (T // 2)],
                                           start=True, stop=True)
                ins.then_inc(map_mm, 1)
            for i in range(4 * TC):
                c, k = i // 4, min(P, T - (i // 4) * P)
                if i % 4 == 0:
                    pe.wait_ge(group_in[c], 16)
                if i >= 2:
                    pe.wait_ge(field_copy[i % 2], i // 2)
                rows = group_rows[c].rearrange("p (e w) -> p e w", w=REC)
                for j in range(1 if i % 4 == 1 else 4):
                    ins = nc.tensor.transpose(psT[:, i % 2, j, 0:k], rows[0:k, :, 4 * (i % 4) + j], ident[0:k, 0:k])
                ins.then_inc(group_t, 1)
            to_scan(0)
            pe.wait_ge(edge_in, 1)
            nc.tensor.matmul(psG[:, 0, 0, 0:1], ident_w[:, 0:P], ends[:, 1:2], start=True, stop=True)
            nc.tensor.matmul(psG[:, 0, 0, 1:2], ident_w[:, 2 * HEADS:2 * HEADS + P], ends[:, 0:1],
                             start=True, stop=True).then_inc(edge_mm, 1)
            pe.wait_ge(edge_in, 2)
            nc.tensor.matmul(psG[0:1, 0, 0, :], ends[:, 2:3], ident, start=True, stop=True)
            nc.tensor.matmul(psG[0:1, 0, 1, :], ends[:, 3:4], ident, start=True, stop=True).then_inc(edge_mm, 1)

            fetch("0a", lambda r: nodes[:, bass.ds(r, 1), :], F)
            with pe.Fori(0, BODIES) as g:
                for h in range(2):
                    pe.wait_ge(oh_rdy, g * 2 + (at_oh["0b"] + h + 1))
                    sum_half("0b", 32, g, h, lambda j: msg_ring[:, h * HALF + j, 0:F], F)
            for i, src in enumerate((H, H2)):
                pe.wait_ge(bn_in, i + 1)
                for b in range(NB):
                    k = NLAST if b == NB - 1 else P
                    ins = nc.tensor.matmul(psG[:, 0, 0, :], ones[0:k, :], src[0:k, b, :],
                                           start=(b == 0), stop=(b == NB - 1))
                ins.then_inc(bn_mm, 1)
            node_products(1, [w_rel[:, 0:4, :], w_rel[:, 4:8, :]])
            with pe.Fori(0, BODIES) as g:
                for k in range(4):
                    pe.wait_ge(oh_rdy, g * 4 + (at_oh["1"] + k + 1))
                    for j in range(QUAD):
                        s = 4 * k + j
                        pe.wait_ge(slot[s], g * 16 + (at_slot["1"] + 16))
                        nc.tensor.matmul(psA[:, s % HALF, 0:F], onehot[:, k % 2, j, :], row_ring[:, s, :],
                                         start=True, stop=True).then_inc(agg, 1)
            node_products(2, [att_blk[:]])
            fetch("2a", lambda r: s_dst[:, bass.ds(r, 1), :], HEADS)
            to_scan(1)
            carries(0)
            carries(1)
            from_scan(2)
            weighted_sums(2)
            node_products(3, [wqkv[:, :, :]])
            fetch("3a", lambda r: nodes[:, bass.ds(r, 1), :], F)
            to_scan(3)
            carries(2)
            carries(3)
            from_scan(4)
            weighted_sums(3)
            node_products(4, [wo[:]])

        @block.vector
        def _(dve):
            V = nc.vector
            sc = scores[:, :].rearrange("p (c j h) -> p c j h", c=CH, h=HEADS)

            def drain():
                dve.drain()

            def one_hots(first, k):
                V.tensor_tensor(onehot[:, k % 2, 0:QUAD, :], rep(iota[:, :], QUAD),
                                bc(dst_local[:, bass.ds(first, QUAD)], P), ALU.is_equal).then_inc(oh_rdy, 1)

            def zero_sums():
                V.memset(acc[:, :, :], 0.0).then_inc(added, HALF)

            def add(ph, reg, g, t, s, width, n=1):
                dve.wait_ge(added, g * BODY + (at_added[ph] + t))
                V.tensor_tensor(acc[:, bass.ds(reg, 1), 0:width], acc[:, bass.ds(reg, 1), 0:width],
                                psA[:, s:s + 1, 0:width], ALU.add).then_inc(added, n)

            def block_sums(ph, row, width, prepare):
                def body(g, last):
                    for h in range(2):
                        if not (last and h == 1):
                            prepare(g, h + 1)
                        first = g * BODY + h * HALF
                        lo, hi = half_blocks(ENG.DVE, row, first)
                        with dve.If(hi - lo):
                            regs = blocks_of(ENG.DVE, row, first, HALF)
                            for j in range(HALF):
                                if j % 2 == 0:
                                    dve.wait_ge(agg, g * BODY + (at_agg[ph] + h * HALF + j + 2))
                                add(ph, regs[j], g, h * HALF + j, 4 * h + j % 4, width)
                        with dve.Else():
                            dve.wait_ge(agg, g * BODY + (at_agg[ph] + (h + 1) * HALF))
                            add(ph, lo, g, h * HALF, 4 * h, width, HALF)
                prepare(0, 0)
                with dve.Fori(0, BODIES - 1) as g:
                    body(g, False)
                body(BODIES - 1, True)
                dve.wait_ge(added, at_added[ph] + T)

            def layernorm(n):
                V.tensor_reduce(col[:, 0, :], X[:, :, :], AXX, ALU.add)
                drain()
                V.tensor_scalar(col[:, 1, :], col[:, 0, :], 1.0 / F, None, ALU.mult)
                drain()
                V.tensor_tensor(H, X[:, :, :], bc(col[:, 1, :], F), ALU.subtract)
                drain()
                V.tensor_tensor(H2, H, H, ALU.mult)
                drain()
                V.tensor_reduce(col[:, 2, :], H2, AXX, ALU.add)
                drain()
                V.tensor_scalar(col[:, 3, :], col[:, 2, :], 1.0 / F, LN_EPS, ALU.mult, ALU.add).then_inc(ln_var, 1)
                dve.wait_ge(ln_sd, n)
                V.reciprocal(col[:, 5, :], col[:, 4, :])
                drain()
                V.tensor_tensor(H, H, bc(col[:, 5, :], F), ALU.mult)
                drain()
                V.tensor_scalar(H, H, 0.0, None, ALU.max).then_inc(h_rdy, 1)

            def block_out(n, b, put):
                dve.wait_ge(h_mm, n * NB + b + 1)
                put(b, pout(b)).then_inc(h_out, 1)

            def move_out(m, dest):
                for q in range(MG):
                    k = min(4, CT - 4 * q)
                    dve.wait_ge(mv_t, m * MG + q + 1)
                    d, s = dest(q, k, psT[:, q % 2, 0:k, :])
                    V.tensor_copy(d, s).then_inc(mv_copy, 1)
                drain()

            def to_scan_out(m):
                move_out(m, lambda q, k, ps: (SCAN[:, 4 * q * P:(4 * q + k) * P].rearrange("p (j e) -> p j e", e=P), ps))

            def from_scan_out(m):
                move_out(m, lambda q, k, ps: (sc_c[:, 4 * q:4 * q + k, :, :],
                                              ps.rearrange("p j (c h) -> p j c h", h=HEADS)))

            def segment_max(d0):
                for d in range(2):
                    fwd = d == 0
                    rev = slice(None) if fwd else slice(None, None, -1)
                    fl = flags[:, 0:CE] if fwd else flags[:, 1:CE + 1]
                    start = SCAN if fwd else MAXS
                    V.tensor_tensor_scan(MAXS[:, rev], fl[:, rev], start[:, rev], -BIG, ALU.add, ALU.max)\
                        .then_inc(edge_in, 1)
                    dve.wait_ge(edge_mm, 2 * (d0 + d) + 3)
                    V.tensor_copy(tails[0:1, :], psG[0:1, 0, 0, :])
                    V.memset(carried[0:1, :], -BIG)
                    drain()
                    row = carried[0:1, HEADS:HEADS + P]
                    for h in range(HEADS):
                        V.tensor_tensor_scan(row[:, h::HEADS][:, rev], link[0:1, d, h::HEADS][:, rev],
                                             tails[0:1, h::HEADS][:, rev], -BIG, ALU.add, ALU.max)
                    drain()
                    V.tensor_copy(tails[0:1, 0:1], carried[0:1, 0:1]).then_inc(edge_in, 1)
                    dve.wait_ge(edge_mm, 2 * (d0 + d) + 4)
                    V.tensor_copy(carry[:, 0:1], psG[:, 1, 0, 0:1])
                    drain()
                    V.tensor_tensor_scan(MAXS[:, rev], fl[:, rev], MAXS[:, rev], carry[:, 0:1], ALU.add, ALU.max)
                    drain()

            def weighted(n):
                ph = f"{n}b"

                def prepare(g, h):
                    b, first = h % 2, g * BODY + h * HALF
                    dve.wait_ge(seq_in[b], g * 16 + (16 * BODIES * (n - 2) + 16 * (h // 2 + 1)))
                    ex = sc_t[:, bass.ds(first, HALF), :]
                    V.tensor_tensor(
                        wgt_ring[:, b, :, 0:F].rearrange("p s (h d) -> p s h d", d=HD),
                        seq_ring[:, b, :, :].rearrange("p s (h d) -> p s h d", d=HD),
                        ex.rearrange("p s (h o) -> p s h o", o=1).to_broadcast([P, HALF, HEADS, HD]), ALU.mult)
                    V.tensor_copy(wgt_ring[:, b, :, F:F + HEADS], ex).then_inc(wgt_rdy, 1)
                    V.tensor_tensor(onehot[:, b, :, :], rep(iota[:, :], HALF),
                                    bc(dst_local[:, bass.ds(first, HALF)], P), ALU.is_equal).then_inc(oh_rdy, 1)
                block_sums(ph, 0, F + HEADS, prepare)

            def shares(eps_op):
                den = H2[:, :, 0:HEADS]
                V.tensor_scalar(den, acc[:, 0:NB, F:F + HEADS], 1e-10, None, eps_op)
                drain()
                V.reciprocal(den, den)
                drain()
                V.tensor_tensor(H.rearrange("p b (h d) -> p b h d", d=HD),
                                acc[:, 0:NB, 0:F].rearrange("p b (h d) -> p b h d", d=HD),
                                den.rearrange("p b (h o) -> p b h o", o=1).to_broadcast([P, NB, HEADS, HD]), ALU.mult)

            V.memset(dst_i, PADKEY)
            V.memset(src_i, PADKEY)
            V.memset(typ_i, 0)
            V.memset(nxt[:], PADKEY)
            V.memset(w_in, 0.0).then_inc(pads_set, 1)
            V.memset(X[:, NB - 1, :], 0.0)
            V.memset(we_blk[:], 0.0).then_inc(pads_set, 1)
            V.memset(ones[:], 1.0)
            V.memset(nodes[:, NB, :], 0.0)
            V.memset(s_dst[:, NB, :], 0.0)
            V.memset(zeros, 0.0)
            V.memset(place, 0.0)
            V.memset(vio[:], 0.0)
            V.memset(dst_local[:, T:T + BODY], -1.0)
            V.memset(idx_a[:, T:T + BODY], 0)
            V.memset(idx_b[:, T:T + BODY], 0)
            dve.wait_ge(iota_set, 10)
            V.tensor_copy(iota[:], iota_i[:])
            V.tensor_copy(map_rhs, tile_no_i)
            drain()
            V.tensor_copy(tile_no, map_rhs)
            V.tensor_scalar(thr[:], iota[:, 0:NKEY], float(P), None, ALU.mult)
            V.tensor_copy(node_no[:], node_no_i[:]).then_inc(dve_consts, 1)
            dve.wait_ge(x_in, 32)
            layernorm(1)
            drain()
            V.tensor_tensor(X[:, :, :], X[:, :, :], H, ALU.add).then_inc(work_free, 1)
            dve.wait_ge(edges_in, 5 * 16)
            V.tensor_tensor(hit[:, 0:EC - 1], dst_i[:, 0:EC - 1], dst_i[:, 1:EC], ALU.is_gt)
            V.tensor_tensor(vio[:, 1:2], dst_i[:, EC - 1:EC], nxt[:, 0:1], ALU.is_gt)
            drain()
            V.tensor_reduce(vio[:, 0:1], hit[:, 0:EC - 1], AXX, ALU.add)
            drain()
            V.tensor_tensor(vio[:, 2:3], vio[:, 0:1], vio[:, 1:2], ALU.add)
            V.tensor_copy(key, dst_i)
            V.tensor_copy(cnt, src_i)
            drain()
            with dve.Fori(0, NBX + 1) as b:
                V.tensor_scalar(hit, key, thr[:, bass.ds(b, 1)], 0.0, ALU.is_lt, ALU.add,
                                accum_out=cum[:, 0, bass.ds(b, 1)])
                V.tensor_scalar(key_i.bitcast(F32), cnt, thr[:, bass.ds(b, 1)], 0.0, ALU.is_lt, ALU.add,
                                accum_out=cum[:, 1, bass.ds(b, 1)])
                drain()
            V.tensor_tensor(tot[:, 0:NB], cum[:, 1, 1:NB + 1], cum[:, 1, 0:NB], ALU.subtract)
            V.tensor_scalar(key_i, src_i, 7, None, ALU.arith_shift_right)
            drain()
            V.tensor_copy(key, key_i).then_inc(counts_set, 1)
            for b in range(NB):
                block_out(0, b, lambda b, ps: V.tensor_copy(nodes[:, b, :], ps[:, 0:F]))
            dve.wait_ge(base_mm, 1)
            V.tensor_scalar(flag[:, 0:1], psG[:, 0, 1, 0:1], 0.5, None, ALU.is_gt)
            V.tensor_copy(below[:], psG[0:NBX, 0, 2, 0:4])
            drain()
            V.tensor_scalar(rounded[:, 0:1], below[:, 1:2], float(P - 1), None, ALU.add)
            V.tensor_copy(rounded[:, 1:2], below[:, 0:1])
            V.tensor_tensor(bounds[:, 1:2], below[:, 3:4], below[:, 2:3], ALU.subtract)
            V.tensor_tensor(bounds[:, 2:3], below[:, 1:2], below[:, 0:1], ALU.is_gt)
            drain()
            V.tensor_scalar(rounded[:, 2:3], bounds[:, 1:2], float(P - 1), None, ALU.add)
            drain()
            V.tensor_scalar(rounded[:], rounded[:], 7, None, ALU.arith_shift_right)
            drain()
            V.tensor_copy(rounded_f[:], rounded[:])
            drain()
            V.tensor_tensor(n_tiles[:, 0:1], rounded_f[:, 0:1], rounded_f[:, 1:2], ALU.subtract)
            drain()
            V.tensor_tensor(n_tiles[:, 0:1], n_tiles[:, 0:1], bounds[:, 2:3], ALU.mult)
            V.tensor_copy(n_tiles[:, 1:2], rounded_f[:, 2:3]).then_inc(map_col, 1)
            dve.wait_ge(map_mm, 1)
            V.tensor_copy(first_tile[:], psG[0:NBX, 0, 2, 0:2])
            drain()
            V.tensor_tensor(end_tile[:], first_tile[:], n_tiles[:], ALU.add)
            V.tensor_tensor(shift[:], rounded_f[:, 1:2], first_tile[:, 0:1], ALU.subtract)
            V.tensor_scalar(bounds[:, 0:1], first_tile[:, 1:2], float(P), None, ALU.mult)
            drain()
            V.tensor_tensor(bounds[:, 1:2], bounds[:, 1:2], bounds[:, 0:1], ALU.add)
            V.tensor_scalar(bounds[:, 2:3], end_tile[:, 1:2], float(P), None, ALU.mult)
            drain()
            for i in range(3):
                V.tensor_scalar(diag[:, i, :], ident[0:NBX, 0:NBX], bounds[:, i:i + 1], None, ALU.mult)
            V.scalar_tensor_tensor(end_tile[:], ident[0:NBX, NB:NB + 1].to_broadcast([NBX, 2]), 1e6, end_tile[:],
                                   ALU.mult, ALU.add).then_inc(map_col, 1)
            dve.wait_ge(base_mm, 2)
            V.tensor_scalar(base[:, 0:NB], psG[:, 0, 0, 0:NB], -1.0, None, ALU.add)
            V.tensor_scalar(gap[:, 0, :], psG[:, 0, 1, 0:NB], node_no[:], None, ALU.add)
            V.tensor_copy(gap[:, 1, :], psG[:, 0, 1, NBX:NBX + NB]).then_inc(base_set, 1)
            drain()
            V.tensor_copy(gap_i[:, 0, :], gap[:, 0, :])
            V.tensor_tensor(gap[:, 1, :], gap[:, 0, :], gap[:, 1, :], ALU.is_lt)
            drain()
            V.tensor_scalar(gap_i[:, 1, :], gap_i[:, 0, :], P - 1, None, ALU.bitwise_and)
            V.tensor_scalar(gap_i[:, 2, :], gap_i[:, 0, :], 7, None, ALU.arith_shift_right)
            drain()
            V.tensor_copy(gap[:, 2:4, :], gap_i[:, 1:3, :])
            drain()
            V.scalar_tensor_tensor(gap[:, 0, :], gap[:, 2, :], float(T), gap[:, 3, :], ALU.mult, ALU.add)
            drain()
            V.scalar_tensor_tensor(gap[:, 0, :], gap[:, 0, :], -float(PLACES), gap[:, 1, :], ALU.add, ALU.mult)
            drain()
            V.tensor_scalar(gap_i[:, 0, :], gap[:, 0, :], float(PLACES), None, ALU.add).then_inc(gap_set, 1)

            def places(n):
                with dve.Fori(0, n) as b:
                    V.tensor_scalar(hit, key, iota[:, bass.ds(b, 1)], None, ALU.is_equal)
                    drain()
                    V.tensor_tensor_scan(cnt, hit, zeros, base[:, bass.ds(b, 1)], ALU.add, ALU.add)
                    drain()
                    V.tensor_tensor(cnt, cnt, hit, ALU.mult)
                    drain()
                    V.tensor_tensor(place, place, cnt, ALU.add)
                    drain()

            places(NB)
            dve.wait_ge(work_zero, 1)
            V.tensor_copy(recs[:, :, D_], dst_i)
            V.tensor_copy(recs[:, :, S_], src_i)
            V.tensor_copy(recs[:, :, T_], typ_i)
            V.tensor_copy(recs[:, :, W_], w_in)
            dve.wait_ge(bias_put, EC // ATT)
            V.tensor_copy(recs[:, :, POS_], place).then_inc(recs_set, 1)
            V.tensor_copy(vio[:, 0:1], zeros[:, 0:1]).then_inc(flag_set, 1)
            unsorted = dve.value_load(flag[0:1, 0:1], min_val=0, max_val=1)
            with dve.If(unsorted):
                dve.wait_ge(rec_out, 16)
                for n in range(2):
                    if n:
                        dve.wait_ge(so_in, 16)
                    V.tensor_copy(dst_i, recs[:, :, D_])
                    V.memset(place, 0.0)
                    drain()
                    if n:
                        V.tensor_scalar(key_i, dst_i, 6, None, ALU.arith_shift_right)
                    else:
                        V.tensor_scalar(key_i, dst_i, NKEY - 1, None, ALU.bitwise_and)
                    drain()
                    V.tensor_copy(key, key_i)
                    drain()
                    with dve.Fori(0, NKEY) as b:
                        V.tensor_scalar(hit, key, iota[:, bass.ds(b, 1)], 0.0, ALU.is_equal, ALU.add,
                                        accum_out=tot[:, bass.ds(b, 1)])
                        drain()
                    V.tensor_tensor_scan(totc[:], tot[:], zeros[:, 0:NKEY], 0.0, ALU.add, ALU.add)
                    drain()
                    V.tensor_tensor(totc[:], totc[:], tot[:], ALU.subtract).then_inc(so_tot, 1)
                    dve.wait_ge(so_base, n + 1)
                    V.tensor_scalar(base[:], psG[:, 1, 0, 0:NKEY], -1.0, None, ALU.add)
                    drain()
                    places(NKEY)
                    V.tensor_copy(place_i, place).then_inc(so_place, 1)
                dve.wait_ge(so_pass, 2)
            with dve.Else():
                dve.nop()

            dve.wait_ge(consts_in, 16 * N_CONSTS)
            V.tensor_scalar(att_blk[:, 0:HEADS], head_mask[:], att_col[:, 0:1], None, ALU.mult)
            V.tensor_scalar(att_blk[:, HEADS:2 * HEADS], head_mask[:], att_col[:, 1:2], None, ALU.mult)
            drain()
            for m in range(2):
                V.tensor_scalar(map_tmp[0:NBX, :], tile_no[0:NBX, :], first_tile[:, m:m + 1], None, ALU.is_ge)
                V.tensor_scalar(map_tmp2[0:NBX, :], tile_no[0:NBX, :], end_tile[:, m:m + 1], None, ALU.is_lt)
                drain()
                V.tensor_tensor(map_tmp[0:NBX, :], map_tmp[0:NBX, :], map_tmp2[0:NBX, :], ALU.mult)
                drain()
                V.tensor_scalar(map_rhs[0:NBX, :], map_tmp[0:NBX, :], node_no[0:NBX, :], None, ALU.mult)\
                    .then_inc(map_col, 1)
                dve.wait_ge(map_mm, 2 + m)
                if m == 0:
                    for c in range(TC):
                        k = min(P, T - c * P)
                        V.scalar_tensor_tensor(group_f[0:k, c:c + 1], node_no[0:k, :], float(c * P),
                                               psG[0:k, 1, 3, c:c + 1], ALU.add, ALU.add)
                    drain()
                    for c in range(TC):
                        k = min(P, T - c * P)
                        V.tensor_scalar(group_i[0:k, c:c + 1], group_f[0:k, c:c + 1], float(GROUPS - 1), None, ALU.min)
                    V.tensor_copy(vio[:, 1:2], zeros[:, 0:1]).then_inc(map_set, 1)
                for c in range(2):
                    ps = psA[:, 4 * m + 2 * c:4 * m + 2 * c + 2, :].rearrange("p a b -> p (a b)")[:, 0:T // 2]
                    cs = slice(c * (T // 2), (c + 1) * (T // 2))
                    V.tensor_copy(maps[32 * m:32 * m + 32, cs], ps[32 * m:32 * m + 32, :])
                    V.tensor_scalar((src_lo if m else block_lo)[:, cs], ps, float(P), None, ALU.mult)
                drain()

            for i in range(0, 4 * TC, 2):
                field_out(V.tensor_copy, dve, i)
            dve.wait_ge(field_copy[1], 2 * TC)
            drain()
            V.tensor_tensor(dst_local[:, 0:T], fields[:, 0, :], block_lo[:], ALU.subtract)
            V.tensor_copy(place_t, fields[:, 4, :])
            V.tensor_scalar(map_rhs, src_f, float(NB * P - 1), None, ALU.min)
            V.tensor_scalar(dst_id, fields[:, 0, :], 1.0, None, ALU.add)
            drain()
            V.tensor_copy(block_lo[:], src_lo)
            V.tensor_scalar(place_t2, place_t, P - 1, None, ALU.bitwise_and)
            V.tensor_scalar(map_tmp, dst_local[:, 0:T], float(P), None, ALU.is_lt)
            V.tensor_scalar(map_tmp2, dst_local[:, 0:T], 0.0, None, ALU.is_ge)
            V.scalar_tensor_tensor(idx_b[:, 0:T], map_rhs, float(NREL), fields[:, 2, :], ALU.mult, ALU.add)
            drain()
            V.tensor_scalar(place_t, place_t, 7, None, ALU.arith_shift_right)
            V.tensor_tensor(map_tmp, map_tmp, map_tmp2, ALU.mult)
            V.tensor_copy(fields[:, 0, :], place_t2)
            drain()
            V.tensor_copy(fields[:, 4, :], place_t)
            V.tensor_tensor(dst_id, dst_id, map_tmp, ALU.mult)
            drain()
            V.scalar_tensor_tensor(fields[:, 0, :], fields[:, 0, :], float(T), fields[:, 4, :], ALU.mult, ALU.add)
            V.tensor_scalar(dst_id, dst_id, -1.0, None, ALU.add)
            drain()
            V.scalar_tensor_tensor(fields[:, 0, :], fields[:, 0, :], -float(PLACES), map_tmp, ALU.add, ALU.mult)
            drain()
            V.tensor_scalar(idx_a[:, 0:T], fields[:, 0, :], float(PLACES), None, ALU.add).then_inc(tiles_set, 1)
            V.tensor_copy(by_chunk, dst_id.rearrange("p (c j o) -> p c j o", c=CH, o=1)
                          .to_broadcast([P, CH, CT, HEADS])).then_inc(mv_rdy, 1)
            to_scan_out(0)
            V.tensor_copy(ends[:, 0:1], SCAN[:, 0:1])
            V.tensor_copy(ends[:, 1:2], SCAN[:, CE - 1:CE]).then_inc(edge_in, 1)
            V.tensor_tensor(flags[:, 1:CE], SCAN[:, 1:CE], SCAN[:, 0:CE - 1], ALU.not_equal)
            dve.wait_ge(edge_mm, 1)
            V.tensor_tensor(flags[:, 0:1], ends[:, 0:1], psG[:, 0, 0, 0:1], ALU.not_equal)
            V.tensor_tensor(flags[:, CE:CE + 1], ends[:, 1:2], psG[:, 0, 0, 1:2], ALU.not_equal)
            drain()
            V.tensor_scalar(flags[:, 0:CE + 1], flags[:, 0:CE + 1], -BIG, None, ALU.mult)
            drain()
            V.tensor_reduce(ends[:, 2:3], flags[:, 0:CE], AXX, ALU.min)
            V.tensor_reduce(ends[:, 3:4], flags[:, 1:CE + 1], AXX, ALU.min).then_inc(edge_in, 1)
            dve.wait_ge(edge_mm, 2)
            V.tensor_copy(link[0:1, :, :], psG[0:1, 0, 0:2, :])
            zero_sums()

            drain()
            one_hots(0, 0)

            def messages(g):
                for k in range(4):
                    wait_if(dve, tr_done, g * 4 + (at_quad["0a"] + k))
                    one_hots(g * BODY + 4 * (k + 1), k + 1)
                    dve.wait_ge(got, g * 4 + (at_quad["0a"] + k + 1))
                    for j in range(QUAD):
                        wait_if(dve, slot[4 * k + j], g * 16)
                    V.tensor_tensor(msg_ring[:, 4 * k:4 * k + 4, 0:F], psG[:, k % 2, :, :],
                                    bc(weight[:, bass.ds(g * BODY + 4 * k, QUAD)], F), ALU.mult)
                    V.tensor_copy(msg_ring[:, 4 * k:4 * k + 4, F], src_f[:, bass.ds(g * BODY + 4 * k, QUAD)])
                    V.tensor_copy(idx_ring[:, 4 * k:4 * k + 4], idx_a[:, bass.ds(g * BODY + 4 * k, QUAD)])\
                        .then_inc(quad_rdy, 1)
            bodies(dve, messages)
            dve.wait_ge(msgs_done, 1)
            V.tensor_scalar(idx_a[:, 0:T], src_f, float(NB * P - 1), None, ALU.min)

            def prepare(g, h):
                b, first = h % 2, g * BODY + h * HALF
                dve.wait_ge(msg_in[b], g * 16 + 16 * (h // 2 + 1))
                V.tensor_tensor(src_local[:, b * HALF:(b + 1) * HALF], msg_ring[:, b * HALF:(b + 1) * HALF, F],
                                block_lo[:, bass.ds(first, HALF)], ALU.subtract).then_inc(src_sub, 1)
                dve.wait_ge(src_sub, g * 2 + (h + 1))
                V.tensor_tensor(onehot[:, b, :, :], rep(iota[:, :], HALF),
                                bc(src_local[:, b * HALF:(b + 1) * HALF], P), ALU.is_equal).then_inc(oh_rdy, 1)
            dve.wait_ge(oh_rdy, at_oh["0b"])
            block_sums("0b", 32, F, prepare)
            V.tensor_tensor(H, acc[:, 0:NB, 0:F], rep(vecs[:, 0, :], NB), ALU.add).then_inc(bn_in, 1)
            dve.wait_ge(bn_mm, 1)
            V.tensor_scalar(bn[:, 0, :], psG[:, 0, 0, :], 1.0 / N, None, ALU.mult)
            drain()
            V.tensor_tensor(H, H, rep(bn[:, 0, :], NB), ALU.subtract)
            drain()
            V.tensor_tensor(H2, H, H, ALU.mult).then_inc(bn_in, 1)
            dve.wait_ge(bn_mm, 2)
            V.tensor_scalar(bn[:, 1, :], psG[:, 0, 0, :], 1.0 / N, LN_EPS, ALU.mult, ALU.add).then_inc(bn_var, 1)
            dve.wait_ge(bn_sd, 1)
            V.reciprocal(bn[:, 3, :], bn[:, 2, :])
            drain()
            V.tensor_tensor(bn[:, 3, :], bn[:, 3, :], vecs[:, 1, :], ALU.mult)
            drain()
            V.tensor_tensor(H, H, rep(bn[:, 3, :], NB), ALU.mult)
            drain()
            V.tensor_tensor(H, H, rep(vecs[:, 2, :], NB), ALU.add)
            drain()
            V.scalar_tensor_tensor(X[:, :, :], H, 0.0, X[:, :, :], ALU.max, ALU.add)
            zero_sums()
            drain()

            layernorm(2)

            def rel_out(b, ps):
                if b >= 2:
                    dve.wait_ge(tab_out[b % 2], 16 * (b // 2))
                return V.tensor_copy(rel_stage[:, b % 2, 512:1024], ps[:, 512:1024])
            for b in range(NB):
                block_out(1, b, rel_out)
            one_hots(0, 0)
            with dve.Fori(0, BODIES) as g:
                for k in range(4):
                    dve.wait_ge(agg, g * BODY + (at_agg["1"] + 4 * k))
                    one_hots(g * BODY + 4 * (k + 1), k + 1)
                    regs = blocks_of(ENG.DVE, 0, g * BODY + 4 * k, QUAD)
                    for j in range(QUAD):
                        if j % 2 == 0:
                            dve.wait_ge(agg, g * BODY + (at_agg["1"] + 4 * k + j + 2))
                        add("1", regs[j], g, 4 * k + j, (4 * k + j) % HALF, F)
            dve.wait_ge(added, at_added["1"] + T)
            V.tensor_tensor(X[:, :, :], X[:, :, :], acc[:, 0:NB, 0:F], ALU.add)
            drain()
            zero_sums()

            layernorm(3)

            def gat_out(b, ps):
                V.tensor_copy(H2[:, b, 0:HEADS], ps[:, 0:HEADS])
                return V.tensor_copy(s_dst[:, b, :], ps[:, HEADS:2 * HEADS])
            for b in range(NB):
                block_out(2, b, gat_out)
            one_hots(0, 0)
            with dve.Fori(0, BODIES) as g:
                for k in range(4):
                    dve.wait_ge(tr_done, g * 4 + (at_quad["2a"] + k))
                    one_hots(g * BODY + 4 * (k + 1), k + 1)
                    dve.wait_ge(got, g * 4 + (at_quad["2a"] + k + 1))
                    for j in range(QUAD):
                        dve.wait_ge(slot[4 * k + j], g * 16 + (at_slot["2a"] + 16))
                    V.tensor_tensor(sc_t[:, bass.ds(g * BODY + 4 * k, QUAD), :], psG[:, k % 2, :, 0:HEADS],
                                    gat_ring[:, 4 * k:4 * k + 4, F:F + HEADS], ALU.add).then_inc(quad_rdy, 1)
            dve.wait_ge(quad_rdy, at_quad["3a"])
            V.scalar_tensor_tensor(scores[:, :], scores[:, :], 0.2, scores[:, :], ALU.mult, ALU.max)
            drain()
            V.tensor_copy(by_chunk, sc).then_inc(mv_rdy, 1)
            for k in range(4):
                dve.wait_ge(wb[k], 16 * BODIES)
            to_scan_out(1)
            segment_max(0)
            V.tensor_scalar(MAXS, MAXS, 0.0, None, ALU.max)
            drain()
            V.tensor_tensor(MAXS, SCAN, MAXS, ALU.subtract).then_inc(diff_rdy, 1)
            dve.wait_ge(exp_rdy, 1)
            V.tensor_copy(carry[:, 0:1], ones[:, 0:1]).then_inc(mv_rdy, 1)
            from_scan_out(2)
            V.tensor_copy(carry[:, 0:1], ones[:, 0:1]).then_inc(ring_free, 1)
            weighted(2)
            shares(ALU.max)
            drain()
            V.tensor_tensor(X[:, :, :], X[:, :, :], H, ALU.add)
            zero_sums()
            drain()

            layernorm(4)

            def kv_out(b, ps):
                if b >= 2:
                    dve.wait_ge(tab_out[b % 2], 16 * (b // 2 + tab_at[2][b % 2]))
                V.tensor_tensor(nodes[:, b, :], ps[:, 0:F], vecs[:, 3, :], ALU.add)
                return V.tensor_tensor(kv_stage[:, b % 2, :], ps[:, F:3 * F],
                                       vecs[:, 4:6, :].rearrange("p a f -> p (a f)"), ALU.add)
            for b in range(NB):
                block_out(3, b, kv_out)
            one_hots(0, 0)
            with dve.Fori(0, BODIES) as g:
                for k in range(4):
                    dve.wait_ge(tr_done, g * 4 + (at_quad["3a"] + k))
                    one_hots(g * BODY + 4 * (k + 1), k + 1)
                    dve.wait_ge(got, g * 4 + (at_quad["3a"] + k + 1))
                    for j in range(QUAD):
                        dve.wait_ge(slot[4 * k + j], g * 16 + (at_slot["3a"] + 16))
                    dve.wait_ge(quad_rdy, g * 4 + (at_quad["3a"] + k))
                    V.tensor_tensor(prod.rearrange("p (s w) -> p s w", w=F), psG[:, k % 2, :, :],
                                    kv_ring[:, 4 * k:4 * k + 4, 0:F], ALU.mult).then_inc(prod_rdy, 1)
                    dve.wait_ge(prod_rdy, g * 4 + (k + 1))
                    V.tensor_reduce(scores[:, bass.ds(g * (BODY * HEADS) + 4 * k * HEADS, QUAD * HEADS)],
                                    prod.rearrange("p (s d) -> p s d", d=HD), AXX, ALU.add).then_inc(quad_rdy, 1)
            dve.wait_ge(quad_rdy, at_quad["3a"] + NQ)
            V.tensor_copy(carry[:, 0:1], ones[:, 0:1]).then_inc(raw_done, 1)
            dve.wait_ge(bias_in, 16)
            V.scalar_tensor_tensor(scores[:, :], scores[:, :], float(HD) ** -0.5, work[:, 0:T * HEADS],
                                   ALU.mult, ALU.add)
            drain()
            V.tensor_copy(by_chunk, sc).then_inc(mv_rdy, 1)
            to_scan_out(3)
            segment_max(2)
            V.tensor_tensor(MAXS, SCAN, MAXS, ALU.subtract).then_inc(diff_rdy, 1)
            dve.wait_ge(exp_rdy, 2)
            V.tensor_copy(carry[:, 0:1], ones[:, 0:1]).then_inc(mv_rdy, 1)
            from_scan_out(4)
            V.tensor_copy(carry[:, 0:1], ones[:, 0:1]).then_inc(ring_free, 1)
            weighted(3)
            shares(ALU.add)
            drain()
            V.tensor_tensor(X[:, :, :], X[:, :, :], rep(vecs[:, 6, :], NB), ALU.add).then_inc(h_rdy, 1)
            for b in range(NB):
                block_out(4, b, lambda b, ps: V.tensor_tensor(X[:, b, :], X[:, b, :], ps[:, 0:F], ALU.add))


_INS = ["x", "src", "dst", "edge_attr_32", "edge_type_8", "edge_weight", "L0_gnn_weight", "L0_gnn_bias",
        "L0_gnn_bn_gamma", "L0_gnn_bn_beta", "L1_gnn_weight", "L2_gnn_att", "L3_gnn_Wq", "L3_gnn_bq",
        "L3_gnn_Wk", "L3_gnn_bk", "L3_gnn_Wv", "L3_gnn_bv", "L3_gnn_We", "L3_gnn_be", "L3_gnn_Wo", "L3_gnn_bo"]


def kernel(**inputs):
    import numpy as np
    import concourse.bacc as bacc
    from concourse.bass_utils import run_bass_kernel_spmd

    nc = bacc.Bacc("TRN2", target_bir_lowering=False, num_devices=1)
    arrays, args = {}, {}
    for name in _INS:
        arr = np.ascontiguousarray(inputs[name])
        arrays[f"in_{name}"] = arr
        args[name] = nc.dram_tensor(f"in_{name}", arr.shape, mybir.dt.from_np(arr.dtype), kind="ExternalInput").ap()
    out = nc.dram_tensor("out_x", (N, F), F32, kind="ExternalOutput").ap()
    gnn(nc, args, out)
    r = run_bass_kernel_spmd(nc, [arrays], core_ids=[0])
    return r.results[0]["out_x"]
```

```python
import concourse.bass as bass
from concourse import mybir
from contextlib import ExitStack

F32 = mybir.dt.float32
BF16 = mybir.dt.bfloat16
I32 = mybir.dt.int32
ALU = mybir.AluOpType
ACT = mybir.ActivationFunctionType
AXX = mybir.AxisListType.X
ENG = mybir.EngineType

P = 128
N = 3125
F = 128
E = 100000
EF = 32
NREL = 8
HEADS = 8
HD = F // HEADS
NB = -(-N // P)
NBX = NB + 1
NLAST = N - (NB - 1) * P
EP = 125
EC = E // EP
REC = 16
D_, S_, T_, W_, POS_, EE_ = 0, 1, 2, 3, 4, 8
NKEY = 64
PADKEY = NKEY * NKEY - 1
BODY = 16
QUAD = 4
HALF = 8
T = -(-(E // P + 1 + NB) // BODY) * BODY
BODIES = T // BODY
CH = P // HEADS
CT = T // CH
CE = CT * P
BIG = 1e30
LN_EPS = 1e-5
ATT = 16
ATT_BUFS = 5
ATT_STEPS = 2 * ATT_BUFS
ATT_ROUNDS = EC // ATT // ATT_STEPS
GROUPS = P * EC // P
MG_T = E // P
TC = -(-T // P)
MSG = F + 1
PLACES = P * T
NQ = T // QUAD
NH = T // HALF
RING = 6
SPAN = RING * HALF
ENDS = 6
AHEAD = 3
ROUNDS = T // SPAN
MG = -(-CT // QUAD)
N_CONSTS = 6 + 7 + 2 * QUAD + 2 * HEADS
assert EP * EC == E and T % CH == 0 and EC % (2 * ATT * ATT_BUFS) == 0 and NB % 2 == 1 and T * REC * 4 <= 56 * 1024
assert CE * CH == T * P and 2 * CE <= T * REC and ROUNDS * SPAN == T and RING % 2 == RING % AHEAD == 0


def gnn(nc, a, out):
    ctx = ExitStack()
    with ctx:
        def sb(name, shape, dt=F32):
            return ctx.enter_context(nc.sbuf_tensor(name, shape, dt))

        def sem(name):
            return ctx.enter_context(nc.semaphore(name))

        def dram(name, shape, dt=F32):
            return nc.dram_tensor(name, shape, dt, kind="Internal").ap()

        rec = dram("rec", [P * EC, REC])
        rec2 = dram("rec2", [P * EC, REC])
        msgs = dram("msgs", [PLACES, MSG])
        rel_table = dram("rel_table", [NB * P * NREL, F])
        gat_table = dram("gat_table", [NB * P, F + HEADS])
        kv_table = dram("kv_table", [NB * P, 2 * F])
        rows_seq = dram("rows_seq", [P, T * F])
        bias_seq = dram("bias_seq", [P, T * HEADS])

        work = sb("work", [P, T * REC])
        scores = sb("scores", [P, T * HEADS])
        flags = sb("flags", [P, CE + 2], BF16)
        X = sb("X", [P, NB, F])
        nodes = sb("nodes", [P, NBX, F])
        acc = sb("acc", [P, NBX, F + HEADS])
        onehot = sb("onehot", [P, AHEAD, HALF, P])
        dst_local = sb("dst_local", [P, T + BODY])
        fields = sb("fields", [P, 5, T])
        block_lo = sb("block_lo", [P, T])
        maps = sb("maps", [P, T], I32)
        end_maps = sb("end_maps", [P, 2 * NH], I32)
        idx_a = sb("idx_a", [P, T + BODY], I32)
        idx_b = sb("idx_b", [P, T + BODY], I32)
        idx_ring = sb("idx_ring", [P, BODY], I32)
        ident_w = sb("ident_w", [P, P + 2 * HEADS])
        node_no_i = sb("node_no_i", [P, 1], I32)
        node_no = sb("node_no", [P, 1])
        ones = sb("ones", [P, P])
        lower = sb("lower", [P, P])
        iota = sb("iota", [P, P])
        iota_i = sb("iota_i", [P, P], I32)
        thr = sb("thr", [P, NKEY])
        head_mask = sb("head_mask", [P, HEADS])
        att_col = sb("att_col", [P, 2])
        att_blk = sb("att_blk", [P, 2 * HEADS])
        s_dst = sb("s_dst", [P, NBX, HEADS])
        we_blk = sb("we_blk", [P, QUAD * HEADS])
        be_row = sb("be_row", [1, QUAD * HEADS])
        be_step = sb("be_step", [1, ATT * HEADS])
        attr = sb("attr", [P, ATT_BUFS, ATT, EF])
        w0 = sb("w0", [P, F])
        w_rel = sb("w_rel", [P, NREL, F])
        wqkv = sb("wqkv", [P, 3, F])
        wo = sb("wo", [P, F])
        vecs = sb("vecs", [P, 7, F])
        hT = sb("hT", [P, 2, F])
        col = sb("col", [P, 8, NB])
        cum = sb("cum", [P, 2, 28])
        tot = sb("tot", [P, NKEY])
        totc = sb("totc", [P, NKEY])
        base = sb("base", [P, NKEY])
        below = sb("below", [NBX, 4])
        rounded = sb("rounded", [NBX, 3], I32)
        rounded_f = sb("rounded_f", [NBX, 3])
        n_tiles = sb("n_tiles", [NBX, 2])
        first_tile = sb("first_tile", [NBX, 2])
        end_tile = sb("end_tile", [NBX, 2])
        shift = sb("shift", [NBX, 1])
        bounds = sb("bounds", [NBX, 3])
        diag = sb("diag", [NBX, 3, NBX])
        group_f = sb("group_f", [P, TC])
        group_i = sb("group_i", [P, TC], I32)
        gap = sb("gap", [P, 4, NB])
        gap_i = sb("gap_i", [P, 3, NB], I32)
        nxt = sb("nxt", [P, 2], I32)
        flag = sb("flag", [P, 1], I32)
        vio = sb("vio", [P, 4])
        bn = sb("bn", [P, 4, F])
        chunk_ends = sb("chunk_ends", [P, 4])
        link = sb("link", [1, 2, P])
        tails = sb("tails", [1, P])
        carried = sb("carried", [1, P + 2 * HEADS])
        carry = sb("carry", [P, 1])
        psA = ctx.enter_context(nc.psum_tensor("psA", [P, HALF, 256], F32))
        psT = ctx.enter_context(nc.psum_tensor("psT", [P, 2, QUAD, P], F32))
        psG = ctx.enter_context(nc.psum_tensor("psG", [P, 2, QUAD, P], F32))

        onehot_t = onehot[:, 2, :, :].rearrange("p (a b) c -> p a b c", b=QUAD)
        recs = work[:, 0:EC * REC].rearrange("p (c w) -> p c w", w=REC)
        H = work[:, 0:NB * F].rearrange("p (b f) -> p b f", f=F)
        H2 = work[:, NB * F:2 * NB * F].rearrange("p (b f) -> p b f", f=F)
        SCAN = work[:, 0:CE]
        MAXS = work[:, CE:2 * CE]
        sc_t = scores[:, :].rearrange("p (t h) -> p t h", h=HEADS)
        by_chunk = MAXS.rearrange("p (j c h) -> p c j h", c=CH, h=HEADS)
        sc_c = scores[:, :].rearrange("p (c j h) -> p j c h", c=CH, h=HEADS)
        msg_ring = work[:, 0:BODY * MSG].rearrange("p (s w) -> p s w", w=MSG)
        msg_seq = work[:, 0:SPAN * MSG].rearrange("p (i s f) -> p i s f", i=RING, f=MSG)
        group_rows = [work[:, c * P * REC:(c + 1) * P * REC] for c in range(TC - 1)] + [
            attr[:, :, :, :].rearrange("p a b c -> p (a b c)")[:, 0:P * REC]]
        src_lo = flags[:, 0:2 * T].bitcast(F32)
        src_f = fields[:, 1, :]
        weight = fields[:, 3, :]
        src_local = work[:, SPAN * MSG:SPAN * MSG + AHEAD * HALF]
        gat_ring = work[:, 0:BODY * (F + HEADS)].rearrange("p (s w) -> p s w", w=F + HEADS)
        kv_ring = work[:, 0:BODY * 2 * F].rearrange("p (s w) -> p s w", w=2 * F)
        row_ring = work[:, 0:BODY * F].rearrange("p (s w) -> p s w", w=F)
        prod = work[:, BODY * 2 * F:BODY * 2 * F + QUAD * F]
        RAW0 = BODY * 2 * F + QUAD * F
        seq_ring = work[:, 0:SPAN * F].rearrange("p (i s f) -> p i s f", i=RING, f=F)
        wgt0 = SPAN * F
        wgt_ring = work[:, wgt0:wgt0 + SPAN * (F + HEADS)].rearrange(
            "p (i s f) -> p i s f", i=RING, f=F + HEADS)
        stage0 = 2 * NB * F
        rel_stage = work[:, stage0:stage0 + 2 * NREL * F].rearrange("p (r w) -> p r w", r=2)
        kv_stage = rel_stage[:, :, 0:2 * F]

        dst_i = scores[:, 0:EC].bitcast(I32)
        src_i = scores[:, EC:2 * EC].bitcast(I32)
        typ_i = scores[:, 2 * EC:3 * EC].bitcast(I32)
        w_in = scores[:, 3 * EC:4 * EC]
        key = scores[:, 4 * EC:5 * EC]
        hit = scores[:, 5 * EC:6 * EC]
        cnt = scores[:, 6 * EC:7 * EC]
        key_i = scores[:, 7 * EC:8 * EC].bitcast(I32)
        zeros = onehot[:, :, :, :].rearrange("p a b c -> p (a b c)")[:, 0:EC]
        place = onehot[:, :, :, :].rearrange("p a b c -> p (a b c)")[:, EC:2 * EC]
        flat_acc = acc[:, :, :].rearrange("p b f -> p (b f)")
        hits = hit, key_i.bitcast(F32)
        ranks = cnt, flat_acc[:, T:T + EC]
        picked = flat_acc[:, 0:EC], flat_acc[:, 3 * T:3 * T + EC]
        base_ps = psA[:, 2:4, :].rearrange("p a (b c) -> p (a b) c", c=P)
        ident = ident_w[:, HEADS:HEADS + P]
        place_i = acc[:, :, :].rearrange("p b f -> p (b f)")[:, 0:EC].bitcast(I32)
        sort_rec = acc[:, :, :].rearrange("p b f -> p (b f)")[:, EC:EC + HALF * REC].rearrange(
            "p (c w) -> p c w", w=REC)
        dst_id = acc[:, :, :].rearrange("p b f -> p (b f)")[:, 0:T]
        map_tmp = onehot[:, :, :, :].rearrange("p a b c -> p (a b c)")[:, 0:T]
        map_tmp2 = onehot[:, :, :, :].rearrange("p a b c -> p (a b c)")[:, T:2 * T]
        map_rhs = acc[:, :, :].rearrange("p b f -> p (b f)")[:, T:2 * T]
        tile_no = acc[:, :, :].rearrange("p b f -> p (b f)")[:, 2 * T:3 * T]
        tile_no_i = tile_no.bitcast(I32)
        place_t = acc[:, :, :].rearrange("p b f -> p (b f)")[:, 3 * T:4 * T].bitcast(I32)
        place_t2 = idx_a[:, 0:T]

        def bc(ap, n):
            return ap.rearrange("p (k o) -> p k o", o=1).to_broadcast([ap.shape[0], ap.shape[1], n])

        def rep(ap, n):
            return ap.rearrange("p (o k) -> p o k", o=1).to_broadcast([ap.shape[0], n, ap.shape[1]])

        def blocks_of(engine, row, first, n):
            _, regs = nc.values_load_multi_w_load_instructions(
                maps[row:row + 1, bass.ds(first, n)], engines=[engine], min_val=0, max_val=NB,
                skip_runtime_bounds_check_because="the tile map points to blocks 0 to NB")
            return regs

        pads_set = sem("pads_set")
        edges_in = sem("edges_in")
        consts_in = sem("consts_in")
        x_in = sem("x_in")
        row_zero = sem("row_zero")
        work_zero = sem("work_zero")
        work_free = sem("work_free")
        iota_set = sem("iota_set")
        dve_consts = sem("dve_consts")
        attr_in = [sem(f"attr_in{i}") for i in range(ATT_BUFS)]
        attr_t = sem("attr_t")
        attr_t_sb = sem("attr_t_sb")
        attr_mm = sem("attr_mm")
        bias_put = sem("bias_put")
        counts_set = sem("counts_set")
        base_mm = sem("base_mm")
        recs_set = sem("recs_set")
        rec_out = sem("rec_out")
        flag_set = sem("flag_set")
        so_tot = sem("so_tot")
        so_base = sem("so_base")
        so_place = sem("so_place")
        so_copy = sem("so_copy")
        so_sent = sem("so_sent")
        so_pass = sem("so_pass")
        so_in = sem("so_in")
        map_col = sem("map_col")
        map_mm = sem("map_mm")
        map_set = sem("map_set")
        gap_set = sem("gap_set")
        gap_out = sem("gap_out")
        tail_out = sem("tail_out")
        group_in = [sem(f"group_in{i}") for i in range(TC)]
        group_t = sem("group_t")
        field_copy = [sem(f"field_copy{i}") for i in range(2)]
        picked_set = sem("picked_set")
        place_add = sem("place_add")
        bias_out = sem("bias_out")
        bias_in = sem("bias_in")
        tiles_set = sem("tiles_set")
        slot = [sem(f"slot{i}") for i in range(BODY)]
        msg_in = [sem(f"msg_in{i}") for i in range(RING)]
        wb = [sem(f"wb{i}") for i in range(QUAD)]
        seq_in = [sem(f"seq_in{i}") for i in range(RING)]
        idx_rdy = sem("idx_rdy")
        oh_rdy = sem("oh_rdy")
        tr_done = sem("tr_done")
        oht_rdy = sem("oht_rdy")
        got = sem("got")
        pool_turns = sem("pool_turns")
        quad_rdy = sem("quad_rdy")
        prod_rdy = sem("prod_rdy")
        sum_rdy = sem("sum_rdy")
        agg = sem("agg")
        added = sem("added")
        acc_used = sem("acc_used")
        wgt_rdy = sem("wgt_rdy")
        ex_rdy = sem("ex_rdy")
        src_sub = sem("src_sub")
        centred = sem("centred")
        squared = sem("squared")
        ln_var = sem("ln_var")
        ln_sd = sem("ln_sd")
        h_rdy = sem("h_rdy")
        h_t = sem("h_t")
        h_t_sb = sem("h_t_sb")
        h_mm = sem("h_mm")
        h_out = sem("h_out")
        h_out_act = sem("h_out_act")
        tab_out = [sem(f"tab_out{i}") for i in range(2)]
        msgs_done = sem("msgs_done")
        bn_in = sem("bn_in")
        bn_mm = sem("bn_mm")
        bn_var = sem("bn_var")
        bn_sd = sem("bn_sd")
        mv_rdy = sem("mv_rdy")
        mv_t = sem("mv_t")
        mv_copy = sem("mv_copy")
        edge_in = sem("edge_in")
        edge_mm = sem("edge_mm")
        diff_rdy = sem("diff_rdy")
        exp_rdy = sem("exp_rdy")
        ring_free = sem("ring_free")
        out_done = sem("out_done")
        block = ctx.enter_context(nc.Block())

        at_slot = {"0a": 0, "1": 16 * BODIES, "2a": 32 * BODIES, "3a": 48 * BODIES}
        at_agg = {"0b": 0, "1": T, "2b": 2 * T, "3b": 3 * T}
        at_added = {ph: at + 2 * HALF * (i + 1) for i, (ph, at) in enumerate(at_agg.items())}
        at_quad = {"0a": 0, "2a": NQ, "3a": 2 * NQ}
        at_half = {"2b": 0, "3b": NH}
        at_idx = {"1": 0, "2a": NQ + 3, "3a": 2 * (NQ + 3)}
        at_oh = {"0a": 0, "0b": NQ + 1, "1": NQ + 1 + NH, "2a": 2 * (NQ + 1) + NH, "2b": 3 * (NQ + 1) + NH,
                 "3a": 3 * (NQ + 1) + 2 * NH, "3b": 4 * (NQ + 1) + 2 * NH}
        squares_at = {1: 0, "bn": 2, 2: 4, 3: 6, 4: 8}
        tab_at = {0: (0, 0), 1: (13, 12), 2: (14, 13), 3: (27, 25)}

        def bodies(engine, body):
            body(0)
            with engine.Fori(1, BODIES) as g:
                body(g)

        def attr_rounds(engine, start, stop, first, second):
            def round_(g):
                for i in range(ATT_STEPS):
                    first(g, i)
                    if start or i:
                        second(g, i - 1)
            if stop - start == 1:
                round_(start)
            else:
                with engine.Fori(start, stop) as g:
                    round_(g)

        def part(i):
            return slice(0, MG // 2 * QUAD * P) if i == 0 else slice(MG // 2 * QUAD * P, CE)

        def nodes_part(i):
            return slice(0, NB // 2) if i == 0 else slice(NB // 2, NB)

        def wait_if(engine, semaphore, value):
            if not (isinstance(value, int) and value == 0):
                engine.wait_ge(semaphore, value)

        def half_ends(name, row, g, h):
            _, regs = nc.values_load_multi_w_load_instructions(
                end_maps[row:row + 1, bass.ds(g * (2 * RING) + 2 * h, 2 * ENDS)], engines=[name],
                min_val=0, max_val=NB,
                skip_runtime_bounds_check_because="the tile map points to blocks 0 to NB")
            return [(regs[2 * i], regs[2 * i + 1]) for i in range(ENDS)]

        def spans(engine, name, row, first, leaf, ends, t=0, n=HALF):
            lo, hi = ends
            with engine.If(hi - lo):
                if n == 2:
                    leaf(t, 1, lo)
                    leaf(t + 1, 1, hi)
                else:
                    m = t + n // 2
                    mid = blocks_of(name, row, first + (m - 1), 2)
                    spans(engine, name, row, first, leaf, (lo, mid[0]), t, n // 2)
                    spans(engine, name, row, first, leaf, (mid[1], hi), m, n // 2)
            with engine.Else():
                leaf(t, n, lo)

        def span_sum(h, t, n):
            return {8: psA[:, 4 * (h % 2), :], 4: psA[:, 4 * (h % 2) + 2 * (t // 4 % 2), :],
                    2: psT[:, t // 2 % 2, :, :].rearrange("p a b -> p (a b)"),
                    1: psG[:, t % 2, :, :].rearrange("p a b -> p (a b)")}[n]

        def field_out(copy, engine, i):
            engine.wait_ge(group_t, i + 1)
            k = min(P, T - (i // 4) * P)
            ts = slice((i // 4) * P, (i // 4) * P + k)
            ps = psT[:, i % 2, :, 0:k]
            if i % 4 == 0:
                ins = copy(fields[:, 0:4, ts], ps)
            elif i % 4 == 1:
                ins = copy(fields[:, 4, ts], ps[:, 0, :])
            else:
                h = 4 * (i % 4 - 2)
                ins = copy(sc_t[:, ts, h:h + 4].rearrange("p t h -> p h t"), ps)
            ins.then_inc(field_copy[i % 2], 1)

        def pout(b):
            return psA[:, 4 * (b % 2):4 * (b % 2) + 4, :].rearrange("p a b -> p (a b)")

        @block.sync
        def _(sp):
            sp.wait_ge(pads_set, 1)
            for dst, name in ((dst_i, "dst"), (src_i, "src"), (typ_i, "edge_type_8")):
                sp.dma_start(dst[0:EP, :], a[name].rearrange("(p c) -> p c", c=EC)).then_inc(edges_in, 16)
            sp.dma_start(w_in[0:EP, :], a["edge_weight"].rearrange("(p c) -> p c", c=EC)).then_inc(edges_in, 16)
            with nc.allow_non_contiguous_dma("one element of each partition's successor"):
                sp.dma_start(nxt[0:EP - 1, 0:1], a["dst"].rearrange("(p c) -> p c", c=EC)[1:EP, 0:1])\
                    .then_inc(edges_in, 16)
            attr_d = a["edge_attr_32"].rearrange("(p c) f -> p c f", c=EC)
            for i in range(ATT_BUFS):
                sp.dma_start(attr[0:EP, i, :, :], attr_d[:, i * ATT:(i + 1) * ATT, :]).then_inc(attr_in[i], 16)
            with sp.Fori(0, EC // ATT // ATT_BUFS - 1) as g:
                for i in range(ATT_BUFS):
                    sp.wait_ge(attr_t, g * ATT_BUFS + (i + 1))
                    sp.dma_start(attr[0:EP, i, :, :],
                                 attr_d[:, bass.ds(g * (ATT_BUFS * ATT) + (i + ATT_BUFS) * ATT, ATT), :])\
                        .then_inc(attr_in[i], 16)
            sp.wait_ge(recs_set, 1)
            sp.dma_start(rec.rearrange("(p c) w -> p (c w)", c=EC), work[:, 0:EC * REC]).then_inc(rec_out, 16)
            sp.wait_ge(rec_out, 16)
            sp.wait_ge(flag_set, 1)
            unsorted = sp.value_load(flag[0:1, 0:1], min_val=0, max_val=1)
            with sp.If(unsorted):
                sp.wait_ge(so_pass, 1)
                sp.dma_start(work[:, 0:EC * REC], rec2.rearrange("(p c) w -> p (c w)", c=EC)).then_inc(so_in, 16)
                sp.wait_ge(so_pass, 2)
            with sp.Else():
                sp.nop()
            sp.wait_ge(tiles_set, 1)
            sp.dma_start(bias_seq, scores[:, :]).then_inc(bias_out, 16)
            msgs_p = msgs.rearrange("(p t) w -> p (t w)", t=T)

            def load_half(first, h):
                sp.dma_start(msg_seq[:, h, :, :].rearrange("p s w -> p (s w)"),
                             msgs_p[:, bass.ds(first * MSG, HALF * MSG)]).then_inc(msg_in[h], 16)
            sp.wait_ge(msgs_done, 1)
            for h in range(RING):
                load_half(h * HALF, h)
            with sp.Fori(0, ROUNDS - 1) as g:
                for h in range(RING):
                    sp.wait_ge(agg, g * SPAN + (at_agg["0b"] + (h + 1) * HALF))
                    load_half(g * SPAN + (h + RING) * HALF, h)

            for b in range(NB):
                sp.wait_ge(h_out, NB + b + 1)
                sp.wait_ge(h_out_act, b + 1)
                sp.dma_start(rel_table.rearrange("(n r) f -> n (r f)", r=NREL)[b * P:(b + 1) * P, :],
                             rel_stage[:, b % 2, :]).then_inc(tab_out[b % 2], 16)

            def write_back(n, rows):
                g0 = at_slot[f"{n}a"]
                with sp.Fori(0, BODIES) as g:
                    for k in range(4):
                        for j in range(QUAD):
                            sp.wait_ge(slot[4 * k + j], g * 16 + (g0 + 16))
                        sp.dma_start(rows_seq[:, bass.ds(g * (BODY * F) + 4 * k * F, QUAD * F)]
                                     .rearrange("p (s w) -> p s w", w=F), rows(k)).then_inc(wb[k], 16)

            def read_rows(n):
                for k in range(4):
                    sp.wait_ge(wb[k], 16 * BODIES * (n - 1))
                sp.wait_ge(diff_rdy, 2 * (n - 1))
                for h in range(RING):
                    sp.dma_start(seq_ring[:, h, :, :], rows_seq[:, h * HALF * F:(h + 1) * HALF * F]
                                 .rearrange("p (s w) -> p s w", w=F)).then_inc(seq_in[h], 16)
                with sp.Fori(0, ROUNDS - 1) as g:
                    for h in range(RING):
                        sp.wait_ge(wgt_rdy, g * RING + (at_half[f"{n}b"] + h + 1))
                        sp.dma_start(seq_ring[:, h, :, :],
                                     rows_seq[:, bass.ds(g * (SPAN * F) + (h + RING) * HALF * F, HALF * F)]
                                     .rearrange("p (s w) -> p s w", w=F)).then_inc(seq_in[h], 16)

            sp.wait_ge(h_rdy, 3)
            sp.dma_start(gat_table.rearrange("(b p) w -> p b w", p=P)[:, :, 0:F], H).then_inc(tab_out[0], 16)
            sp.wait_ge(h_out, 3 * NB)
            sp.dma_start(gat_table.rearrange("(b p) w -> p b w", p=P)[:, :, F:F + HEADS],
                         H2[:, :, 0:HEADS]).then_inc(tab_out[1], 16)
            write_back(2, lambda k: gat_ring[:, 4 * k:4 * k + 4, 0:F])
            read_rows(2)
            for b in range(NB):
                sp.wait_ge(h_out, 3 * NB + b + 1)
                sp.dma_start(kv_table[b * P:(b + 1) * P, :], kv_stage[:, b % 2, :]).then_inc(tab_out[b % 2], 16)
            for i in range(2):
                sp.wait_ge(tab_out[i], 16 * tab_at[3][i])
            sp.wait_ge(bias_out, 16)
            sp.dma_start(MAXS, bias_seq).then_inc(bias_in, 16)
            write_back(3, lambda k: kv_ring[:, 4 * k:4 * k + 4, F:2 * F])
            read_rows(3)
            sp.wait_ge(h_out, 5 * NB)
            sp.dma_start(out[0:(NB - 1) * P, :].rearrange("(b p) f -> p b f", p=P), X[:, 0:NB - 1, :])\
                .then_inc(out_done, 16)
            sp.dma_start(out[(NB - 1) * P:N, :], X[0:NLAST, NB - 1, :]).then_inc(out_done, 16)
            sp.wait_ge(out_done, 32)

        @block.gpsimd
        def _(pool):
            def weigh(n):
                pool.wait_ge(ring_free, n - 1)
                with pool.Fori(0, ROUNDS) as g:
                    for h in range(RING):
                        first = g * SPAN + h * HALF
                        pool.wait_ge(agg, g * SPAN + (at_agg[f"{n}b"] + (h + 1 - RING) * HALF))
                        pool.wait_ge(seq_in[h], g * 16 + (16 * ROUNDS * (n - 2) + 16))
                        ex = sc_t[:, bass.ds(first, HALF), :]
                        nc.gpsimd.tensor_tensor(
                            wgt_ring[:, h, :, 0:F].rearrange("p s (h d) -> p s h d", d=HD),
                            seq_ring[:, h, :, :].rearrange("p s (h d) -> p s h d", d=HD),
                            ex.rearrange("p s (h o) -> p s h o", o=1).to_broadcast([P, HALF, HEADS, HD]),
                            ALU.mult).then_inc(wgt_rdy, 1)
            nc.gpsimd.memset(ident_w[:], 0.0).then_inc(iota_set, 1)
            nc.gpsimd.memset(lower[:], 1.0).then_inc(iota_set, 1)
            nc.gpsimd.memset(head_mask[:], 1.0).then_inc(iota_set, 1)
            nc.gpsimd.iota(iota_i[:], pattern=[[1, P]], base=0, channel_multiplier=0).then_inc(iota_set, 1)
            nc.gpsimd.iota(node_no_i[:], pattern=[[1, 1]], base=0, channel_multiplier=1).then_inc(iota_set, 1)
            nc.gpsimd.iota(tile_no_i, pattern=[[1, T]], base=0, channel_multiplier=0).then_inc(iota_set, 1)
            pool.wait_ge(iota_set, 6)
            nc.gpsimd.affine_select(out=ident_w[:], in_=ident_w[:], compare_op=ALU.not_equal, fill=1.0,
                                    base=HEADS, pattern=[[-1, P + 2 * HEADS]], channel_multiplier=1)\
                .then_inc(iota_set, 1)
            nc.gpsimd.affine_select(out=lower[:], in_=lower[:], compare_op=ALU.is_gt, fill=0.0, base=0,
                                    pattern=[[1, P]], channel_multiplier=-1).then_inc(iota_set, 1)
            nc.gpsimd.affine_select(out=head_mask[:], in_=head_mask[:], compare_op=ALU.is_ge, fill=0.0, base=0,
                                    pattern=[[-HD, HEADS]], channel_multiplier=1).then_inc(iota_set, 1)
            pool.wait_ge(iota_set, 9)
            nc.gpsimd.affine_select(out=head_mask[:], in_=head_mask[:], compare_op=ALU.is_ge, fill=0.0,
                                    base=HD - 1, pattern=[[HD, HEADS]], channel_multiplier=-1)\
                .then_inc(iota_set, 1)
            nc.gpsimd.memset(bn[:, :, :], 0.0).then_inc(row_zero, 1)
            pool.wait_ge(row_zero, 1)
            pool.dma_start(msgs.rearrange("(p t) w -> p t w", t=T)[:, MG_T:T, :],
                           rep(bn[:, :, :].rearrange("p a f -> p (a f)")[:, 0:MSG], T - MG_T)).then_inc(tail_out, 16)
            pool.wait_ge(work_free, 1)
            pool.wait_ge(h_t, NB)
            nc.gpsimd.memset(recs[:, :, POS_ + 1:EE_], 0.0).then_inc(work_zero, 1)
            def add_picked(b, i):
                pool.wait_ge(picked_set, b + 1)
                if not (isinstance(b, int) and b == 0):
                    pool.wait_ge(place_add, b)
                nc.gpsimd.tensor_tensor(place, place, picked[i], ALU.add).then_inc(place_add, 1)
            add_picked(0, 0)
            with pool.Fori(0, NB // 2) as g:
                for i in range(2):
                    add_picked(g * 2 + (i + 1), 1 - i)
            pool.wait_ge(tail_out, 16)
            pool.wait_ge(gap_set, 1)
            for b in range(NB):
                nc.gpsimd.indirect_dma_start(
                    msgs, bass.IndirectOffsetOnAxis(ap=gap_i[:, 0, b:b + 1], axis=0),
                    bn[:, :, :].rearrange("p a f -> p (a f)")[:, 0:MSG], None,
                    bounds_check=PLACES - 1, oob_is_err=False).then_inc(gap_out, 16)
            pool.wait_ge(flag_set, 1)
            unsorted = pool.value_load(flag[0:1, 0:1], min_val=0, max_val=1)
            with pool.If(unsorted):
                pool.wait_ge(rec_out, 16)
                for n, target in enumerate((rec2, rec)):
                    pool.wait_ge(so_place, n + 1)
                    c0, s0 = n * 2 * (EC // HALF), n * 16 * HALF * (EC // HALF)
                    with pool.Fori(0, EC // HALF) as g:
                        nc.gpsimd.tensor_copy(sort_rec, recs[:, bass.ds(g * HALF, HALF), :]).then_inc(so_copy, 1)
                        nc.gpsimd.tensor_copy(idx_ring[:, 0:HALF], place_i[:, bass.ds(g * HALF, HALF)])\
                            .then_inc(so_copy, 1)
                        pool.wait_ge(so_copy, g * 2 + (c0 + 2))
                        pool.sem_inc(pool_turns, 1)
                        for j in range(HALF):
                            nc.gpsimd.indirect_dma_start(
                                target, bass.IndirectOffsetOnAxis(ap=idx_ring[:, j:j + 1], axis=0),
                                sort_rec[:, j, :], None, bounds_check=P * EC - 1, oob_is_err=False)\
                                .then_inc(so_sent, 16)
                        pool.wait_ge(so_sent, g * (16 * HALF) + (s0 + 16 * HALF))
                    pool.sem_inc(so_pass, 1)
            with pool.Else():
                pool.nop()
            pool.wait_ge(rec_out, 16)
            pool.wait_ge(map_set, 1)
            for c in range(TC):
                k = min(P, T - c * P)
                nc.gpsimd.indirect_dma_start(
                    group_rows[c][0:k, :], None, rec.rearrange("(g e) w -> g (e w)", e=P),
                    bass.IndirectOffsetOnAxis(ap=group_i[0:k, c:c + 1], axis=0),
                    bounds_check=GROUPS - 1, oob_is_err=False).then_inc(group_in[c], 16)
            pool.wait_ge(gap_out, 16 * NB)
            with pool.Fori(0, BODIES) as g:
                for k in range(4):
                    pool.wait_ge(quad_rdy, g * 4 + (k + 1))
                    pool.sem_inc(pool_turns, 1)
                    for j in range(QUAD):
                        s = 4 * k + j
                        nc.gpsimd.indirect_dma_start(
                            msgs, bass.IndirectOffsetOnAxis(ap=idx_ring[:, s:s + 1], axis=0),
                            msg_ring[:, s, :], None, bounds_check=PLACES - 1, oob_is_err=False).then_inc(slot[s], 16)
            for s in range(BODY):
                pool.wait_ge(slot[s], 16 * BODIES)
            pool.sem_inc(msgs_done, 1)
            for n, ph, table, ring in ((1, "1", rel_table, row_ring), (2, "2a", gat_table, gat_ring),
                                       (3, "3a", kv_table, kv_ring)):
                if n == 1:
                    pool.wait_ge(bn_in, 1)
                else:
                    pool.wait_ge(acc_used, n - 1)
                nc.gpsimd.memset(acc[:, :, :], 0.0).then_inc(added, 2 * HALF)
                for i in range(2):
                    pool.wait_ge(tab_out[i], 16 * tab_at[n][i])
                with pool.Fori(0, BODIES) as g:
                    for k in range(4):
                        pool.wait_ge(idx_rdy, g * 4 + (at_idx[ph] + k + 1))
                        pool.sem_inc(pool_turns, 1)
                        for j in range(QUAD):
                            s = 4 * k + j
                            nc.gpsimd.indirect_dma_start(
                                ring[:, s, :], None, table,
                                bass.IndirectOffsetOnAxis(ap=idx_ring[:, s:s + 1], axis=0),
                                bounds_check=table.shape[0] - 1, oob_is_err=False).then_inc(slot[s], 16)
                if n > 1:
                    weigh(n)

        @block.scalar
        def _(act):
            loads = []

            def load(dst, src):
                act.dma_start(dst, src).then_inc(consts_in, 16)
                loads.append(dst)
            act.dma_start(X[:, 0:NB - 1, :], a["x"][0:(NB - 1) * P, :].rearrange("(b p) f -> p b f", p=P))\
                .then_inc(x_in, 16)
            act.wait_ge(pads_set, 2)
            act.dma_start(X[0:NLAST, NB - 1, :], a["x"][(NB - 1) * P:N, :]).then_inc(x_in, 16)
            load(w0[:], a["L0_gnn_weight"])
            load(w_rel[:], a["L1_gnn_weight"].rearrange("r i o -> i r o"))
            for i, n in enumerate(("Wq", "Wk", "Wv")):
                load(wqkv[:, i, :], a["L3_gnn_" + n])
            load(wo[:], a["L3_gnn_Wo"])
            for i, n in enumerate(("L0_gnn_bias", "L0_gnn_bn_gamma", "L0_gnn_bn_beta",
                                   "L3_gnn_bq", "L3_gnn_bk", "L3_gnn_bv", "L3_gnn_bo")):
                load(vecs[:, i, :], a[n].rearrange("(o n) -> o n", o=1).to_broadcast([P, F]))
            for i in range(QUAD):
                load(be_row[0:1, HEADS * i:HEADS * (i + 1)], a["L3_gnn_be"].rearrange("(o n) -> o n", o=1))
                load(we_blk[EF * i:EF * (i + 1), HEADS * i:HEADS * (i + 1)], a["L3_gnn_We"])
            for h in range(HEADS):
                for i in range(2):
                    load(att_col[HD * h:HD * (h + 1), i:i + 1],
                         a["L2_gnn_att"][h, HD * i:HD * (i + 1)].rearrange("(n o) -> n o", o=1))
            assert len(loads) == N_CONSTS

            def squares(at):
                for i in range(2):
                    act.wait_ge(centred, at + i + 1)
                    nc.scalar.activation(H2[:, nodes_part(i), :], H[:, nodes_part(i), :], ACT.Square)\
                        .then_inc(squared, 1)

            def std(n):
                squares(squares_at[n])
                act.wait_ge(ln_var, n)
                nc.scalar.activation(col[:, 4, :], col[:, 3, :], ACT.Sqrt).then_inc(ln_sd, 1)

            def transpose_out(n, b):
                act.wait_ge(h_t, n * NB + b + 1)
                nc.scalar.activation(hT[:, b % 2, :], psT[:, b % 2, 0, :], ACT.Copy).then_inc(h_t_sb, 1)

            def onehots_out(ph, g, k):
                act.wait_ge(tr_done, g * 4 + (at_quad[ph] + k + 1))
                nc.scalar.activation(onehot_t[:, k % 2, :, :], psT[:, k % 2, :, :], ACT.Copy).then_inc(oht_rdy, 1)

            def feed(ph, idx):
                def indices(first, s):
                    nc.scalar.activation(idx_ring[:, s:s + QUAD], idx[:, bass.ds(first, QUAD)], ACT.Copy)\
                        .then_inc(idx_rdy, 1)
                for k in range(3):
                    indices(4 * k, 4 * k)

                def body(g):
                    for k in range(4):
                        if ph == "1":
                            act.wait_ge(agg, g * BODY + (at_agg[ph] + 4 * k))
                        else:
                            onehots_out(ph, g, k)
                            act.wait_ge(quad_rdy, g * 4 + (at_quad[ph] + k))
                            wait_if(act, wb[(k + 3) % 4], g * 16 + (16 * BODIES * (ph == "3a") + 16 * (k > 0)))
                        indices(g * BODY + 4 * (k + 3), 4 * ((k + 3) % 4))
                bodies(act, body)

            def exps(n):
                for i in range(2):
                    act.wait_ge(diff_rdy, 2 * (n - 1) + i + 1)
                    nc.scalar.activation(MAXS[:, part(i)], MAXS[:, part(i)], ACT.Exp, scale=-1.0)\
                        .then_inc(exp_rdy, 1)

            def exps_behind(n):
                act.wait_ge(ring_free, n - 1)
                with act.Fori(0, ROUNDS) as g:
                    for h in range(RING):
                        act.wait_ge(agg, g * SPAN + (at_agg[f"{n}b"] + (h + 1 - RING) * HALF))
                        nc.scalar.activation(wgt_ring[:, h, :, F:F + HEADS],
                                             sc_t[:, bass.ds(g * SPAN + h * HALF, HALF), :], ACT.Copy)\
                            .then_inc(ex_rdy, 1)

            std(1)
            transpose_out(0, 0)
            for b in range(NB):
                if b + 1 < NB:
                    transpose_out(0, b + 1)
                act.wait_ge(h_mm, b + 1)
                nc.scalar.activation(nodes[:, b, :], pout(b)[:, 0:F], ACT.Copy).then_inc(h_out, 1)
            act.wait_ge(work_zero, 1)

            def attr_out(g, i):
                act.wait_ge(attr_t, g * ATT_STEPS + (i + 1))
                if not isinstance(g, int) or i >= 2:
                    act.wait_ge(attr_mm, g * ATT_STEPS + (i - 1))
                nc.scalar.activation(onehot_t[:, i % 2, :, 0:EP], psT[:, i % 2, :, 0:EP], ACT.Copy)\
                    .then_inc(attr_t_sb, 1)

            def biases_out(g, i):
                act.wait_ge(attr_mm, g * ATT_STEPS + (i + 1))
                nc.scalar.activation(recs[:, bass.ds(g * (ATT_STEPS * ATT) + i * ATT, ATT), EE_:EE_ + HEADS],
                                     psG[:, i % 2, 0, :].rearrange("p (c h) -> p c h", h=HEADS), ACT.Copy)\
                    .then_inc(bias_put, 1)
            attr_rounds(act, 0, 1, attr_out, biases_out)
            attr_rounds(act, 1, ATT_ROUNDS, attr_out, biases_out)
            biases_out(ATT_ROUNDS - 1, ATT_STEPS - 1)
            for i in range(1, 4 * TC, 2):
                field_out(nc.scalar.copy, act, i)
            with act.Fori(0, BODIES) as g:
                for k in range(4):
                    onehots_out("0a", g, k)
            squares(squares_at["bn"])
            act.wait_ge(bn_var, 1)
            nc.scalar.activation(bn[:, 2, :], bn[:, 1, :], ACT.Sqrt).then_inc(bn_sd, 1)
            std(2)
            transpose_out(1, 0)
            for b in range(NB):
                if b + 1 < NB:
                    transpose_out(1, b + 1)
                act.wait_ge(h_mm, NB + b + 1)
                if b >= 2:
                    act.wait_ge(tab_out[b % 2], 16 * (b // 2))
                nc.scalar.activation(rel_stage[:, b % 2, 0:512], pout(b)[:, 0:512], ACT.Copy)\
                    .then_inc(h_out_act, 1)
            feed("1", idx_b)
            std(3)
            for b in range(NB):
                transpose_out(2, b)
            feed("2a", idx_a)
            exps(1)
            exps_behind(2)
            std(4)
            for b in range(NB):
                transpose_out(3, b)
            feed("3a", idx_a)
            exps(2)
            exps_behind(3)
            for b in range(NB):
                transpose_out(4, b)

        @block.tensor
        def _(pe):
            def node_products(n, weights):
                pe.wait_ge(h_rdy, n + 1)
                nc.tensor.transpose(psT[:, 0, 0, :], H[:, 0, :], ident).then_inc(h_t, 1)
                for b in range(NB):
                    if b + 1 < NB:
                        nc.tensor.transpose(psT[:, (b + 1) % 2, 0, :], H[:, b + 1, :], ident).then_inc(h_t, 1)
                    pe.wait_ge(h_t_sb, n * NB + b + 1)
                    if b >= 2:
                        pe.wait_ge(h_out, n * NB + b - 1)
                        if n == 1:
                            pe.wait_ge(h_out_act, b - 1)
                    at = 0
                    for w in weights:
                        width = w.shape[1] * (w.shape[2] if len(w.shape) > 2 else 1)
                        ins = nc.tensor.matmul(pout(b)[:, at:at + width], hT[:, b % 2, :], w, start=True, stop=True)
                        at += width
                    ins.then_inc(h_mm, 1)

            def fetch(ph, rows, width):
                with pe.Fori(0, BODIES) as g:
                    regs = blocks_of(ENG.PE, 0, g * BODY, BODY)
                    for k in range(4):
                        pe.wait_ge(oh_rdy, g * 4 + (at_oh[ph] + k + 1))
                        for j in range(QUAD):
                            ins = nc.tensor.transpose(psT[:, k % 2, j, :], onehot[:, k % 2, j, :], ident)
                        ins.then_inc(tr_done, 1)
                        pe.wait_ge(oht_rdy, g * 4 + (at_quad[ph] + k + 1))
                        for j in range(QUAD):
                            ins = nc.tensor.matmul(psG[:, k % 2, j, 0:width], onehot_t[:, k % 2, j, :],
                                                   rows(regs[4 * k + j]), start=True, stop=True)
                        ins.then_inc(got, 1)

            def move(m, source, ready):
                for q in range(MG):
                    ready(q)
                    if q >= 2:
                        pe.wait_ge(mv_copy, m * MG + q - 1)
                    for j in range(4 * q, min(4 * q + 4, CT)):
                        ins = nc.tensor.transpose(psT[:, q % 2, j % 4, :], source[:, j * P:(j + 1) * P], ident)
                    ins.then_inc(mv_t, 1)

            def to_scan(m, n):
                def ready(q):
                    if q == 0:
                        pe.wait_ge(mv_rdy, n)
                move(m, MAXS, ready)

            def from_scan(m, n):
                def ready(q):
                    if q in (0, MG // 2):
                        pe.wait_ge(exp_rdy, 2 * (n - 1) + (1 if q == 0 else 2))
                move(m, MAXS, ready)

            def sum_half(ph, row, g, h, ends, rows, width):
                def leaf(t, n, block):
                    if n < 4:
                        pe.wait_ge(added, g * SPAN + (at_added[ph] + h * HALF + t - n))
                    for j in range(n):
                        ins = nc.tensor.matmul(span_sum(h, t, n)[:, 0:width], onehot[:, h % AHEAD, t + j, :],
                                               rows(t + j), start=(j == 0), stop=(j == n - 1))
                    ins.then_inc(agg, n)
                pe.wait_ge(added, g * SPAN + (at_added[ph] + (h - 1) * HALF))
                spans(pe, ENG.PE, row, g * SPAN + h * HALF, leaf, ends)

            def weighted_sums(n):
                with pe.Fori(0, ROUNDS) as g:
                    for h in range(RING):
                        if h % ENDS == 0:
                            ends = half_ends(ENG.PE, 0, g, h)
                        pe.wait_ge(wgt_rdy, g * RING + (at_half[f"{n}b"] + h + 1))
                        pe.wait_ge(ex_rdy, g * RING + (at_half[f"{n}b"] + h + 1))
                        pe.wait_ge(oh_rdy, g * RING + (at_oh[f"{n}b"] + h + 1))
                        sum_half(f"{n}b", 0, g, h, ends[h % ENDS], lambda j: wgt_ring[:, h, j, :], F + HEADS)

            def carries(d):
                pe.wait_ge(edge_in, 2 * d + 3)
                nc.tensor.matmul(psG[0:1, 0, 0, :], MAXS[:, CE - 1:CE] if d % 2 == 0 else MAXS[:, 0:1], ident,
                                 start=True, stop=True).then_inc(edge_mm, 1)
                pe.wait_ge(edge_in, 2 * d + 4)
                sh = 0 if d % 2 == 0 else 2 * HEADS
                nc.tensor.matmul(psG[:, 1, 0, 0:1], carried[0:1, sh:sh + P], ones[0:1, 0:1],
                                 start=True, stop=True).then_inc(edge_mm, 1)

            pe.wait_ge(iota_set, 10)
            pe.wait_ge(dve_consts, 1)
            pe.wait_ge(consts_in, 16 * N_CONSTS)
            node_products(0, [w0[:]])

            def attr_transposes(g, i):
                pe.wait_ge(attr_in[i % ATT_BUFS], g * 32 + 16 * (1 + i // ATT_BUFS))
                for j in range(QUAD):
                    ins = nc.tensor.transpose(
                        psT[:, i % 2, j, 0:EP],
                        attr[0:EP, i % ATT_BUFS, 4 * j:4 * j + 4, :].rearrange("p c f -> p (c f)"),
                        ident[0:EP, 0:EP])
                ins.then_inc(attr_t, 1)

            def bias_products(g, i):
                pe.wait_ge(attr_t_sb, g * ATT_STEPS + (i + 1))
                nc.tensor.matmul(psG[:, i % 2, 0, :], ones[0:1, :], be_step[0:1, :], start=True, stop=False)
                for j in range(QUAD):
                    k = QUAD * HEADS
                    ins = nc.tensor.matmul(psG[0:EP, i % 2, 0, k * j:k * (j + 1)], onehot_t[:, i % 2, j, 0:EP],
                                           we_blk[:], start=False, stop=(j == QUAD - 1))
                ins.then_inc(attr_mm, 1)
            pe.wait_ge(dve_consts, 2)
            attr_rounds(pe, 0, 1, attr_transposes, bias_products)
            attr_rounds(pe, 1, 2, attr_transposes, bias_products)
            pe.wait_ge(counts_set, 1)
            for m in range(2):
                for i in range(2):
                    nc.tensor.matmul(base_ps[0:NBX, 2, 2 * m + i:2 * m + i + 1], cum[:, m, i:i + NBX],
                                     ones[:, 0:1], start=True, stop=True)
            nc.tensor.matmul(base_ps[:, 1, 0:2], ones[:], vio[:, 2:4], start=True, stop=True).then_inc(base_mm, 1)
            pe.wait_ge(map_col, 1)
            nc.tensor.matmul(base_ps[0:NBX, 2, 0:2], lower[0:NBX, 0:NBX], n_tiles[:], start=True, stop=True)\
                .then_inc(map_mm, 1)
            pe.wait_ge(map_col, 2)
            nc.tensor.matmul(base_ps[:, 0, 0:NB], lower[:], tot[:, 0:NB], start=True, stop=False)
            nc.tensor.matmul(base_ps[:, 0, 0:NB], ones[0:NBX, :], diag[:, 0, 0:NB], start=False, stop=True)
            nc.tensor.matmul(base_ps[:, 1, 0:2 * NBX], ones[0:NBX, :],
                             diag[:, 1:3, :].rearrange("p a b -> p (a b)"), start=True, stop=True).then_inc(base_mm, 1)
            attr_rounds(pe, 2, ATT_ROUNDS, attr_transposes, bias_products)
            bias_products(ATT_ROUNDS - 1, ATT_STEPS - 1)
            pe.wait_ge(flag_set, 1)
            unsorted = pe.value_load(flag[0:1, 0:1], min_val=0, max_val=1)
            with pe.If(unsorted):
                for n in range(2):
                    pe.wait_ge(so_tot, n + 1)
                    nc.tensor.matmul(psG[:, 1, 0, 0:NKEY], lower[:], tot[:], start=True, stop=False)
                    nc.tensor.matmul(psG[:, 1, 0, 0:NKEY], ones[:], totc[:], start=False, stop=True)\
                        .then_inc(so_base, 1)
            with pe.Else():
                pe.nop()
            for m in range(2):
                pe.wait_ge(map_col, 3 + m)
                if m == 0:
                    for c in range(TC):
                        k = min(P, T - c * P)
                        nc.tensor.matmul(psG[0:k, 1, 3, c:c + 1], map_tmp[0:NBX, c * P:c * P + k], shift[:],
                                         start=True, stop=True)
                for c in range(2):
                    ins = nc.tensor.matmul(psA[:, 4 * m + 2 * c:4 * m + 2 * c + 2, :]
                                           .rearrange("p a b -> p (a b)")[:, 0:T // 2],
                                           ones[0:NBX, :], map_rhs[0:NBX, c * (T // 2):(c + 1) * (T // 2)],
                                           start=True, stop=True)
                ins.then_inc(map_mm, 1)
            for i in range(4 * TC):
                c, k = i // 4, min(P, T - (i // 4) * P)
                if i % 4 == 0:
                    pe.wait_ge(group_in[c], 16)
                if i >= 2:
                    pe.wait_ge(field_copy[i % 2], i // 2)
                rows = group_rows[c].rearrange("p (e w) -> p e w", w=REC)
                for j in range(1 if i % 4 == 1 else 4):
                    ins = nc.tensor.transpose(psT[:, i % 2, j, 0:k], rows[0:k, :, 4 * (i % 4) + j], ident[0:k, 0:k])
                ins.then_inc(group_t, 1)
            to_scan(0, 1)
            pe.wait_ge(edge_in, 1)
            nc.tensor.matmul(psG[:, 0, 0, 0:1], ident_w[:, 0:P], chunk_ends[:, 1:2], start=True, stop=True)
            nc.tensor.matmul(psG[:, 0, 0, 1:2], ident_w[:, 2 * HEADS:2 * HEADS + P], chunk_ends[:, 0:1],
                             start=True, stop=True).then_inc(edge_mm, 1)

            pe.wait_ge(h_out, NB)
            fetch("0a", lambda r: nodes[:, bass.ds(r, 1), :], F)
            pe.wait_ge(edge_in, 2)
            nc.tensor.matmul(psG[0:1, 0, 0, :], chunk_ends[:, 2:3], ident, start=True, stop=True)
            nc.tensor.matmul(psG[0:1, 0, 1, :], chunk_ends[:, 3:4], ident, start=True, stop=True).then_inc(edge_mm, 1)
            with pe.Fori(0, ROUNDS) as g:
                for h in range(RING):
                    if h % ENDS == 0:
                        ends = half_ends(ENG.PE, 32, g, h)
                    pe.wait_ge(oh_rdy, g * RING + (at_oh["0b"] + h + 1))
                    sum_half("0b", 32, g, h, ends[h % ENDS], lambda j: msg_seq[:, h, j, 0:F], F)
            for i, src in enumerate((H, H2)):
                if i == 0:
                    pe.wait_ge(bn_in, 1)
                for b in range(NB):
                    if i == 1 and b in (0, nodes_part(1).start):
                        pe.wait_ge(squared, squares_at["bn"] + (1 if b == 0 else 2))
                    k = NLAST if b == NB - 1 else P
                    ins = nc.tensor.matmul(psG[:, 0, 0, :], ones[0:k, :], src[0:k, b, :],
                                           start=(b == 0), stop=(b == NB - 1))
                ins.then_inc(bn_mm, 1)
            node_products(1, [w_rel[:, 0:4, :], w_rel[:, 4:8, :]])
            with pe.Fori(0, BODIES) as g:
                for k in range(4):
                    pe.wait_ge(oh_rdy, g * 4 + (at_oh["1"] + k + 1))
                    for j in range(QUAD):
                        s = 4 * k + j
                        pe.wait_ge(slot[s], g * 16 + (at_slot["1"] + 16))
                        nc.tensor.matmul(psA[:, s % HALF, 0:F], onehot[:, k % 2, j, :], row_ring[:, s, :],
                                         start=True, stop=True).then_inc(agg, 1)
            node_products(2, [att_blk[:]])
            fetch("2a", lambda r: s_dst[:, bass.ds(r, 1), :], HEADS)
            to_scan(1, 2)
            carries(0)
            carries(1)
            from_scan(2, 1)
            weighted_sums(2)
            node_products(3, [wqkv[:, :, :]])
            fetch("3a", lambda r: nodes[:, bass.ds(r, 1), :], F)
            to_scan(3, 3)
            carries(2)
            carries(3)
            from_scan(4, 2)
            weighted_sums(3)
            node_products(4, [wo[:]])

        @block.vector
        def _(dve):
            V = nc.vector
            sc = scores[:, :].rearrange("p (c j h) -> p c j h", c=CH, h=HEADS)

            def drain():
                dve.drain()

            def one_hots(first, k):
                V.tensor_tensor(onehot[:, k % 2, 0:QUAD, :], rep(iota[:, :], QUAD),
                                bc(dst_local[:, bass.ds(first, QUAD)], P), ALU.is_equal).then_inc(oh_rdy, 1)

            def add(ph, reg, g, t, sums, n=1, span=SPAN):
                dve.wait_ge(added, g * span + (at_added[ph] + t))
                V.tensor_tensor(acc[:, bass.ds(reg, 1), 0:sums.shape[1]], acc[:, bass.ds(reg, 1), 0:sums.shape[1]],
                                sums.rearrange("p (o w) -> p o w", o=1), ALU.add).then_inc(added, n)

            def block_sums(ph, row, width, prepare):
                def body(g, last):
                    for h in range(RING):
                        if h % ENDS == 0:
                            ends = half_ends(ENG.DVE, row, g, h)
                        if not (last and h >= RING - 2):
                            prepare(g, h + 2)

                        def leaf(t, n, block):
                            dve.wait_ge(agg, g * SPAN + (at_agg[ph] + h * HALF + t + n))
                            add(ph, block, g, h * HALF + t, span_sum(h, t, n)[:, 0:width], n)
                        spans(dve, ENG.DVE, row, g * SPAN + h * HALF, leaf, ends[h % ENDS])
                prepare(0, 0)
                prepare(0, 1)
                with dve.Fori(0, ROUNDS - 1) as g:
                    body(g, False)
                body(ROUNDS - 1, True)
                dve.wait_ge(added, at_added[ph] + T)

            def layernorm(n):
                V.tensor_reduce(col[:, 0, :], X[:, :, :], AXX, ALU.add)
                drain()
                V.tensor_scalar(col[:, 1, :], col[:, 0, :], 1.0 / F, None, ALU.mult)
                drain()
                for i in range(2):
                    bs = nodes_part(i)
                    V.tensor_tensor(H[:, bs, :], X[:, bs, :], bc(col[:, 1, bs], F), ALU.subtract)\
                        .then_inc(centred, 1)
                for i in range(2):
                    dve.wait_ge(squared, squares_at[n] + i + 1)
                    V.tensor_reduce(col[:, 2, nodes_part(i)], H2[:, nodes_part(i), :], AXX, ALU.add)
                drain()
                V.tensor_scalar(col[:, 3, :], col[:, 2, :], 1.0 / F, LN_EPS, ALU.mult, ALU.add).then_inc(ln_var, 1)
                dve.wait_ge(ln_sd, n)
                V.reciprocal(col[:, 5, :], col[:, 4, :])
                drain()
                V.scalar_tensor_tensor(H, H, 0.0, bc(col[:, 5, :], F), ALU.max, ALU.mult).then_inc(h_rdy, 1)

            def block_out(n, b, put):
                dve.wait_ge(h_mm, n * NB + b + 1)
                put(b, pout(b)).then_inc(h_out, 1)

            def move_out(m, dest):
                for q in range(MG):
                    k = min(4, CT - 4 * q)
                    dve.wait_ge(mv_t, m * MG + q + 1)
                    d, s = dest(q, k, psT[:, q % 2, 0:k, :])
                    V.tensor_copy(d, s).then_inc(mv_copy, 1)
                drain()

            def to_scan_out(m):
                move_out(m, lambda q, k, ps: (SCAN[:, 4 * q * P:(4 * q + k) * P].rearrange("p (j e) -> p j e", e=P), ps))

            def from_scan_out(m):
                move_out(m, lambda q, k, ps: (sc_c[:, 4 * q:4 * q + k, :, :],
                                              ps.rearrange("p j (c h) -> p j c h", h=HEADS)))

            def segment_max(d0):
                for d in range(2):
                    fwd = d == 0
                    rev = slice(None) if fwd else slice(None, None, -1)
                    fl = flags[:, 0:CE] if fwd else flags[:, 1:CE + 1]
                    start = SCAN if fwd else MAXS
                    V.tensor_tensor_scan(MAXS[:, rev], fl[:, rev], start[:, rev], -BIG, ALU.add, ALU.max)\
                        .then_inc(edge_in, 1)
                    dve.wait_ge(edge_mm, 2 * (d0 + d) + 3)
                    V.tensor_copy(tails[0:1, :], psG[0:1, 0, 0, :])
                    V.memset(carried[0:1, :], -BIG)
                    drain()
                    row = carried[0:1, HEADS:HEADS + P]
                    for h in range(HEADS):
                        V.tensor_tensor_scan(row[:, h::HEADS][:, rev], link[0:1, d, h::HEADS][:, rev],
                                             tails[0:1, h::HEADS][:, rev], -BIG, ALU.add, ALU.max)
                    drain()
                    V.tensor_copy(tails[0:1, 0:1], carried[0:1, 0:1]).then_inc(edge_in, 1)
                    dve.wait_ge(edge_mm, 2 * (d0 + d) + 4)
                    V.tensor_copy(carry[:, 0:1], psG[:, 1, 0, 0:1])
                    drain()
                    V.tensor_tensor_scan(MAXS[:, rev], fl[:, rev], MAXS[:, rev], carry[:, 0:1], ALU.add, ALU.max)
                    drain()

            def weighted(n):
                ph = f"{n}b"

                def prepare(g, h):
                    b, first = h % AHEAD, g * SPAN + h * HALF
                    V.tensor_tensor(onehot[:, b, :, :], rep(iota[:, :], HALF),
                                    bc(dst_local[:, bass.ds(first, HALF)], P), ALU.is_equal).then_inc(oh_rdy, 1)
                dve.wait_ge(oh_rdy, at_oh[ph])
                block_sums(ph, 0, F + HEADS, prepare)

            def shares(eps_op):
                den = H2[:, :, 0:HEADS]
                V.tensor_scalar(den, acc[:, 0:NB, F:F + HEADS], 1e-10, None, eps_op)
                drain()
                V.reciprocal(den, den)
                drain()
                V.tensor_tensor(H.rearrange("p b (h d) -> p b h d", d=HD),
                                acc[:, 0:NB, 0:F].rearrange("p b (h d) -> p b h d", d=HD),
                                den.rearrange("p b (h o) -> p b h o", o=1).to_broadcast([P, NB, HEADS, HD]), ALU.mult)\
                    .then_inc(acc_used, 1)

            V.memset(dst_i, PADKEY)
            V.memset(src_i, PADKEY)
            V.memset(typ_i, 0)
            V.memset(nxt[:], PADKEY)
            V.memset(w_in, 0.0).then_inc(pads_set, 1)
            V.memset(X[:, NB - 1, :], 0.0)
            V.memset(we_blk[:], 0.0).then_inc(pads_set, 1)
            V.memset(ones[:], 1.0)
            V.memset(nodes[:, NB, :], 0.0)
            V.memset(s_dst[:, NB, :], 0.0)
            V.memset(zeros, 0.0)
            V.memset(place, 0.0)
            V.memset(vio[:], 0.0)
            V.memset(dst_local[:, T:T + BODY], -1.0)
            V.memset(idx_a[:, T:T + BODY], 0)
            V.memset(idx_b[:, T:T + BODY], 0)
            dve.wait_ge(iota_set, 10)
            V.tensor_copy(iota[:], iota_i[:])
            V.tensor_copy(map_rhs, tile_no_i)
            drain()
            V.tensor_copy(tile_no, map_rhs)
            V.tensor_scalar(thr[:], iota[:, 0:NKEY], float(P), None, ALU.mult)
            V.tensor_copy(node_no[:], node_no_i[:]).then_inc(dve_consts, 1)
            dve.wait_ge(x_in, 32)
            layernorm(1)
            drain()
            V.tensor_tensor(X[:, :, :], X[:, :, :], H, ALU.add).then_inc(work_free, 1)
            dve.wait_ge(consts_in, 16 * N_CONSTS)
            V.tensor_copy(be_step[0:1, :].rearrange("o (n k) -> o n k", n=QUAD), rep(be_row[0:1, :], QUAD))\
                .then_inc(dve_consts, 1)
            dve.wait_ge(edges_in, 5 * 16)
            V.tensor_tensor(hit[:, 0:EC - 1], dst_i[:, 0:EC - 1], dst_i[:, 1:EC], ALU.is_gt)
            V.tensor_tensor(vio[:, 1:2], dst_i[:, EC - 1:EC], nxt[:, 0:1], ALU.is_gt)
            drain()
            V.tensor_reduce(vio[:, 0:1], hit[:, 0:EC - 1], AXX, ALU.add)
            drain()
            V.tensor_tensor(vio[:, 2:3], vio[:, 0:1], vio[:, 1:2], ALU.add)
            V.tensor_copy(key, dst_i)
            V.tensor_copy(cnt, src_i)
            drain()
            with dve.Fori(0, NBX + 1) as b:
                V.tensor_scalar(hit, key, thr[:, bass.ds(b, 1)], 0.0, ALU.is_lt, ALU.add,
                                accum_out=cum[:, 0, bass.ds(b, 1)])
                V.tensor_scalar(key_i.bitcast(F32), cnt, thr[:, bass.ds(b, 1)], 0.0, ALU.is_lt, ALU.add,
                                accum_out=cum[:, 1, bass.ds(b, 1)])
                drain()
            V.tensor_tensor(tot[:, 0:NB], cum[:, 1, 1:NB + 1], cum[:, 1, 0:NB], ALU.subtract)
            V.tensor_scalar(key_i, src_i, 7, None, ALU.arith_shift_right)
            drain()
            V.tensor_copy(key, key_i).then_inc(counts_set, 1)
            dve.wait_ge(base_mm, 1)
            V.tensor_scalar(flag[:, 0:1], base_ps[:, 1, 0:1], 0.5, None, ALU.is_gt)
            V.tensor_copy(below[:], base_ps[0:NBX, 2, 0:4])
            drain()
            V.tensor_scalar(rounded[:, 0:1], below[:, 1:2], float(P - 1), None, ALU.add)
            V.tensor_copy(rounded[:, 1:2], below[:, 0:1])
            V.tensor_tensor(bounds[:, 1:2], below[:, 3:4], below[:, 2:3], ALU.subtract)
            V.tensor_tensor(bounds[:, 2:3], below[:, 1:2], below[:, 0:1], ALU.is_gt)
            drain()
            V.tensor_scalar(rounded[:, 2:3], bounds[:, 1:2], float(P - 1), None, ALU.add)
            drain()
            V.tensor_scalar(rounded[:], rounded[:], 7, None, ALU.arith_shift_right)
            drain()
            V.tensor_copy(rounded_f[:], rounded[:])
            drain()
            V.tensor_tensor(n_tiles[:, 0:1], rounded_f[:, 0:1], rounded_f[:, 1:2], ALU.subtract)
            drain()
            V.tensor_tensor(n_tiles[:, 0:1], n_tiles[:, 0:1], bounds[:, 2:3], ALU.mult)
            V.tensor_copy(n_tiles[:, 1:2], rounded_f[:, 2:3]).then_inc(map_col, 1)
            dve.wait_ge(map_mm, 1)
            V.tensor_copy(first_tile[:], base_ps[0:NBX, 2, 0:2])
            drain()
            V.tensor_tensor(end_tile[:], first_tile[:], n_tiles[:], ALU.add)
            V.tensor_tensor(shift[:], rounded_f[:, 1:2], first_tile[:, 0:1], ALU.subtract)
            V.tensor_scalar(bounds[:, 0:1], first_tile[:, 1:2], float(P), None, ALU.mult)
            drain()
            V.tensor_tensor(bounds[:, 1:2], bounds[:, 1:2], bounds[:, 0:1], ALU.add)
            V.tensor_scalar(bounds[:, 2:3], end_tile[:, 1:2], float(P), None, ALU.mult)
            drain()
            for i in range(3):
                V.tensor_scalar(diag[:, i, :], ident[0:NBX, 0:NBX], bounds[:, i:i + 1], None, ALU.mult)
            V.scalar_tensor_tensor(end_tile[:], ident[0:NBX, NB:NB + 1].to_broadcast([NBX, 2]), 1e6, end_tile[:],
                                   ALU.mult, ALU.add).then_inc(map_col, 1)
            dve.wait_ge(base_mm, 2)
            V.tensor_scalar(base[:, 0:NB], base_ps[:, 0, 0:NB], -1.0, None, ALU.add)
            V.tensor_scalar(gap[:, 0, :], base_ps[:, 1, 0:NB], node_no[:], None, ALU.add)
            V.tensor_copy(gap[:, 1, :], base_ps[:, 1, NBX:NBX + NB])
            drain()
            V.tensor_copy(gap_i[:, 0, :], gap[:, 0, :])
            V.tensor_tensor(gap[:, 1, :], gap[:, 0, :], gap[:, 1, :], ALU.is_lt)
            drain()
            V.tensor_scalar(gap_i[:, 1, :], gap_i[:, 0, :], P - 1, None, ALU.bitwise_and)
            V.tensor_scalar(gap_i[:, 2, :], gap_i[:, 0, :], 7, None, ALU.arith_shift_right)
            drain()
            V.tensor_copy(gap[:, 2:4, :], gap_i[:, 1:3, :])
            drain()
            V.scalar_tensor_tensor(gap[:, 0, :], gap[:, 2, :], float(T), gap[:, 3, :], ALU.mult, ALU.add)
            drain()
            V.scalar_tensor_tensor(gap[:, 0, :], gap[:, 0, :], -float(PLACES), gap[:, 1, :], ALU.add, ALU.mult)
            drain()
            V.tensor_scalar(gap_i[:, 0, :], gap[:, 0, :], float(PLACES), None, ALU.add).then_inc(gap_set, 1)

            def places(n):
                with dve.Fori(0, n) as b:
                    V.tensor_scalar(hit, key, iota[:, bass.ds(b, 1)], None, ALU.is_equal)
                    drain()
                    V.tensor_tensor_scan(cnt, hit, zeros, base[:, bass.ds(b, 1)], ALU.add, ALU.add)
                    drain()
                    V.tensor_tensor(cnt, cnt, hit, ALU.mult)
                    drain()
                    V.tensor_tensor(place, place, cnt, ALU.add)
                    drain()

            V.tensor_scalar(hits[0], key, iota[:, 0:1], None, ALU.is_equal)
            drain()

            def rank(b, i):
                V.tensor_tensor_scan(ranks[i], hits[i], zeros, base[:, bass.ds(b, 1)], ALU.add, ALU.add)
                if not (isinstance(b, int) and b == 0):
                    dve.wait_ge(picked_set, b)
                V.tensor_scalar(hits[1 - i], key, iota[:, bass.ds(b + 1, 1)], None, ALU.is_equal)
                drain()
                if not isinstance(b, int) or b >= 2:
                    dve.wait_ge(place_add, b - 1)
                V.tensor_tensor(picked[i], ranks[i], hits[i], ALU.mult).then_inc(picked_set, 1)
            rank(0, 0)
            rank(1, 1)
            with dve.Fori(1, (NB - 1) // 2) as g:
                for i in range(2):
                    rank(g * 2 + i, i)
            rank(NB - 1, 0)
            dve.wait_ge(work_zero, 1)
            V.tensor_copy(recs[:, :, D_], dst_i)
            V.tensor_copy(recs[:, :, S_], src_i)
            V.tensor_copy(recs[:, :, T_], typ_i)
            V.tensor_copy(recs[:, :, W_], w_in)
            dve.wait_ge(bias_put, EC // ATT)
            dve.wait_ge(place_add, NB)
            V.tensor_copy(recs[:, :, POS_], place).then_inc(recs_set, 1)
            V.tensor_copy(vio[:, 0:1], zeros[:, 0:1]).then_inc(flag_set, 1)
            unsorted = dve.value_load(flag[0:1, 0:1], min_val=0, max_val=1)
            with dve.If(unsorted):
                dve.wait_ge(rec_out, 16)
                for n in range(2):
                    if n:
                        dve.wait_ge(so_in, 16)
                    V.tensor_copy(dst_i, recs[:, :, D_])
                    V.memset(place, 0.0)
                    drain()
                    if n:
                        V.tensor_scalar(key_i, dst_i, 6, None, ALU.arith_shift_right)
                    else:
                        V.tensor_scalar(key_i, dst_i, NKEY - 1, None, ALU.bitwise_and)
                    drain()
                    V.tensor_copy(key, key_i)
                    drain()
                    with dve.Fori(0, NKEY) as b:
                        V.tensor_scalar(hit, key, iota[:, bass.ds(b, 1)], 0.0, ALU.is_equal, ALU.add,
                                        accum_out=tot[:, bass.ds(b, 1)])
                        drain()
                    V.tensor_tensor_scan(totc[:], tot[:], zeros[:, 0:NKEY], 0.0, ALU.add, ALU.add)
                    drain()
                    V.tensor_tensor(totc[:], totc[:], tot[:], ALU.subtract).then_inc(so_tot, 1)
                    dve.wait_ge(so_base, n + 1)
                    V.tensor_scalar(base[:], psG[:, 1, 0, 0:NKEY], -1.0, None, ALU.add)
                    drain()
                    places(NKEY)
                    V.tensor_copy(place_i, place).then_inc(so_place, 1)
                dve.wait_ge(so_pass, 2)
            with dve.Else():
                dve.nop()

            V.tensor_scalar(att_blk[:, 0:HEADS], head_mask[:], att_col[:, 0:1], None, ALU.mult)
            V.tensor_scalar(att_blk[:, HEADS:2 * HEADS], head_mask[:], att_col[:, 1:2], None, ALU.mult)
            drain()
            for m in range(2):
                V.tensor_scalar(map_tmp[0:NBX, :], tile_no[0:NBX, :], first_tile[:, m:m + 1], None, ALU.is_ge)
                V.tensor_scalar(map_tmp2[0:NBX, :], tile_no[0:NBX, :], end_tile[:, m:m + 1], None, ALU.is_lt)
                drain()
                V.tensor_tensor(map_tmp[0:NBX, :], map_tmp[0:NBX, :], map_tmp2[0:NBX, :], ALU.mult)
                drain()
                V.tensor_scalar(map_rhs[0:NBX, :], map_tmp[0:NBX, :], node_no[0:NBX, :], None, ALU.mult)\
                    .then_inc(map_col, 1)
                dve.wait_ge(map_mm, 2 + m)
                if m == 0:
                    for c in range(TC):
                        k = min(P, T - c * P)
                        V.scalar_tensor_tensor(group_f[0:k, c:c + 1], node_no[0:k, :], float(c * P),
                                               psG[0:k, 1, 3, c:c + 1], ALU.add, ALU.add)
                    drain()
                    for c in range(TC):
                        k = min(P, T - c * P)
                        V.tensor_scalar(group_i[0:k, c:c + 1], group_f[0:k, c:c + 1], float(GROUPS - 1), None, ALU.min)
                    V.tensor_copy(vio[:, 1:2], zeros[:, 0:1]).then_inc(map_set, 1)
                for c in range(2):
                    ps = psA[:, 4 * m + 2 * c:4 * m + 2 * c + 2, :].rearrange("p a b -> p (a b)")[:, 0:T // 2]
                    cs = slice(c * (T // 2), (c + 1) * (T // 2))
                    V.tensor_copy(maps[32 * m:32 * m + 32, cs], ps[32 * m:32 * m + 32, :])
                    V.tensor_scalar((src_lo if m else block_lo)[:, cs], ps, float(P), None, ALU.mult)
                drain()
                for i in range(2):
                    V.tensor_copy(end_maps[32 * m:32 * m + 32, i::2],
                                  maps[32 * m:32 * m + 32, i * (HALF - 1)::HALF])

            for i in range(0, 4 * TC, 2):
                field_out(V.tensor_copy, dve, i)
            dve.wait_ge(field_copy[1], 2 * TC)
            drain()
            V.tensor_tensor(dst_local[:, 0:T], fields[:, 0, :], block_lo[:], ALU.subtract)
            V.tensor_copy(place_t, fields[:, 4, :])
            V.tensor_scalar(map_rhs, src_f, float(NB * P - 1), None, ALU.min)
            V.tensor_scalar(dst_id, fields[:, 0, :], 1.0, None, ALU.add)
            drain()
            V.tensor_copy(block_lo[:], src_lo)
            V.tensor_scalar(place_t2, place_t, P - 1, None, ALU.bitwise_and)
            V.tensor_scalar(map_tmp, dst_local[:, 0:T], float(P), None, ALU.is_lt)
            V.tensor_scalar(map_tmp2, dst_local[:, 0:T], 0.0, None, ALU.is_ge)
            V.scalar_tensor_tensor(idx_b[:, 0:T], map_rhs, float(NREL), fields[:, 2, :], ALU.mult, ALU.add)
            drain()
            V.tensor_scalar(place_t, place_t, 7, None, ALU.arith_shift_right)
            V.tensor_tensor(map_tmp, map_tmp, map_tmp2, ALU.mult)
            V.tensor_copy(fields[:, 0, :], place_t2)
            drain()
            V.tensor_copy(fields[:, 4, :], place_t)
            V.tensor_tensor(dst_id, dst_id, map_tmp, ALU.mult)
            drain()
            V.scalar_tensor_tensor(fields[:, 0, :], fields[:, 0, :], float(T), fields[:, 4, :], ALU.mult, ALU.add)
            V.tensor_scalar(dst_id, dst_id, -1.0, None, ALU.add)
            drain()
            V.scalar_tensor_tensor(fields[:, 0, :], fields[:, 0, :], -float(PLACES), map_tmp, ALU.add, ALU.mult)
            drain()
            V.tensor_scalar(idx_a[:, 0:T], fields[:, 0, :], float(PLACES), None, ALU.add).then_inc(tiles_set, 1)
            V.tensor_copy(by_chunk, dst_id.rearrange("p (c j o) -> p c j o", c=CH, o=1)
                          .to_broadcast([P, CH, CT, HEADS])).then_inc(mv_rdy, 1)
            to_scan_out(0)
            V.tensor_copy(chunk_ends[:, 0:1], SCAN[:, 0:1])
            V.tensor_copy(chunk_ends[:, 1:2], SCAN[:, CE - 1:CE]).then_inc(edge_in, 1)
            V.tensor_tensor(flags[:, 1:CE], SCAN[:, 1:CE], SCAN[:, 0:CE - 1], ALU.not_equal)
            dve.wait_ge(edge_mm, 1)
            V.tensor_tensor(flags[:, 0:1], chunk_ends[:, 0:1], psG[:, 0, 0, 0:1], ALU.not_equal)
            V.tensor_tensor(flags[:, CE:CE + 1], chunk_ends[:, 1:2], psG[:, 0, 0, 1:2], ALU.not_equal)

            drain()
            one_hots(0, 0)

            def messages(g):
                for k in range(4):
                    wait_if(dve, tr_done, g * 4 + (at_quad["0a"] + k))
                    one_hots(g * BODY + 4 * (k + 1), k + 1)
                    dve.wait_ge(got, g * 4 + (at_quad["0a"] + k + 1))
                    for j in range(QUAD):
                        wait_if(dve, slot[4 * k + j], g * 16)
                    V.tensor_tensor(msg_ring[:, 4 * k:4 * k + 4, 0:F], psG[:, k % 2, :, :],
                                    bc(weight[:, bass.ds(g * BODY + 4 * k, QUAD)], F), ALU.mult)
                    V.tensor_copy(msg_ring[:, 4 * k:4 * k + 4, F], src_f[:, bass.ds(g * BODY + 4 * k, QUAD)])
                    V.tensor_copy(idx_ring[:, 4 * k:4 * k + 4], idx_a[:, bass.ds(g * BODY + 4 * k, QUAD)])\
                        .then_inc(quad_rdy, 1)
            bodies(dve, messages)
            drain()
            V.tensor_scalar(flags[:, 0:CE + 1], flags[:, 0:CE + 1], -BIG, None, ALU.mult)
            drain()
            V.tensor_reduce(chunk_ends[:, 2:3], flags[:, 0:CE], AXX, ALU.min)
            V.tensor_reduce(chunk_ends[:, 3:4], flags[:, 1:CE + 1], AXX, ALU.min).then_inc(edge_in, 1)
            dve.wait_ge(edge_mm, 2)
            V.tensor_copy(link[0:1, :, :], psG[0:1, 0, 0:2, :])
            V.memset(acc[:, :, :], 0.0).then_inc(added, 2 * HALF)
            dve.wait_ge(msgs_done, 1)
            V.tensor_scalar(idx_a[:, 0:T], src_f, float(NB * P - 1), None, ALU.min)

            def prepare(g, h):
                b, first = h % AHEAD, g * SPAN + h * HALF
                dve.wait_ge(msg_in[h % RING], g * 16 + 16 * (h // RING + 1))
                V.tensor_tensor(src_local[:, b * HALF:(b + 1) * HALF], msg_seq[:, h % RING, :, F],
                                block_lo[:, bass.ds(first, HALF)], ALU.subtract).then_inc(src_sub, 1)
                dve.wait_ge(src_sub, g * RING + (h + 1))
                V.tensor_tensor(onehot[:, b, :, :], rep(iota[:, :], HALF),
                                bc(src_local[:, b * HALF:(b + 1) * HALF], P), ALU.is_equal).then_inc(oh_rdy, 1)
            dve.wait_ge(oh_rdy, at_oh["0b"])
            block_sums("0b", 32, F, prepare)
            V.tensor_tensor(H, acc[:, 0:NB, 0:F], rep(vecs[:, 0, :], NB), ALU.add).then_inc(bn_in, 1)
            dve.wait_ge(bn_mm, 1)
            V.tensor_scalar(bn[:, 0, :], psG[:, 0, 0, :], 1.0 / N, None, ALU.mult)
            drain()
            for i in range(2):
                bs = nodes_part(i)
                V.tensor_tensor(H[:, bs, :], H[:, bs, :], rep(bn[:, 0, :], bs.stop - bs.start), ALU.subtract)\
                    .then_inc(centred, 1)
            dve.wait_ge(bn_mm, 2)
            V.tensor_scalar(bn[:, 1, :], psG[:, 0, 0, :], 1.0 / N, LN_EPS, ALU.mult, ALU.add).then_inc(bn_var, 1)
            dve.wait_ge(bn_sd, 1)
            V.reciprocal(bn[:, 3, :], bn[:, 2, :])
            drain()
            V.tensor_tensor(bn[:, 3, :], bn[:, 3, :], vecs[:, 1, :], ALU.mult)
            drain()
            V.tensor_tensor(H, H, rep(bn[:, 3, :], NB), ALU.mult)
            drain()
            V.tensor_tensor(H, H, rep(vecs[:, 2, :], NB), ALU.add)
            drain()
            V.scalar_tensor_tensor(X[:, :, :], H, 0.0, X[:, :, :], ALU.max, ALU.add)
            drain()

            layernorm(2)

            def rel_out(b, ps):
                if b >= 2:
                    dve.wait_ge(tab_out[b % 2], 16 * (b // 2))
                return V.tensor_copy(rel_stage[:, b % 2, 512:1024], ps[:, 512:1024])
            for b in range(NB):
                block_out(1, b, rel_out)
            one_hots(0, 0)
            with dve.Fori(0, BODIES) as g:
                for k in range(4):
                    dve.wait_ge(agg, g * BODY + (at_agg["1"] + 4 * k))
                    one_hots(g * BODY + 4 * (k + 1), k + 1)
                    regs = blocks_of(ENG.DVE, 0, g * BODY + 4 * k, QUAD)
                    for j in range(QUAD):
                        if j % 2 == 0:
                            dve.wait_ge(agg, g * BODY + (at_agg["1"] + 4 * k + j + 2))
                        add("1", regs[j], g, 4 * k + j, psA[:, (4 * k + j) % HALF, 0:F], span=BODY)
            dve.wait_ge(added, at_added["1"] + T)
            V.tensor_tensor(X[:, :, :], X[:, :, :], acc[:, 0:NB, 0:F], ALU.add).then_inc(acc_used, 1)
            drain()

            layernorm(3)

            def gat_out(b, ps):
                V.tensor_copy(H2[:, b, 0:HEADS], ps[:, 0:HEADS])
                return V.tensor_copy(s_dst[:, b, :], ps[:, HEADS:2 * HEADS])
            for b in range(NB):
                block_out(2, b, gat_out)
            one_hots(0, 0)
            with dve.Fori(0, BODIES) as g:
                for k in range(4):
                    dve.wait_ge(tr_done, g * 4 + (at_quad["2a"] + k))
                    sums = prod[:, (k % 2) * QUAD * HEADS:(k % 2 + 1) * QUAD * HEADS].rearrange(
                        "p (s h) -> p s h", h=HEADS)
                    one_hots(g * BODY + 4 * (k + 1), k + 1)
                    dve.wait_ge(got, g * 4 + (at_quad["2a"] + k + 1))
                    for j in range(QUAD):
                        dve.wait_ge(slot[4 * k + j], g * 16 + (at_slot["2a"] + 16))
                    V.tensor_tensor(sums, psG[:, k % 2, :, 0:HEADS],
                                    gat_ring[:, 4 * k:4 * k + 4, F:F + HEADS], ALU.add).then_inc(sum_rdy, 1)
                    dve.wait_ge(sum_rdy, g * 4 + (k + 1))
                    V.scalar_tensor_tensor(sc_t[:, bass.ds(g * BODY + 4 * k, QUAD), :], sums, 0.2, sums,
                                           ALU.mult, ALU.max).then_inc(quad_rdy, 1)
            dve.wait_ge(quad_rdy, at_quad["3a"])
            V.tensor_copy(by_chunk, sc).then_inc(mv_rdy, 1)
            for k in range(4):
                dve.wait_ge(wb[k], 16 * BODIES)
            to_scan_out(1)
            segment_max(0)
            for i in range(2):
                V.scalar_tensor_tensor(MAXS[:, part(i)], MAXS[:, part(i)], 0.0, SCAN[:, part(i)],
                                       ALU.max, ALU.subtract).then_inc(diff_rdy, 1)
            from_scan_out(2)
            V.tensor_copy(carry[:, 0:1], ones[:, 0:1]).then_inc(ring_free, 1)
            weighted(2)
            shares(ALU.max)
            drain()
            V.tensor_tensor(X[:, :, :], X[:, :, :], H, ALU.add)
            drain()

            layernorm(4)

            def kv_out(b, ps):
                if b >= 2:
                    dve.wait_ge(tab_out[b % 2], 16 * (b // 2 + tab_at[2][b % 2]))
                V.tensor_tensor(nodes[:, b, :], ps[:, 0:F], vecs[:, 3, :], ALU.add)
                return V.tensor_tensor(kv_stage[:, b % 2, :], ps[:, F:3 * F],
                                       vecs[:, 4:6, :].rearrange("p a f -> p (a f)"), ALU.add)
            for b in range(NB):
                block_out(3, b, kv_out)
            dve.wait_ge(bias_in, 16)
            one_hots(0, 0)
            with dve.Fori(0, BODIES) as g:
                for k in range(4):
                    dve.wait_ge(tr_done, g * 4 + (at_quad["3a"] + k))
                    one_hots(g * BODY + 4 * (k + 1), k + 1)
                    dve.wait_ge(got, g * 4 + (at_quad["3a"] + k + 1))
                    for j in range(QUAD):
                        dve.wait_ge(slot[4 * k + j], g * 16 + (at_slot["3a"] + 16))
                    dve.wait_ge(quad_rdy, g * 4 + (at_quad["3a"] + k))
                    raw = work[:, RAW0 + (k % 2) * QUAD * HEADS:RAW0 + (k % 2 + 1) * QUAD * HEADS]
                    V.tensor_tensor(prod.rearrange("p (s w) -> p s w", w=F), psG[:, k % 2, :, :],
                                    kv_ring[:, 4 * k:4 * k + 4, 0:F], ALU.mult).then_inc(prod_rdy, 1)
                    dve.wait_ge(prod_rdy, g * 4 + (k + 1))
                    V.tensor_reduce(raw, prod.rearrange("p (s d) -> p s d", d=HD), AXX, ALU.add)\
                        .then_inc(sum_rdy, 1)
                    dve.wait_ge(sum_rdy, g * 4 + (NQ + k + 1))
                    at = bass.ds(g * (BODY * HEADS) + 4 * k * HEADS, QUAD * HEADS)
                    V.scalar_tensor_tensor(scores[:, at], raw, float(HD) ** -0.5, MAXS[:, at],
                                           ALU.mult, ALU.add).then_inc(quad_rdy, 1)
            dve.wait_ge(quad_rdy, at_quad["3a"] + NQ)
            for k in range(4):
                dve.wait_ge(wb[k], 16 * BODIES * 2)
            V.tensor_copy(by_chunk, sc).then_inc(mv_rdy, 1)
            to_scan_out(3)
            segment_max(2)
            for i in range(2):
                V.tensor_tensor(MAXS[:, part(i)], MAXS[:, part(i)], SCAN[:, part(i)], ALU.subtract)\
                    .then_inc(diff_rdy, 1)
            from_scan_out(4)
            V.tensor_copy(carry[:, 0:1], ones[:, 0:1]).then_inc(ring_free, 1)
            weighted(3)
            shares(ALU.add)
            drain()
            V.tensor_tensor(X[:, :, :], X[:, :, :], rep(vecs[:, 6, :], NB), ALU.add).then_inc(h_rdy, 1)
            for b in range(NB):
                block_out(4, b, lambda b, ps: V.tensor_tensor(X[:, b, :], X[:, b, :], ps[:, 0:F], ALU.add))


_INS = ["x", "src", "dst", "edge_attr_32", "edge_type_8", "edge_weight", "L0_gnn_weight", "L0_gnn_bias",
        "L0_gnn_bn_gamma", "L0_gnn_bn_beta", "L1_gnn_weight", "L2_gnn_att", "L3_gnn_Wq", "L3_gnn_bq",
        "L3_gnn_Wk", "L3_gnn_bk", "L3_gnn_Wv", "L3_gnn_bv", "L3_gnn_We", "L3_gnn_be", "L3_gnn_Wo", "L3_gnn_bo"]


def kernel(**inputs):
    import numpy as np
    import concourse.bacc as bacc
    from concourse.bass_utils import run_bass_kernel_spmd

    nc = bacc.Bacc("TRN2", target_bir_lowering=False, num_devices=1)
    arrays, args = {}, {}
    for name in _INS:
        arr = np.ascontiguousarray(inputs[name])
        arrays[f"in_{name}"] = arr
        args[name] = nc.dram_tensor(f"in_{name}", arr.shape, mybir.dt.from_np(arr.dtype), kind="ExternalInput").ap()
    out = nc.dram_tensor("out_x", (N, F), F32, kind="ExternalOutput").ap()
    gnn(nc, args, out)
    r = run_bass_kernel_spmd(nc, [arrays], core_ids=[0])
    return r.results[0]["out_x"]
```
